# Optimizing a Trainium2 kernel written in Bass

```python
import numpy as np
import jax
import jax.numpy as jnp

def _softmax(x, axis=-1):
    return jax.nn.softmax(x, axis=axis)

def _gelu(x):
    return jax.nn.gelu(x, approximate=True)

def _silu(x):
    return jax.nn.silu(x)

def _sigmoid(x):
    return jax.nn.sigmoid(x)

def _layernorm(x, axis=-1, eps=1e-05):
    m = jnp.mean(x, axis=axis, keepdims=True)
    v = jnp.var(x, axis=axis, keepdims=True)
    return (x - m) / jnp.sqrt(v + eps)

def _scatter_add(tgt, idx, src, axis=0):
    return tgt.at[idx].add(src)

def _segment_sum(src, seg, n):
    return jax.ops.segment_sum(src, seg, n)
kernel_name = 'mk_adaln_attn_ffn_d2_seqx_r8_751dbc'

def setup_inputs(seed: int=0):
    np.random.seed(seed)
    _w = jnp.asarray

    def _rec_inputs():
        import jax
        import jax.numpy as jnp
        _rk = jax.random.key(seed)
        x = -0.000125 + 0.9999 * jax.random.normal(jax.random.fold_in(_rk, 1), (4, 256, 256), jnp.float32)
        _lenS = 256 - jax.random.randint(jax.random.fold_in(_rk, 7), (4,), 0, max(1, 256 // 4) + 1, jnp.int32)
        _lenS2 = 256 - jax.random.randint(jax.random.fold_in(_rk, 8), (4,), 0, max(1, 256 // 4) + 1, jnp.int32)
        fside_BxSxS_0 = -1.52775e-05 + 0.999936 * jax.random.normal(jax.random.fold_in(_rk, 11), (4, 256, 256), jnp.float32)
        cond_512 = -5.03954e-05 + 1.00559 * jax.random.normal(jax.random.fold_in(_rk, 12), (4, 64), jnp.float32)
        return (x, fside_BxSxS_0, cond_512)
    x, fside_BxSxS_0, cond_512 = _rec_inputs()

    def _L0_cond_setup():
        import jax, jax.numpy as jnp
        from jax import lax
        import numpy as np
        B, T, C, TD = (8, 256, 256, 64)

        def _bi_wkv(r, k, v, w, u, time_emb):
            tf = jax.nn.sigmoid(jnp.sum(time_emb, axis=-1))[:, None, None]
            decay = jnp.exp(-jnp.exp(w.astype(jnp.float32)))[None, :] * (0.5 + 0.5 * tf[:, :, 0])
            kf = k.astype(jnp.float32)
            vf = v.astype(jnp.float32)
            ek = jnp.exp(jnp.minimum(kf, 30.0))
            ekv = ek * vf

            def step(carry, x):
                a, b = carry
                ekv_t, ek_t = x
                a = a * decay + ekv_t
                b = b * decay + ek_t
                return ((a, b), (a, b))
            ekv_t = jnp.swapaxes(ekv, 0, 1)
            ek_t = jnp.swapaxes(ek, 0, 1)
            init = (jnp.zeros_like(decay), jnp.zeros_like(decay))
            _, (nf, df) = lax.scan(step, init, (ekv_t, ek_t))
            _, (nb, db) = lax.scan(step, init, (ekv_t, ek_t), reverse=True)
            nf = jnp.swapaxes(nf, 0, 1)
            df = jnp.swapaxes(df, 0, 1)
            nb = jnp.swapaxes(nb, 0, 1)
            db = jnp.swapaxes(db, 0, 1)
            euk = jnp.exp(jnp.minimum(u.astype(jnp.float32)[None, None, :] + kf, 30.0))
            num = nf + nb - ekv + euk * vf
            den = df + db - ek + euk
            base = jax.nn.sigmoid(r.astype(jnp.float32)) * (num / jnp.maximum(den, 1e-08))
            out = base * (0.8 + 0.2 * tf)
            return out.astype(r.dtype)
        key = jax.random.key(seed)
        ks = jax.random.split(key, 6)
        return {'r': jax.random.normal(ks[0], (B, T, C), dtype=jnp.float32), 'k': jax.random.normal(ks[1], (B, T, C), dtype=jnp.float32), 'v': jax.random.normal(ks[2], (B, T, C), dtype=jnp.float32), 'w': jax.random.normal(ks[3], (C,), dtype=jnp.float32), 'u': jax.random.normal(ks[4], (C,), dtype=jnp.float32), 'time_emb': jax.random.normal(ks[5], (B, TD), dtype=jnp.float32)}
    _L0_cond_all = _L0_cond_setup()
    _L0_cond_in = {k: v for k, v in _L0_cond_all.items() if k in ('w', 'u')}
    del _L0_cond_all

    def _L0_attn_setup():
        import jax, jax.numpy as jnp
        import numpy as np
        B_, L, D_MODEL = (2, 512, 256)
        H, P, N, G, K = (32, 64, 128, 1, 4)
        EPS = 1e-05
        INTER = H * P
        CONV_DIM = INTER + 2 * G * N
        PROJ = INTER + CONV_DIM + H

        def _silu(x):
            return x * jax.nn.sigmoid(x)

        def _mamba2_mixer(hidden_states, W_in, conv_w, conv_b, dt_bias, A_log, D_param, norm_w, W_out):
            b, l, _ = hidden_states.shape
            proj = jnp.einsum('bld,pd->blp', hidden_states, W_in)
            gate = proj[..., :INTER]
            hBC = proj[..., INTER:INTER + CONV_DIM]
            dt = proj[..., INTER + CONV_DIM:]
            xc = jnp.transpose(hBC, (0, 2, 1))
            conv = jax.lax.conv_general_dilated(xc, conv_w[:, None, :], window_strides=(1,), padding=[(K - 1, 0)], dimension_numbers=('NCH', 'OIH', 'NCH'), feature_group_count=CONV_DIM)
            hBC = _silu(jnp.transpose(conv + conv_b[None, :, None], (0, 2, 1)))
            xs = hBC[..., :INTER].reshape(b, l, H, P)
            Bm = hBC[..., INTER:INTER + G * N].reshape(b, l, G, N)
            Cm = hBC[..., INTER + G * N:].reshape(b, l, G, N)
            Bh = jnp.repeat(Bm, H // G, axis=2)
            Ch = jnp.repeat(Cm, H // G, axis=2)
            dt = jax.nn.softplus(dt + dt_bias)
            A = -jnp.exp(A_log)
            dA = jnp.exp(dt * A)

            def step(h, inp):
                dA_t, dt_t, x_t, B_t, C_t = inp
                u = (dt_t[:, :, None] * x_t)[..., None] * B_t[:, :, None, :]
                h = dA_t[:, :, None, None] * h + u
                y = jnp.einsum('bhpn,bhn->bhp', h, C_t)
                return (h, y)
            tm = lambda a: jnp.moveaxis(a, 1, 0)
            h0 = jnp.zeros((b, H, P, N), hidden_states.dtype)
            _, ys = jax.lax.scan(step, h0, (tm(dA), tm(dt), tm(xs), tm(Bh), tm(Ch)))
            y = jnp.moveaxis(ys, 0, 1) + D_param[None, None, :, None] * xs
            y = y.reshape(b, l, INTER)
            g = y * _silu(gate)
            g = g * jax.lax.rsqrt(jnp.mean(g * g, axis=-1, keepdims=True) + EPS) * norm_w
            return jnp.einsum('bli,di->bld', g, W_out)
        key = jax.random.key(seed)
        ks = jax.random.split(key, 5)
        hidden_states = jax.random.normal(ks[0], (B_, L, D_MODEL), jnp.float32)
        W_in = jax.random.normal(ks[1], (PROJ, D_MODEL), jnp.float32) * 0.02
        conv_w = jax.random.normal(ks[2], (CONV_DIM, K), jnp.float32) * 0.1
        conv_b = jnp.zeros((CONV_DIM,), jnp.float32)
        dt_bias = jnp.ones((H,), jnp.float32)
        A_log = jnp.log(jnp.arange(1, H + 1, dtype=jnp.float32))
        D_param = jnp.ones((H,), jnp.float32)
        norm_w = jnp.ones((INTER,), jnp.float32)
        W_out = jax.random.normal(ks[3], (D_MODEL, INTER), jnp.float32) * 0.02
        return dict(hidden_states=hidden_states, W_in=W_in, conv_w=conv_w, conv_b=conv_b, dt_bias=dt_bias, A_log=A_log, D_param=D_param, norm_w=norm_w, W_out=W_out)
    _L0_attn_all = _L0_attn_setup()
    _L0_attn_in = {k: v for k, v in _L0_attn_all.items() if k in ('W_in', 'conv_w', 'conv_b', 'dt_bias', 'A_log', 'D_param', 'norm_w', 'W_out')}
    del _L0_attn_all

    def _L0_cond2_setup():
        import jax, jax.numpy as jnp
        from jax import lax
        import numpy as np
        B, T, C, TD = (8, 256, 256, 64)

        def _bi_wkv(r, k, v, w, u, time_emb):
            tf = jax.nn.sigmoid(jnp.sum(time_emb, axis=-1))[:, None, None]
            decay = jnp.exp(-jnp.exp(w.astype(jnp.float32)))[None, :] * (0.5 + 0.5 * tf[:, :, 0])
            kf = k.astype(jnp.float32)
            vf = v.astype(jnp.float32)
            ek = jnp.exp(jnp.minimum(kf, 30.0))
            ekv = ek * vf

            def step(carry, x):
                a, b = carry
                ekv_t, ek_t = x
                a = a * decay + ekv_t
                b = b * decay + ek_t
                return ((a, b), (a, b))
            ekv_t = jnp.swapaxes(ekv, 0, 1)
            ek_t = jnp.swapaxes(ek, 0, 1)
            init = (jnp.zeros_like(decay), jnp.zeros_like(decay))
            _, (nf, df) = lax.scan(step, init, (ekv_t, ek_t))
            _, (nb, db) = lax.scan(step, init, (ekv_t, ek_t), reverse=True)
            nf = jnp.swapaxes(nf, 0, 1)
            df = jnp.swapaxes(df, 0, 1)
            nb = jnp.swapaxes(nb, 0, 1)
            db = jnp.swapaxes(db, 0, 1)
            euk = jnp.exp(jnp.minimum(u.astype(jnp.float32)[None, None, :] + kf, 30.0))
            num = nf + nb - ekv + euk * vf
            den = df + db - ek + euk
            base = jax.nn.sigmoid(r.astype(jnp.float32)) * (num / jnp.maximum(den, 1e-08))
            out = base * (0.8 + 0.2 * tf)
            return out.astype(r.dtype)
        key = jax.random.key(seed)
        ks = jax.random.split(key, 6)
        return {'r': jax.random.normal(ks[0], (B, T, C), dtype=jnp.float32), 'k': jax.random.normal(ks[1], (B, T, C), dtype=jnp.float32), 'v': jax.random.normal(ks[2], (B, T, C), dtype=jnp.float32), 'w': jax.random.normal(ks[3], (C,), dtype=jnp.float32), 'u': jax.random.normal(ks[4], (C,), dtype=jnp.float32), 'time_emb': jax.random.normal(ks[5], (B, TD), dtype=jnp.float32)}
    _L0_cond2_all = _L0_cond2_setup()
    _L0_cond2_in = {k: v for k, v in _L0_cond2_all.items() if k in ('w', 'u')}
    del _L0_cond2_all

    def _L0_ffn_setup():
        import jax, jax.numpy as jnp
        import numpy as np
        TOP_K = 4
        key = jax.random.key(seed)
        ks = jax.random.split(key, 9)
        B, T, D, H, NE = (2, 128, 256, 176, 16)
        s = 0.02
        return {'x': jax.random.normal(ks[0], (B, T, D), jnp.float32), 'gate_w': jax.random.normal(ks[1], (NE, D), jnp.float32) * s, 'gate_b': jax.random.normal(ks[2], (NE,), jnp.float32) * s, 'w1_shared': jax.random.normal(ks[3], (D, H), jnp.float32) * s, 'w2_shared': jax.random.normal(ks[4], (H, D), jnp.float32) * s, 'w3_shared': jax.random.normal(ks[5], (D, H), jnp.float32) * s, 'w1_routed': jax.random.normal(ks[6], (NE, D, H), jnp.float32) * s, 'w2_routed': jax.random.normal(ks[7], (NE, H, D), jnp.float32) * s, 'w3_routed': jax.random.normal(ks[8], (NE, D, H), jnp.float32) * s}
    _L0_ffn_all = _L0_ffn_setup()
    _L0_ffn_in = {k: v for k, v in _L0_ffn_all.items() if k in ('gate_w', 'gate_b', 'w1_shared', 'w2_shared', 'w3_shared', 'w1_routed', 'w2_routed', 'w3_routed')}
    del _L0_ffn_all

    def _L1_cond_setup():
        import jax, jax.numpy as jnp
        from jax import lax
        import numpy as np
        B, T, C, TD = (8, 256, 256, 64)

        def _bi_wkv(r, k, v, w, u, time_emb):
            tf = jax.nn.sigmoid(jnp.sum(time_emb, axis=-1))[:, None, None]
            decay = jnp.exp(-jnp.exp(w.astype(jnp.float32)))[None, :] * (0.5 + 0.5 * tf[:, :, 0])
            kf = k.astype(jnp.float32)
            vf = v.astype(jnp.float32)
            ek = jnp.exp(jnp.minimum(kf, 30.0))
            ekv = ek * vf

            def step(carry, x):
                a, b = carry
                ekv_t, ek_t = x
                a = a * decay + ekv_t
                b = b * decay + ek_t
                return ((a, b), (a, b))
            ekv_t = jnp.swapaxes(ekv, 0, 1)
            ek_t = jnp.swapaxes(ek, 0, 1)
            init = (jnp.zeros_like(decay), jnp.zeros_like(decay))
            _, (nf, df) = lax.scan(step, init, (ekv_t, ek_t))
            _, (nb, db) = lax.scan(step, init, (ekv_t, ek_t), reverse=True)
            nf = jnp.swapaxes(nf, 0, 1)
            df = jnp.swapaxes(df, 0, 1)
            nb = jnp.swapaxes(nb, 0, 1)
            db = jnp.swapaxes(db, 0, 1)
            euk = jnp.exp(jnp.minimum(u.astype(jnp.float32)[None, None, :] + kf, 30.0))
            num = nf + nb - ekv + euk * vf
            den = df + db - ek + euk
            base = jax.nn.sigmoid(r.astype(jnp.float32)) * (num / jnp.maximum(den, 1e-08))
            out = base * (0.8 + 0.2 * tf)
            return out.astype(r.dtype)
        key = jax.random.key(seed)
        ks = jax.random.split(key, 6)
        return {'r': jax.random.normal(ks[0], (B, T, C), dtype=jnp.float32), 'k': jax.random.normal(ks[1], (B, T, C), dtype=jnp.float32), 'v': jax.random.normal(ks[2], (B, T, C), dtype=jnp.float32), 'w': jax.random.normal(ks[3], (C,), dtype=jnp.float32), 'u': jax.random.normal(ks[4], (C,), dtype=jnp.float32), 'time_emb': jax.random.normal(ks[5], (B, TD), dtype=jnp.float32)}
    _L1_cond_all = _L1_cond_setup()
    _L1_cond_in = {k: v for k, v in _L1_cond_all.items() if k in ('w', 'u')}
    del _L1_cond_all

    def _L1_attn_setup():
        import jax, jax.numpy as jnp
        import numpy as np
        import math
        D_MODEL = 256
        N_HEADS = 16
        Q_PROJ = D_MODEL // 4
        KV_PROJ = D_MODEL // 4
        DH = D_MODEL // N_HEADS
        LN_EPS = 1e-05

        def _layernorm(x, gamma, beta):
            mu = jnp.mean(x, axis=-1, keepdims=True)
            var = jnp.var(x, axis=-1, keepdims=True)
            return (x - mu) * jax.lax.rsqrt(var + LN_EPS) * gamma + beta
        key = jax.random.key(seed)
        ks = jax.random.split(key, 7)
        B, S = (2, 256)
        x = jax.random.normal(ks[0], (B, S, D_MODEL), dtype=jnp.float32)
        W_dq = 0.01 * jax.random.normal(ks[1], (D_MODEL, Q_PROJ), dtype=jnp.float32)
        W_uq = 0.01 * jax.random.normal(ks[2], (Q_PROJ, D_MODEL), dtype=jnp.float32)
        W_dkv = 0.01 * jax.random.normal(ks[3], (D_MODEL, KV_PROJ), dtype=jnp.float32)
        W_ukv = 0.01 * jax.random.normal(ks[4], (KV_PROJ, 2 * D_MODEL), dtype=jnp.float32)
        W_o = 0.01 * jax.random.normal(ks[5], (D_MODEL, D_MODEL), dtype=jnp.float32)
        q_ln_g = jnp.ones((Q_PROJ,), jnp.float32)
        q_ln_b = jnp.zeros((Q_PROJ,), jnp.float32)
        kv_ln_g = jnp.ones((KV_PROJ,), jnp.float32)
        kv_ln_b = jnp.zeros((KV_PROJ,), jnp.float32)
        return {'x': x, 'W_dq': W_dq, 'W_uq': W_uq, 'q_ln_g': q_ln_g, 'q_ln_b': q_ln_b, 'W_dkv': W_dkv, 'W_ukv': W_ukv, 'kv_ln_g': kv_ln_g, 'kv_ln_b': kv_ln_b, 'W_o': W_o}
    _L1_attn_all = _L1_attn_setup()
    _L1_attn_in = {k: v for k, v in _L1_attn_all.items() if k in ('W_dq', 'W_uq', 'q_ln_g', 'q_ln_b', 'W_dkv', 'W_ukv', 'kv_ln_g', 'kv_ln_b', 'W_o')}
    del _L1_attn_all

    def _L1_cond2_setup():
        import jax, jax.numpy as jnp
        from jax import lax
        import numpy as np
        B, T, C, TD = (8, 256, 256, 64)

        def _bi_wkv(r, k, v, w, u, time_emb):
            tf = jax.nn.sigmoid(jnp.sum(time_emb, axis=-1))[:, None, None]
            decay = jnp.exp(-jnp.exp(w.astype(jnp.float32)))[None, :] * (0.5 + 0.5 * tf[:, :, 0])
            kf = k.astype(jnp.float32)
            vf = v.astype(jnp.float32)
            ek = jnp.exp(jnp.minimum(kf, 30.0))
            ekv = ek * vf

            def step(carry, x):
                a, b = carry
                ekv_t, ek_t = x
                a = a * decay + ekv_t
                b = b * decay + ek_t
                return ((a, b), (a, b))
            ekv_t = jnp.swapaxes(ekv, 0, 1)
            ek_t = jnp.swapaxes(ek, 0, 1)
            init = (jnp.zeros_like(decay), jnp.zeros_like(decay))
            _, (nf, df) = lax.scan(step, init, (ekv_t, ek_t))
            _, (nb, db) = lax.scan(step, init, (ekv_t, ek_t), reverse=True)
            nf = jnp.swapaxes(nf, 0, 1)
            df = jnp.swapaxes(df, 0, 1)
            nb = jnp.swapaxes(nb, 0, 1)
            db = jnp.swapaxes(db, 0, 1)
            euk = jnp.exp(jnp.minimum(u.astype(jnp.float32)[None, None, :] + kf, 30.0))
            num = nf + nb - ekv + euk * vf
            den = df + db - ek + euk
            base = jax.nn.sigmoid(r.astype(jnp.float32)) * (num / jnp.maximum(den, 1e-08))
            out = base * (0.8 + 0.2 * tf)
            return out.astype(r.dtype)
        key = jax.random.key(seed)
        ks = jax.random.split(key, 6)
        return {'r': jax.random.normal(ks[0], (B, T, C), dtype=jnp.float32), 'k': jax.random.normal(ks[1], (B, T, C), dtype=jnp.float32), 'v': jax.random.normal(ks[2], (B, T, C), dtype=jnp.float32), 'w': jax.random.normal(ks[3], (C,), dtype=jnp.float32), 'u': jax.random.normal(ks[4], (C,), dtype=jnp.float32), 'time_emb': jax.random.normal(ks[5], (B, TD), dtype=jnp.float32)}
    _L1_cond2_all = _L1_cond2_setup()
    _L1_cond2_in = {k: v for k, v in _L1_cond2_all.items() if k in ('w', 'u')}
    del _L1_cond2_all

    def _L1_ffn_setup():
        import jax, jax.numpy as jnp
        import numpy as np
        ROPE_THETA = 1000000.0
        TOP_K = 2

        def rmsnorm(x, w, eps=1e-06):
            xf = x.astype(jnp.float32)
            n = jax.lax.rsqrt(jnp.mean(xf * xf, axis=-1, keepdims=True) + eps)
            return (xf * n).astype(x.dtype) * w

        def rope_tables(seq_len, head_dim):
            freqs = 1.0 / ROPE_THETA ** (jnp.arange(0, head_dim, 2, dtype=jnp.float32) / head_dim)
            t = jnp.arange(seq_len, dtype=jnp.float32)
            f = jnp.outer(t, freqs)
            return (jnp.cos(f), jnp.sin(f))

        def apply_rope(x, cos, sin):
            half = x.shape[-1] // 2
            x1, x2 = (x[..., :half], x[..., half:])
            c = cos[None, None]
            s = sin[None, None]
            return jnp.concatenate([x1 * c - x2 * s, x2 * c + x1 * s], axis=-1)
        key = jax.random.key(seed)
        ks = jax.random.split(key, 8)
        B, S, D = (2, 256, 256)
        Hq, Hkv, hd = (16, 4, 128)
        E, I = (8, 176)
        sc = 0.02
        return {'hidden': jax.random.normal(ks[0], (B, S, D), jnp.float32), 'attn_norm_w': jnp.ones((D,), jnp.float32), 'q_w': jax.random.normal(ks[1], (Hq * hd, D), jnp.float32) * sc, 'k_w': jax.random.normal(ks[2], (Hkv * hd, D), jnp.float32) * sc, 'v_w': jax.random.normal(ks[3], (Hkv * hd, D), jnp.float32) * sc, 'o_w': jax.random.normal(ks[4], (D, Hq * hd), jnp.float32) * sc, 'q_norm_w': jnp.ones((hd,), jnp.float32), 'k_norm_w': jnp.ones((hd,), jnp.float32), 'ffn_norm_w': jnp.ones((D,), jnp.float32), 'gate_w': jax.random.normal(ks[5], (E, D), jnp.float32) * sc, 'wg': jax.random.normal(ks[6], (E, I, D), jnp.float32) * sc, 'wu': jax.random.normal(ks[7], (E, I, D), jnp.float32) * sc, 'wd': jax.random.normal(jax.random.fold_in(key, 99), (E, D, I), jnp.float32) * sc}
    _L1_ffn_all = _L1_ffn_setup()
    _L1_ffn_in = {k: v for k, v in _L1_ffn_all.items() if k in ('attn_norm_w', 'q_w', 'k_w', 'v_w', 'o_w', 'q_norm_w', 'k_norm_w', 'ffn_norm_w', 'gate_w', 'wg', 'wu', 'wd')}
    del _L1_ffn_all
    return {'x': x, 'fside_BxSxS_0': fside_BxSxS_0, 'cond_512': cond_512, 'L0_cond_w': _L0_cond_in['w'], 'L0_cond_u': _L0_cond_in['u'], 'L0_attn_W_in': _L0_attn_in['W_in'], 'L0_attn_conv_w': _L0_attn_in['conv_w'], 'L0_attn_conv_b': _L0_attn_in['conv_b'], 'L0_attn_dt_bias': _L0_attn_in['dt_bias'], 'L0_attn_A_log': _L0_attn_in['A_log'], 'L0_attn_D_param': _L0_attn_in['D_param'], 'L0_attn_norm_w': _L0_attn_in['norm_w'], 'L0_attn_W_out': _L0_attn_in['W_out'], 'L0_cond2_w': _L0_cond2_in['w'], 'L0_cond2_u': _L0_cond2_in['u'], 'L0_ffn_gate_w': _L0_ffn_in['gate_w'], 'L0_ffn_gate_b': _L0_ffn_in['gate_b'], 'L0_ffn_w1_shared': _L0_ffn_in['w1_shared'], 'L0_ffn_w2_shared': _L0_ffn_in['w2_shared'], 'L0_ffn_w3_shared': _L0_ffn_in['w3_shared'], 'L0_ffn_w1_routed': _L0_ffn_in['w1_routed'], 'L0_ffn_w2_routed': _L0_ffn_in['w2_routed'], 'L0_ffn_w3_routed': _L0_ffn_in['w3_routed'], 'L1_cond_w': _L1_cond_in['w'], 'L1_cond_u': _L1_cond_in['u'], 'L1_attn_W_dq': _L1_attn_in['W_dq'], 'L1_attn_W_uq': _L1_attn_in['W_uq'], 'L1_attn_q_ln_g': _L1_attn_in['q_ln_g'], 'L1_attn_q_ln_b': _L1_attn_in['q_ln_b'], 'L1_attn_W_dkv': _L1_attn_in['W_dkv'], 'L1_attn_W_ukv': _L1_attn_in['W_ukv'], 'L1_attn_kv_ln_g': _L1_attn_in['kv_ln_g'], 'L1_attn_kv_ln_b': _L1_attn_in['kv_ln_b'], 'L1_attn_W_o': _L1_attn_in['W_o'], 'L1_cond2_w': _L1_cond2_in['w'], 'L1_cond2_u': _L1_cond2_in['u'], 'L1_ffn_attn_norm_w': _L1_ffn_in['attn_norm_w'], 'L1_ffn_q_w': _L1_ffn_in['q_w'], 'L1_ffn_k_w': _L1_ffn_in['k_w'], 'L1_ffn_v_w': _L1_ffn_in['v_w'], 'L1_ffn_o_w': _L1_ffn_in['o_w'], 'L1_ffn_q_norm_w': _L1_ffn_in['q_norm_w'], 'L1_ffn_k_norm_w': _L1_ffn_in['k_norm_w'], 'L1_ffn_ffn_norm_w': _L1_ffn_in['ffn_norm_w'], 'L1_ffn_gate_w': _L1_ffn_in['gate_w'], 'L1_ffn_wg': _L1_ffn_in['wg'], 'L1_ffn_wu': _L1_ffn_in['wu'], 'L1_ffn_wd': _L1_ffn_in['wd']}

def reference(x, fside_BxSxS_0, cond_512, L0_cond_w, L0_cond_u, L0_attn_W_in, L0_attn_conv_w, L0_attn_conv_b, L0_attn_dt_bias, L0_attn_A_log, L0_attn_D_param, L0_attn_norm_w, L0_attn_W_out, L0_cond2_w, L0_cond2_u, L0_ffn_gate_w, L0_ffn_gate_b, L0_ffn_w1_shared, L0_ffn_w2_shared, L0_ffn_w3_shared, L0_ffn_w1_routed, L0_ffn_w2_routed, L0_ffn_w3_routed, L1_cond_w, L1_cond_u, L1_attn_W_dq, L1_attn_W_uq, L1_attn_q_ln_g, L1_attn_q_ln_b, L1_attn_W_dkv, L1_attn_W_ukv, L1_attn_kv_ln_g, L1_attn_kv_ln_b, L1_attn_W_o, L1_cond2_w, L1_cond2_u, L1_ffn_attn_norm_w, L1_ffn_q_w, L1_ffn_k_w, L1_ffn_v_w, L1_ffn_o_w, L1_ffn_q_norm_w, L1_ffn_k_norm_w, L1_ffn_ffn_norm_w, L1_ffn_gate_w, L1_ffn_wg, L1_ffn_wu, L1_ffn_wd):
    import jax
    import jax.numpy as jnp

    def _L0_cond_ref(r, k, v, w, u, time_emb):
        import jax, jax.numpy as jnp
        from jax import lax
        import numpy as np
        B, T, C, TD = (8, 256, 256, 64)

        def _bi_wkv(r, k, v, w, u, time_emb):
            tf = jax.nn.sigmoid(jnp.sum(time_emb, axis=-1))[:, None, None]
            decay = jnp.exp(-jnp.exp(w.astype(jnp.float32)))[None, :] * (0.5 + 0.5 * tf[:, :, 0])
            kf = k.astype(jnp.float32)
            vf = v.astype(jnp.float32)
            ek = jnp.exp(jnp.minimum(kf, 30.0))
            ekv = ek * vf

            def step(carry, x):
                a, b = carry
                ekv_t, ek_t = x
                a = a * decay + ekv_t
                b = b * decay + ek_t
                return ((a, b), (a, b))
            ekv_t = jnp.swapaxes(ekv, 0, 1)
            ek_t = jnp.swapaxes(ek, 0, 1)
            init = (jnp.zeros_like(decay), jnp.zeros_like(decay))
            _, (nf, df) = lax.scan(step, init, (ekv_t, ek_t))
            _, (nb, db) = lax.scan(step, init, (ekv_t, ek_t), reverse=True)
            nf = jnp.swapaxes(nf, 0, 1)
            df = jnp.swapaxes(df, 0, 1)
            nb = jnp.swapaxes(nb, 0, 1)
            db = jnp.swapaxes(db, 0, 1)
            euk = jnp.exp(jnp.minimum(u.astype(jnp.float32)[None, None, :] + kf, 30.0))
            num = nf + nb - ekv + euk * vf
            den = df + db - ek + euk
            base = jax.nn.sigmoid(r.astype(jnp.float32)) * (num / jnp.maximum(den, 1e-08))
            out = base * (0.8 + 0.2 * tf)
            return out.astype(r.dtype)
        return _bi_wkv(r, k, v, w, u, time_emb)

    def _L0_attn_ref(hidden_states, W_in, conv_w, conv_b, dt_bias, A_log, D_param, norm_w, W_out):
        import jax, jax.numpy as jnp
        import numpy as np
        B_, L, D_MODEL = (2, 512, 256)
        H, P, N, G, K = (32, 64, 128, 1, 4)
        EPS = 1e-05
        INTER = H * P
        CONV_DIM = INTER + 2 * G * N
        PROJ = INTER + CONV_DIM + H

        def _silu(x):
            return x * jax.nn.sigmoid(x)

        def _mamba2_mixer(hidden_states, W_in, conv_w, conv_b, dt_bias, A_log, D_param, norm_w, W_out):
            b, l, _ = hidden_states.shape
            proj = jnp.einsum('bld,pd->blp', hidden_states, W_in)
            gate = proj[..., :INTER]
            hBC = proj[..., INTER:INTER + CONV_DIM]
            dt = proj[..., INTER + CONV_DIM:]
            xc = jnp.transpose(hBC, (0, 2, 1))
            conv = jax.lax.conv_general_dilated(xc, conv_w[:, None, :], window_strides=(1,), padding=[(K - 1, 0)], dimension_numbers=('NCH', 'OIH', 'NCH'), feature_group_count=CONV_DIM)
            hBC = _silu(jnp.transpose(conv + conv_b[None, :, None], (0, 2, 1)))
            xs = hBC[..., :INTER].reshape(b, l, H, P)
            Bm = hBC[..., INTER:INTER + G * N].reshape(b, l, G, N)
            Cm = hBC[..., INTER + G * N:].reshape(b, l, G, N)
            Bh = jnp.repeat(Bm, H // G, axis=2)
            Ch = jnp.repeat(Cm, H // G, axis=2)
            dt = jax.nn.softplus(dt + dt_bias)
            A = -jnp.exp(A_log)
            dA = jnp.exp(dt * A)

            def step(h, inp):
                dA_t, dt_t, x_t, B_t, C_t = inp
                u = (dt_t[:, :, None] * x_t)[..., None] * B_t[:, :, None, :]
                h = dA_t[:, :, None, None] * h + u
                y = jnp.einsum('bhpn,bhn->bhp', h, C_t)
                return (h, y)
            tm = lambda a: jnp.moveaxis(a, 1, 0)
            h0 = jnp.zeros((b, H, P, N), hidden_states.dtype)
            _, ys = jax.lax.scan(step, h0, (tm(dA), tm(dt), tm(xs), tm(Bh), tm(Ch)))
            y = jnp.moveaxis(ys, 0, 1) + D_param[None, None, :, None] * xs
            y = y.reshape(b, l, INTER)
            g = y * _silu(gate)
            g = g * jax.lax.rsqrt(jnp.mean(g * g, axis=-1, keepdims=True) + EPS) * norm_w
            return jnp.einsum('bli,di->bld', g, W_out)
        return _mamba2_mixer(hidden_states, W_in, conv_w, conv_b, dt_bias, A_log, D_param, norm_w, W_out)

    def _L0_cond2_ref(r, k, v, w, u, time_emb):
        import jax, jax.numpy as jnp
        from jax import lax
        import numpy as np
        B, T, C, TD = (8, 256, 256, 64)

        def _bi_wkv(r, k, v, w, u, time_emb):
            tf = jax.nn.sigmoid(jnp.sum(time_emb, axis=-1))[:, None, None]
            decay = jnp.exp(-jnp.exp(w.astype(jnp.float32)))[None, :] * (0.5 + 0.5 * tf[:, :, 0])
            kf = k.astype(jnp.float32)
            vf = v.astype(jnp.float32)
            ek = jnp.exp(jnp.minimum(kf, 30.0))
            ekv = ek * vf

            def step(carry, x):
                a, b = carry
                ekv_t, ek_t = x
                a = a * decay + ekv_t
                b = b * decay + ek_t
                return ((a, b), (a, b))
            ekv_t = jnp.swapaxes(ekv, 0, 1)
            ek_t = jnp.swapaxes(ek, 0, 1)
            init = (jnp.zeros_like(decay), jnp.zeros_like(decay))
            _, (nf, df) = lax.scan(step, init, (ekv_t, ek_t))
            _, (nb, db) = lax.scan(step, init, (ekv_t, ek_t), reverse=True)
            nf = jnp.swapaxes(nf, 0, 1)
            df = jnp.swapaxes(df, 0, 1)
            nb = jnp.swapaxes(nb, 0, 1)
            db = jnp.swapaxes(db, 0, 1)
            euk = jnp.exp(jnp.minimum(u.astype(jnp.float32)[None, None, :] + kf, 30.0))
            num = nf + nb - ekv + euk * vf
            den = df + db - ek + euk
            base = jax.nn.sigmoid(r.astype(jnp.float32)) * (num / jnp.maximum(den, 1e-08))
            out = base * (0.8 + 0.2 * tf)
            return out.astype(r.dtype)
        return _bi_wkv(r, k, v, w, u, time_emb)

    def _L0_ffn_ref(x, gate_w, gate_b, w1_shared, w2_shared, w3_shared, w1_routed, w2_routed, w3_routed):
        import jax, jax.numpy as jnp
        import numpy as np
        TOP_K = 4
        n_experts = w1_routed.shape[0]
        logits = jnp.einsum('ed,btd->bte', gate_w, x)
        scores = jax.nn.sigmoid(logits) + gate_b
        weights, indices = jax.lax.top_k(scores, TOP_K)
        weights = weights / weights.sum(-1, keepdims=True)
        shared_out = jax.nn.silu(x @ w1_shared) * (x @ w3_shared) @ w2_shared
        one_hot = jax.nn.one_hot(indices, n_experts, dtype=x.dtype)
        router_probs = (weights[..., None] * one_hot).sum(-2)
        h1 = jnp.einsum('btd,edc->btec', x, w1_routed)
        h2 = jnp.einsum('btd,edc->btec', x, w3_routed)
        h3 = jax.nn.silu(h1 * h2)
        experts_out = jnp.einsum('btec,ecd->bted', h3, w2_routed)
        routed_out = jnp.einsum('bted,bte->btd', experts_out, router_probs)
        return shared_out + routed_out

    def _L1_cond_ref(r, k, v, w, u, time_emb):
        import jax, jax.numpy as jnp
        from jax import lax
        import numpy as np
        B, T, C, TD = (8, 256, 256, 64)

        def _bi_wkv(r, k, v, w, u, time_emb):
            tf = jax.nn.sigmoid(jnp.sum(time_emb, axis=-1))[:, None, None]
            decay = jnp.exp(-jnp.exp(w.astype(jnp.float32)))[None, :] * (0.5 + 0.5 * tf[:, :, 0])
            kf = k.astype(jnp.float32)
            vf = v.astype(jnp.float32)
            ek = jnp.exp(jnp.minimum(kf, 30.0))
            ekv = ek * vf

            def step(carry, x):
                a, b = carry
                ekv_t, ek_t = x
                a = a * decay + ekv_t
                b = b * decay + ek_t
                return ((a, b), (a, b))
            ekv_t = jnp.swapaxes(ekv, 0, 1)
            ek_t = jnp.swapaxes(ek, 0, 1)
            init = (jnp.zeros_like(decay), jnp.zeros_like(decay))
            _, (nf, df) = lax.scan(step, init, (ekv_t, ek_t))
            _, (nb, db) = lax.scan(step, init, (ekv_t, ek_t), reverse=True)
            nf = jnp.swapaxes(nf, 0, 1)
            df = jnp.swapaxes(df, 0, 1)
            nb = jnp.swapaxes(nb, 0, 1)
            db = jnp.swapaxes(db, 0, 1)
            euk = jnp.exp(jnp.minimum(u.astype(jnp.float32)[None, None, :] + kf, 30.0))
            num = nf + nb - ekv + euk * vf
            den = df + db - ek + euk
            base = jax.nn.sigmoid(r.astype(jnp.float32)) * (num / jnp.maximum(den, 1e-08))
            out = base * (0.8 + 0.2 * tf)
            return out.astype(r.dtype)
        return _bi_wkv(r, k, v, w, u, time_emb)

    def _L1_attn_ref(x, W_dq, W_uq, q_ln_g, q_ln_b, W_dkv, W_ukv, kv_ln_g, kv_ln_b, W_o):
        import jax, jax.numpy as jnp
        import numpy as np
        import math
        D_MODEL = 256
        N_HEADS = 16
        Q_PROJ = D_MODEL // 4
        KV_PROJ = D_MODEL // 4
        DH = D_MODEL // N_HEADS
        LN_EPS = 1e-05

        def _layernorm(x, gamma, beta):
            mu = jnp.mean(x, axis=-1, keepdims=True)
            var = jnp.var(x, axis=-1, keepdims=True)
            return (x - mu) * jax.lax.rsqrt(var + LN_EPS) * gamma + beta
        B, S, D = x.shape
        H, dh = (N_HEADS, DH)
        cq = _layernorm(x @ W_dq, q_ln_g, q_ln_b)
        Q = cq @ W_uq
        ckv = _layernorm(x @ W_dkv, kv_ln_g, kv_ln_b)
        KV = ckv @ W_ukv
        K, V = (KV[..., :D], KV[..., D:])
        q = Q.reshape(B, S, H, dh).transpose(0, 2, 1, 3)
        k = K.reshape(B, S, H, dh).transpose(0, 2, 1, 3)
        v = V.reshape(B, S, H, dh).transpose(0, 2, 1, 3)
        scores = jnp.einsum('bhqd,bhkd->bhqk', q, k) / math.sqrt(float(dh))
        causal = jnp.tril(jnp.ones((S, S), dtype=bool))
        scores = jnp.where(causal, scores, -jnp.inf)
        attn = jax.nn.softmax(scores, axis=-1)
        o = jnp.einsum('bhqk,bhkd->bhqd', attn, v)
        o = o.transpose(0, 2, 1, 3).reshape(B, S, D)
        return o @ W_o.T

    def _L1_cond2_ref(r, k, v, w, u, time_emb):
        import jax, jax.numpy as jnp
        from jax import lax
        import numpy as np
        B, T, C, TD = (8, 256, 256, 64)

        def _bi_wkv(r, k, v, w, u, time_emb):
            tf = jax.nn.sigmoid(jnp.sum(time_emb, axis=-1))[:, None, None]
            decay = jnp.exp(-jnp.exp(w.astype(jnp.float32)))[None, :] * (0.5 + 0.5 * tf[:, :, 0])
            kf = k.astype(jnp.float32)
            vf = v.astype(jnp.float32)
            ek = jnp.exp(jnp.minimum(kf, 30.0))
            ekv = ek * vf

            def step(carry, x):
                a, b = carry
                ekv_t, ek_t = x
                a = a * decay + ekv_t
                b = b * decay + ek_t
                return ((a, b), (a, b))
            ekv_t = jnp.swapaxes(ekv, 0, 1)
            ek_t = jnp.swapaxes(ek, 0, 1)
            init = (jnp.zeros_like(decay), jnp.zeros_like(decay))
            _, (nf, df) = lax.scan(step, init, (ekv_t, ek_t))
            _, (nb, db) = lax.scan(step, init, (ekv_t, ek_t), reverse=True)
            nf = jnp.swapaxes(nf, 0, 1)
            df = jnp.swapaxes(df, 0, 1)
            nb = jnp.swapaxes(nb, 0, 1)
            db = jnp.swapaxes(db, 0, 1)
            euk = jnp.exp(jnp.minimum(u.astype(jnp.float32)[None, None, :] + kf, 30.0))
            num = nf + nb - ekv + euk * vf
            den = df + db - ek + euk
            base = jax.nn.sigmoid(r.astype(jnp.float32)) * (num / jnp.maximum(den, 1e-08))
            out = base * (0.8 + 0.2 * tf)
            return out.astype(r.dtype)
        return _bi_wkv(r, k, v, w, u, time_emb)

    def _L1_ffn_ref(hidden, attn_norm_w, q_w, k_w, v_w, o_w, q_norm_w, k_norm_w, ffn_norm_w, gate_w, wg, wu, wd):
        import jax, jax.numpy as jnp
        import numpy as np
        ROPE_THETA = 1000000.0
        TOP_K = 2

        def rmsnorm(x, w, eps=1e-06):
            xf = x.astype(jnp.float32)
            n = jax.lax.rsqrt(jnp.mean(xf * xf, axis=-1, keepdims=True) + eps)
            return (xf * n).astype(x.dtype) * w

        def rope_tables(seq_len, head_dim):
            freqs = 1.0 / ROPE_THETA ** (jnp.arange(0, head_dim, 2, dtype=jnp.float32) / head_dim)
            t = jnp.arange(seq_len, dtype=jnp.float32)
            f = jnp.outer(t, freqs)
            return (jnp.cos(f), jnp.sin(f))

        def apply_rope(x, cos, sin):
            half = x.shape[-1] // 2
            x1, x2 = (x[..., :half], x[..., half:])
            c = cos[None, None]
            s = sin[None, None]
            return jnp.concatenate([x1 * c - x2 * s, x2 * c + x1 * s], axis=-1)
        B, S, D = hidden.shape
        hd = q_norm_w.shape[0]
        Hq = q_w.shape[0] // hd
        Hkv = k_w.shape[0] // hd
        n_rep = Hq // Hkv
        h = rmsnorm(hidden, attn_norm_w)
        q = (h @ q_w.T).reshape(B, S, Hq, hd)
        k = (h @ k_w.T).reshape(B, S, Hkv, hd)
        v = (h @ v_w.T).reshape(B, S, Hkv, hd)
        q = rmsnorm(q, q_norm_w).transpose(0, 2, 1, 3)
        k = rmsnorm(k, k_norm_w).transpose(0, 2, 1, 3)
        v = v.transpose(0, 2, 1, 3)
        cos, sin = rope_tables(S, hd)
        q = apply_rope(q, cos, sin)
        k = apply_rope(k, cos, sin)
        k = jnp.repeat(k, n_rep, axis=1)
        v = jnp.repeat(v, n_rep, axis=1)
        scale = 1.0 / jnp.sqrt(jnp.float32(hd))
        scores = jnp.einsum('bhqd,bhkd->bhqk', q, k) * scale
        causal = jnp.tril(jnp.ones((S, S), bool))
        scores = jnp.where(causal[None, None], scores, jnp.finfo(scores.dtype).min)
        attn = jnp.einsum('bhqk,bhkd->bhqd', jax.nn.softmax(scores, axis=-1), v)
        attn = attn.transpose(0, 2, 1, 3).reshape(B, S, Hq * hd)
        hidden = hidden + attn @ o_w.T
        h2 = rmsnorm(hidden, ffn_norm_w)
        T = B * S
        E = gate_w.shape[0]
        tok = h2.reshape(T, D)
        probs = jax.nn.softmax(tok @ gate_w.T, axis=-1)
        topv, topi = jax.lax.top_k(probs, TOP_K)
        topw = topv / (jnp.sum(topv, axis=-1, keepdims=True) + 1e-09)
        combine = jnp.zeros((T, E), tok.dtype).at[jnp.arange(T)[:, None], topi].set(topw)
        eg = jnp.einsum('td,eid->eti', tok, wg)
        eu = jnp.einsum('td,eid->eti', tok, wu)
        eo = jnp.einsum('eti,edi->etd', jax.nn.silu(eg) * eu, wd)
        moe_out = jnp.einsum('te,etd->td', combine, eo).reshape(B, S, D)
        return hidden + moe_out
    x = x + _L0_attn_ref(_L0_cond_ref(x, fside_BxSxS_0, fside_BxSxS_0, L0_cond_w, L0_cond_u, cond_512), L0_attn_W_in, L0_attn_conv_w, L0_attn_conv_b, L0_attn_dt_bias, L0_attn_A_log, L0_attn_D_param, L0_attn_norm_w, L0_attn_W_out)
    x = x + _L0_ffn_ref(_L0_cond2_ref(x, fside_BxSxS_0, fside_BxSxS_0, L0_cond2_w, L0_cond2_u, cond_512), L0_ffn_gate_w, L0_ffn_gate_b, L0_ffn_w1_shared, L0_ffn_w2_shared, L0_ffn_w3_shared, L0_ffn_w1_routed, L0_ffn_w2_routed, L0_ffn_w3_routed)
    x = x + _L1_attn_ref(_L1_cond_ref(x, fside_BxSxS_0, fside_BxSxS_0, L1_cond_w, L1_cond_u, cond_512), L1_attn_W_dq, L1_attn_W_uq, L1_attn_q_ln_g, L1_attn_q_ln_b, L1_attn_W_dkv, L1_attn_W_ukv, L1_attn_kv_ln_g, L1_attn_kv_ln_b, L1_attn_W_o)
    x = x + _L1_ffn_ref(_L1_cond2_ref(x, fside_BxSxS_0, fside_BxSxS_0, L1_cond2_w, L1_cond2_u, cond_512), L1_ffn_attn_norm_w, L1_ffn_q_w, L1_ffn_k_w, L1_ffn_v_w, L1_ffn_o_w, L1_ffn_q_norm_w, L1_ffn_k_norm_w, L1_ffn_ffn_norm_w, L1_ffn_gate_w, L1_ffn_wg, L1_ffn_wu, L1_ffn_wd)
    return x

_drawn_inputs = setup_inputs


def setup_inputs(seed=0):
    import zlib

    import numpy as np

    out = dict(_drawn_inputs(seed))
    spreads = {'L0_attn_conv_b': (0.0, 0.1),
     'L0_attn_dt_bias': (1.0, 0.6),
     'L0_attn_D_param': (1.0, 0.2),
     'L0_attn_norm_w': (1.0, 0.2),
     'L1_attn_q_ln_g': (1.0, 0.6),
     'L1_attn_q_ln_b': (0.0, 0.8),
     'L1_attn_kv_ln_g': (1.0, 0.6),
     'L1_attn_kv_ln_b': (0.0, 0.8),
     'L1_ffn_attn_norm_w': (1.0, 0.6),
     'L1_ffn_q_norm_w': (1.0, 0.6),
     'L1_ffn_k_norm_w': (1.0, 0.6),
     'L1_ffn_ffn_norm_w': (1.0, 0.6)}
    factors = {'L0_attn_A_log': 8.0,
     'L0_cond2_w': 8.0,
     'L0_cond2_u': 8.0,
     'L0_ffn_gate_w': 8.0,
     'L0_ffn_gate_b': 8.0,
     'L0_ffn_w1_shared': 8.0,
     'L0_ffn_w2_shared': 8.0,
     'L0_ffn_w3_shared': 8.0,
     'L0_ffn_w1_routed': 8.0,
     'L0_ffn_w2_routed': 8.0,
     'L0_ffn_w3_routed': 8.0,
     'L1_cond_w': 8.0,
     'L1_cond_u': 8.0,
     'L1_attn_W_dq': 8.0,
     'L1_attn_W_uq': 8.0,
     'L1_attn_W_dkv': 8.0,
     'L1_attn_W_ukv': 8.0,
     'L1_attn_W_o': 8.0,
     'L1_ffn_gate_w': 8.0,
     'L1_ffn_wg': 7.779,
     'L1_ffn_wu': 7.925,
     'L1_ffn_wd': 7.708}
    for name, (base, spread) in spreads.items():
        noise = np.random.default_rng([zlib.crc32(name.encode()), seed]).standard_normal(out[name].shape)
        drawn = base * np.exp(spread * noise) if base else spread * noise
        out[name] = jnp.asarray(drawn.astype(out[name].dtype))
    for name, factor in factors.items():
        out[name] = (out[name] * factor).astype(out[name].dtype)
    return out
```

```python
from contextlib import ExitStack

import concourse.bass as bass
import numpy as np
from concourse import mybir

F32 = mybir.dt.float32
BF16 = mybir.dt.bfloat16
ALU = mybir.AluOpType
ACT = mybir.ActivationFunctionType
AX_X = mybir.AxisListType.X
ds = bass.ds

P = 128
BATCH, SEQ, D = 4, 256, 256
KT = D // P
PAIRS = 2
BB = BATCH // PAIRS
TOK = BB * SEQ
PAIR = KT * TOK
SEG = SEQ + 1
UNIT = KT * BB * SEG
ST = SEQ // P

HEADS, HEAD, STATE, TAPS = 32, 64, 128, 4
INNER = HEADS * HEAD
XT_TILES = INNER // P
CONV_TILES = XT_TILES + 2
TILE_HEADS = P // HEAD
TRI = SEQ + P
EPS_MIXER = 1e-5

FF = 176
E0, K0 = 16, 4
E1, K1 = 8, 2
SHARED_TILES = 2
MOE0_TILES = SHARED_TILES + E0 * FF // P
MOE1_TILES = E1 * FF // P
MOE_COLS = 3 * D

(PP_W, PP_U, PP_CONVW, PP_CONVB, PP_DTB, PP_ALOG, PP_D, PP_NORM, PP_EPS_MIXER, PP_LN_HALF, PP_LNG,
 PP_LNB, PP_EPS_LN, PP_ATTN_NORM, PP_FFN_NORM, PP_EPS_RMS, PP_HEADMASK, PP_COND, PP_GATEB,
 PP_QNORM, PP_KNORM, PP_END) = np.cumsum(
    [0, 4 * KT, 4 * KT, CONV_TILES * TAPS, CONV_TILES, 1, 1, XT_TILES, XT_TILES, 1, 1, 1, 1, 1,
     KT, KT, 1, 8, BATCH * 64, E0, 1, 1]).tolist()

CB_IDENT, CB_MASK_QK, CB_MASK_ST, CB_SEL, CB_END = np.cumsum([0, P, SEQ, P, HEADS * P]).tolist()

W_DT, W_BCXG, W_OUT0 = np.cumsum([0, KT * HEADS, (2 * XT_TILES + 2) * KT * P]).tolist()
W_MIXER = W_OUT0 + XT_TILES * D


STAGE_SEMS = 44


class Links:

    def __init__(self, engine, sem, i=0, per=0):
        self.engine, self.sem, self.i, self.per, self.n = engine, sem, i, per, 0

    def __call__(self, instruction):
        self.n += 1
        instruction.then_inc(self.sem, 1)
        self.engine.wait_ge(self.sem, self.i * self.per + self.n)
        return instruction

    def check(self):
        assert self.n == self.per, self.n


class Net:

    def __init__(self, nc, stack, dram):
        self.nc, self.stack, self.dram = nc, stack, dram

        def sb(name, shape, dt=F32):
            return stack.enter_context(nc.sbuf_tensor(name, shape, dt))

        self.x = sb("x_res", [P, PAIRS * PAIR])
        self.h = sb("h", [P, PAIRS * PAIR])
        self.m = sb("m", [P, PAIRS * PAIR])
        self.f = sb("f", [P, PAIRS * UNIT])
        self.e = sb("e", [P, PAIRS * UNIT])
        self.e_pair = sb("e_pair", [P, UNIT])
        self.ev_pair = sb("ev_pair", [P, UNIT])
        self.decay = sb("decay", [P, UNIT])
        self.num = sb("num", [P, UNIT])
        self.num_b = sb("num_b", [P, UNIT])
        self.den = sb("den", [P, UNIT])
        self.den_b = sb("den_b", [P, UNIT])
        self.euk = sb("euk", [P, UNIT])
        self.pp = sb("pp", [P, PP_END])
        self.cb = sb("cb", [P, CB_SEL], BF16)
        self.ident = sb("ident", [P, P])
        self.ones = sb("ones", [P, P])
        self.dcol = sb("dcol", [P, 4 * KT * BATCH])
        self.scol = sb("scol", [P, BATCH])
        self.tf = sb("tf", [P, 3 * BATCH])

        def sem(name):
            return stack.enter_context(nc.semaphore(name))

        self.sem = sem
        self.stage, self.named = 0, 0
        ids = [nc.alloc_semaphore(f"stage_sem{n}") for n in range(2 * STAGE_SEMS)]
        for handle in ids:
            nc.release_semaphore(handle)
        self.banks = [[handle.num for handle in ids[n * STAGE_SEMS:(n + 1) * STAGE_SEMS]]
                      for n in range(2)]
        self.params_loaded = sem("params_loaded")
        self.x_loaded = sem("x_loaded")
        self.f_loaded = sem("f_loaded")
        self.win_loaded = [sem(f"win_loaded{n}") for n in range(4)]
        self.out_stored = sem("out_stored")
        self.consts_made = sem("consts_made")


    def next_stage(self):
        self.stage, self.named = self.stage + 1, 0

    def stage_sem(self, mem, name):
        self.named += 1
        return mem.enter_context(
            self.nc.semaphore(name, num=self.banks[self.stage % 2][self.named - 1]))

    def clear_last_stage(self, pool):
        if self.stage > 1:
            bank = self.banks[(self.stage - 1) % 2]
            pool.sem_clear(range(bank[0], bank[-1] + 1))



class CondUnit:

    VECTOR_LINKS = 13

    def __init__(self, net, c, sems):
        self.net, self.c = net, c
        self.u_ready, self.euk_ready, self.operand_ready, self.scans_done = sems

    def pool(self, pair, turn):
        net, nc = self.net, self.net.nc
        nc.gpsimd.wait_ge(self.scans_done, turn)
        for kt in range(KT):
            src = net.dcol[:, ds((self.c * KT + kt) * BATCH + pair * BB, BB)]
            last = nc.gpsimd.tensor_tensor(
                net.decay[:, kt * BB * SEG:(kt + 1) * BB * SEG].rearrange(
                    "p (b t) -> p b t", b=BB)[:, :, 1:SEG],
                src[:, :, None].to_broadcast([P, BB, SEQ]),
                net.ones[:, 0:1, None].to_broadcast([P, BB, SEQ]), ALU.mult)
            last.then_inc(self.operand_ready, 1)
        unit = ds(pair * UNIT, UNIT)
        nc.gpsimd.tensor_tensor(net.ev_pair[:], net.e[:, unit], net.f[:, unit], ALU.mult) \
            .then_inc(self.operand_ready, 1)
        nc.gpsimd.tensor_tensor(net.e_pair[:], net.e[:, unit],
                                net.ones[:, 0:1].to_broadcast([P, UNIT]), ALU.mult) \
            .then_inc(self.operand_ready, 1)

    def scalar(self, turn):
        net, nc = self.net, self.net.nc
        nc.scalar.wait_ge(self.u_ready, turn + 1)
        nc.scalar.activation(net.euk[:], net.euk[:], ACT.Exp).then_inc(self.euk_ready, 1)

    def vector(self, link, pair, turn):
        net, nc, c = self.net, self.net.nc, self.c
        v = nc.vector
        unit = ds(pair * UNIT, UNIT)

        def add_u():
            for kt in range(KT):
                n = BB * SEG
                op = v.tensor_scalar(net.euk[:, kt * n:(kt + 1) * n],
                                     net.f[:, ds(pair * UNIT + kt * n, n)],
                                     net.pp[:, PP_U + c * KT + kt:PP_U + c * KT + kt + 1], 30.0,
                                     ALU.add, ALU.min)
            op.then_inc(self.u_ready, 1)

        def scan(out, x, operands, reverse):
            def step():
                v.wait_ge(self.operand_ready, 4 * turn + operands)
                o, dcy = out[:], net.decay[:]
                if reverse:
                    o, dcy, x_ = out[:, ::-1], net.decay[:, ::-1], x[:, ::-1]
                else:
                    x_ = x
                op = v.tensor_tensor_scan(o, dcy, x_, 0.0, ALU.mult, ALU.add)
                if out is net.den_b:
                    op.then_inc(self.scans_done, 1)
                    v.wait_ge(self.scans_done, turn + 1)
                else:
                    link(op)
            return step

        def tt(out, a, b, op):
            return lambda: link(v.tensor_tensor(out, a, b, op))

        def extra():
            v.wait_ge(self.euk_ready, turn + 1)
            link(v.tensor_tensor(net.euk[:], net.euk[:], net.e[:, unit], ALU.subtract))

        def finish():
            link(v.tensor_scalar(net.den[:], net.den[:], 1e-8, None, ALU.max))
            link(v.reciprocal(net.den[:], net.den[:]))

        def out():
            for b in range(BB):
                shape = dict(k=KT, b=BB)
                num = net.num[:].rearrange("p (k b t) -> p k b t", **shape)[:, :, b, 1:SEG]
                den = net.den[:].rearrange("p (k b t) -> p k b t", **shape)[:, :, b, 1:SEG]
                m = net.m[:, ds(pair * PAIR, PAIR)].rearrange("p (k b t) -> p k b t", **shape)
                link(v.scalar_tensor_tensor(m[:, :, b, :], num, net.scol[:, ds(pair * BB + b, 1)],
                                            den, ALU.mult, ALU.mult))

        return [
            add_u,
            scan(net.den, net.e[:, unit], 2, False),
            scan(net.num, net.ev_pair[:], 3, False), scan(net.num_b, net.ev_pair[:], 3, True),
            scan(net.den_b, net.e_pair[:], 4, True),
            tt(net.num[:], net.num[:], net.num_b[:], ALU.add),
            tt(net.den[:], net.den[:], net.den_b[:], ALU.add),
            extra,
            tt(net.den[:], net.den[:], net.euk[:], ALU.add),
            tt(net.euk[:], net.euk[:], net.f[:, unit], ALU.mult),
            tt(net.num[:], net.num[:], net.euk[:], ALU.add),
            finish, out,
        ]


def stage_condition(net):
    nc, dram = net.nc, net.dram
    sem = net.sem
    e0_exp, e_padded = sem("e0_exp"), sem("e_padded")
    min_ready = sem("min_ready")
    tf_sum, tf_tanh, w_exp = sem("tf_sum"), sem("tf_tanh"), sem("w_exp")
    cols_ready = sem("cols_ready")
    pads_ready, links = sem("pads_ready"), sem("cond_links")
    net.cond_sems = [sem(n) for n in ("u_ready", "euk_ready", "operand_ready", "scans_done")]
    unit = CondUnit(net, 0, net.cond_sems)

    with nc.Block() as block:
        @block.sync
        def _(sp):
            sp.dma_start(net.pp[:], dram["pp"]).then_inc(net.params_loaded, 16)
            sp.dma_start(net.cb[:], dram["cb"][:, 0:CB_SEL]).then_inc(net.params_loaded, 16)
            sp.dma_start(net.ident[:], dram["ident"]).then_inc(net.params_loaded, 16)
            for p in range(PAIRS):
                rows = net.f[:, p * UNIT:(p + 1) * UNIT].rearrange("p (r t) -> p r t", t=SEG)
                src = dram["f"][:, p * PAIR:(p + 1) * PAIR].rearrange("p (r t) -> p r t", t=SEQ)
                sp.dma_start(rows[:, :, 1:SEG], src).then_inc(net.f_loaded, 16)
            sp.dma_start(net.x[:], dram["x"]).then_inc(net.x_loaded, 16)
            for n, (a, b) in enumerate(net.win_chunks):
                sp.dma_start(net.weights[:, a:b], dram["w_mixer"][:, a:b]).then_inc(
                    net.win_loaded[n], 16)

        @block.gpsimd
        def _(pool):
            nc.gpsimd.memset(net.ones[:], 1.0).then_inc(net.consts_made, 1)
            pool.wait_ge(net.consts_made, 1)
            nc.gpsimd.memset(net.f[:].rearrange("p (r t) -> p r t", t=SEG)[:, :, 0:1], 0.0) \
                .then_inc(pads_ready, 1)
            nc.gpsimd.memset(net.decay[:].rearrange("p (r t) -> p r t", t=SEG)[:, :, 0:1], 0.0) \
                .then_inc(pads_ready, 1)
            pool.wait_ge(cols_ready, 3)
            pool.wait_ge(e_padded, 1)
            for pair in range(PAIRS):
                unit.pool(pair, pair)

        @block.scalar
        def _(act):
            act.wait_ge(net.params_loaded, 48)
            w = net.pp[:, PP_W:PP_W + 4 * KT]
            nc.scalar.activation(w, w, ACT.Exp).then_inc(w_exp, 1)
            act.wait_ge(w_exp, 1)
            nc.scalar.activation(w, w, ACT.Exp, scale=-1.0).then_inc(w_exp, 1)
            act.wait_ge(tf_sum, 1)
            nc.scalar.activation(net.tf[:, 0:BATCH], net.tf[:, 0:BATCH], ACT.Tanh, scale=0.5) \
                .then_inc(tf_tanh, 1)
            act.wait_ge(min_ready, 1)
            nc.scalar.activation(net.e[:], net.e[:], ACT.Exp).then_inc(e0_exp, 1)
            for turn in range(PAIRS):
                unit.scalar(turn)

        @block.vector
        def _(dve):
            v = nc.vector
            link = Links(dve, links)
            dve.wait_ge(net.params_loaded, 48)
            cond = net.pp[:, PP_COND:PP_COND + BATCH * 64].rearrange("p (b c) -> p b c", b=BATCH)
            v.tensor_reduce(net.tf[:, 0:BATCH], cond, AX_X, ALU.add).then_inc(tf_sum, 1)
            dve.wait_ge(tf_tanh, 1)
            v.tensor_scalar(net.tf[:, BATCH:2 * BATCH], net.tf[:, 0:BATCH], 0.25, 0.75, ALU.mult,
                            ALU.add).then_inc(cols_ready, 1)
            v.tensor_scalar(net.scol[:], net.tf[:, 0:BATCH], 0.05, 0.45, ALU.mult,
                            ALU.add).then_inc(cols_ready, 1)
            dve.wait_ge(w_exp, 2)
            dve.wait_ge(cols_ready, 2)
            v.tensor_tensor(
                net.dcol[:].rearrange("p (c b) -> p c b", b=BATCH),
                net.pp[:, PP_W:PP_W + 4 * KT][:, :, None].to_broadcast([P, 4 * KT, BATCH]),
                net.tf[:, BATCH:2 * BATCH][:, None, :].to_broadcast([P, 4 * KT, BATCH]),
                ALU.mult).then_inc(cols_ready, 1)
            dve.wait_ge(net.f_loaded, 32)
            dve.wait_ge(pads_ready, 2)
            v.tensor_scalar(net.e[:], net.f[:], 30.0, None, ALU.min).then_inc(min_ready, 1)
            dve.wait_ge(e0_exp, 1)
            v.memset(net.e[:].rearrange("p (r t) -> p r t", t=SEG)[:, :, 0:1], 0.0) \
                .then_inc(e_padded, 1)
            dve.wait_ge(e_padded, 1)
            for pair in range(PAIRS):
                for step in unit.vector(link, pair, pair):
                    step()


def condition_input(net, tag):
    nc = net.nc
    half_tanh, h_ready = net.sem(f"half_tanh{tag}"), net.sem(f"h_ready{tag}")

    def scalar():
        nc.scalar.wait_ge(net.x_loaded, 16)
        for pair in range(PAIRS):
            s = slice(pair * PAIR, (pair + 1) * PAIR)
            nc.scalar.activation(net.h[:, s], net.x[:, s], ACT.Tanh, scale=0.5) \
                .then_inc(half_tanh, 1)

    def vector():
        nc.vector.wait_ge(net.x_loaded, 16)
        for pair in range(PAIRS):
            s = slice(pair * PAIR, (pair + 1) * PAIR)
            nc.vector.wait_ge(half_tanh, pair + 1)
            nc.vector.scalar_tensor_tensor(net.h[:, s], net.h[:, s], 1.0, net.m[:, s], ALU.add,
                                           ALU.mult).then_inc(h_ready, 1)

    return scalar, vector, h_ready



LAG_HEADS, LAG_Y, LAG_OUT = 2, 3, 4
MIXER_LINKS = CondUnit.VECTOR_LINKS + 45


def stage_mixer(net):
    nc = net.nc
    N = XT_TILES
    STEPS = N + LAG_OUT
    net.next_stage()
    with ExitStack() as mem:
        def sb(name, shape, dt=F32):
            return mem.enter_context(nc.sbuf_tensor(name, shape, dt))

        def ps(name):
            return mem.enter_context(nc.psum_tensor(name, [P, 512], F32))

        def sem(name):
            return net.stage_sem(mem, name)

        w = net.weights
        sel = sb("sel", [3 * HEADS, HEADS * P], BF16)
        conv = sb("conv", [P, 2, TOK])
        tanh_x = sb("tanh_x", [P, 2, TOK])
        tanh_g = sb("tanh_g", [P, TOK])
        bc = sb("bc", [P, 2, TOK])
        xs = sb("xs", [P, 4, TOK])
        gate = sb("gate", [P, 4, TOK])
        x_tok = sb("x_tok", [P, 3, BB * ST, P])
        scores = sb("scores", [P, BB, TRI])
        decays = sb("decays", [P, 4, BB, TRI])
        y = sb("y", [P, TOK])
        g = sb("g", [P, 2, TOK])
        square = sb("square", [P, TOK])
        square_sum = sb("square_sum", [P, TOK])
        parts = sb("parts", [3 * HEADS, TOK], BF16)
        part = sb("part", [HEADS, TOK], BF16)
        neg_cum = sb("neg_cum", [P, BB * ST * HEADS])
        dt_tok = sb("dt_tok", [P, BB * ST * HEADS])
        z, soft, dt, cum = (gate[0:HEADS, n, :] for n in range(4))
        rest = y[0:HEADS, :]
        ones_row = net.ones[0:HEADS, 0:1].to_broadcast([HEADS, SEQ])
        root = y

        px, pg, py, pt = ps("px"), ps("pg"), ps("py"), ps("pt")
        pcum = [ps(f"pcum{n}") for n in range(ST)]
        pout = [ps(f"pout{n}") for n in range(KT)]

        sel_loaded = sem("sel_loaded")
        norm_folded, alog_exp, d_halved = sem("norm_folded"), sem("alog_exp"), sem("d_halved")
        px_ready, px_free = sem("px_ready"), sem("px_free")
        pg_ready, pg_free = sem("pg_ready"), sem("pg_free")
        conv_begun, tanh_x_ready, xs_ready = sem("conv_begun"), sem("tanh_x_ready"), sem("xs_ready")
        soft_in, soft_exp, soft_ready = sem("soft_in"), sem("soft_exp"), sem("soft_ready")
        cum_ready, parts_ready = sem("cum_ready"), sem("parts_ready")
        pt_ready, pt_free = sem("pt_ready"), sem("pt_free")
        pcum_ready = [sem(f"pcum_ready{n}") for n in range(ST)]
        pcum_free = [sem(f"pcum_free{n}") for n in range(ST)]
        row_cols_ready = sem("row_cols_ready")
        tanh_g_ready = sem("tanh_g_ready")
        decay_scaled = sem("decay_scaled")
        y_ready, y_free, g_ready = sem("y_ready"), sem("y_free"), sem("g_ready")
        square_ready, square_used = sem("square_ready"), sem("square_used")
        out_used, out_ready, out_free = sem("out_used"), sem("out_ready"), sem("out_free")
        root_ready = sem("root_ready")
        links = sem("mixer_links")
        unit = CondUnit(net, 1, net.cond_sems)
        tanh_h, make_h, h_ready = condition_input(net, "_mixer")

        def conv_w(n, k):
            return net.pp[:, PP_CONVW + n * TAPS + k:PP_CONVW + n * TAPS + k + 1]

        def chunk_of(col):
            return next(n for n, (a, b) in enumerate(net.win_chunks) if a <= col < b)

        block = mem.enter_context(nc.Block())

        @block.sync
        def _(sp):
            sp.dma_start(sel[:], net.dram["cb"][0:3 * HEADS, CB_SEL:CB_SEL + HEADS * P]) \
                .then_inc(sel_loaded, 16)
            sp.wait_ge(px_ready, PAIRS * (N + 2))
            sp.wait_ge(pg_ready, PAIRS * (N + 1))
            for dst, src, done in net.moe0_early:
                sp.dma_start(dst, src).then_inc(done, 16)

        @block.tensor
        def _(pe):
            def project(out, m, col, i, free, ready, count):
                pe.wait_ge(net.win_loaded[chunk_of(col)], 16)
                if count is not None:
                    pe.wait_ge(free, count)
                for k in range(KT):
                    op = nc.tensor.matmul(out[0:m, :], w[:, col + k * m:col + (k + 1) * m],
                                          net.h[:, ds(i * PAIR + k * TOK, TOK)],
                                          start=(k == 0), stop=(k == KT - 1))
                op.then_inc(ready, 1)

            def x_like(i, n):
                col = W_BCXG + (n if n < 2 else 2 + 2 * (n - 2)) * KT * P
                project(px, P, col, i, px_free, px_ready, i * (N + 2) + n)

            def gate_like(i, s):
                m, col = (HEADS, W_DT) if s < 0 else (P, W_BCXG + (3 + 2 * s) * KT * P)
                project(pg, m, col, i, pg_free, pg_ready, i * (N + 1) + s + 1)

            def turn_cum(i):
                for n, src in enumerate((cum, dt)):
                    for r in range(BB * ST):
                        at = (n * BB * ST + r) * HEADS
                        op = nc.tensor.transpose(pt[:, at:at + HEADS], src[:, r * P:(r + 1) * P],
                                                 net.ident[0:HEADS, 0:HEADS])
                op.then_inc(pt_ready, 1)

            def key_query(i):
                pe.wait_ge(cum_ready, i + 1)
                pe.wait_ge(pt_free, i * (N + 2))
                pe.wait_ge(xs_ready, i * (N + 2) + 2)
                for b in range(BB):
                    pe.wait_ge(pcum_free[b], i * (HEADS + 1))
                    at = b * SEQ
                    nc.tensor.matmul(pcum[b][:, 0:SEQ], bc[:, 0, at:at + P],
                                     bc[:, 1, at:at + SEQ], start=True, stop=True)
                    nc.tensor.matmul(pcum[b][:, SEQ:TRI], bc[:, 0, at + P:at + SEQ],
                                     bc[:, 1, at + P:at + SEQ], start=True, stop=True) \
                        .then_inc(pcum_ready[b], 1)

            def spread_cum(i, head):
                pe.wait_ge(parts_ready, i + 1)
                for r in range(ST):
                    pe.wait_ge(pcum_free[r], i * (HEADS + 1) + head + 1)
                    rows = parts[:].rearrange("p (b t) -> p b t", b=BB)[:, :, r * P:SEQ]
                    out = pcum[r][:, 0:BB * (SEQ - r * P)].rearrange("p (b t) -> p b t", b=BB)
                    nc.tensor.matmul(out, sel[:, head * P:(head + 1) * P], rows, start=True,
                                     stop=False)
                    nc.tensor.matmul(out[:, :, 0:P], net.cb[:, CB_IDENT:CB_IDENT + P],
                                     net.cb[:, CB_MASK_ST:CB_MASK_ST + P][:, None, :]
                                     .to_broadcast([P, BB, P]), start=False, stop=True) \
                        .then_inc(pcum_ready[r], 1)

            def turn_x(i, s):
                pe.wait_ge(xs_ready, i * (N + 2) + s + 3)
                pe.wait_ge(pt_free, i * (N + 2) + s + 1)
                for r in range(BB * ST):
                    op = nc.tensor.transpose(pt[:, r * P:(r + 1) * P],
                                             xs[:, s % 4, r * P:(r + 1) * P], net.ident[:])
                op.then_inc(pt_ready, 1)

            def mix(i, s):
                pe.wait_ge(pt_free, i * (N + 2) + s + 2)
                pe.wait_ge(y_free, i * N + s)
                for hh in range(TILE_HEADS):
                    head = s * TILE_HEADS + hh
                    pe.wait_ge(decay_scaled, i * HEADS + head + 1)
                    rows = slice(hh * HEAD, (hh + 1) * HEAD)
                    for b in range(BB):
                        for r in range(ST):
                            cols = slice(0, SEQ) if r == 0 else slice(SEQ, TRI)
                            op = nc.tensor.matmul(
                                py[rows, b * SEQ + r * P:(b + 1) * SEQ],
                                x_tok[:, s % 3, b * ST + r, rows],
                                decays[:, head % 4, b, cols], start=(r == 0), stop=(r == ST - 1))
                op.then_inc(y_ready, 1)

            def project_out(i, s):
                pe.wait_ge(g_ready, i * N + s + 1)
                if s == 0:
                    pe.wait_ge(norm_folded, N)
                    pe.wait_ge(out_free, i)
                for k in range(KT):
                    at = W_OUT0 + s * D + k * P
                    op = nc.tensor.matmul(pout[k][:], w[:, at:at + P], g[:, s % 2, :],
                                          start=(s == 0), stop=(s == N - 1))
                op.then_inc(out_used, 1)

            pe.wait_ge(h_ready, PAIRS)
            pe.wait_ge(sel_loaded, 16)
            with nc.tensor.Fori(0, PAIRS) as i:
                gate_like(i, -1)
                x_like(i, 0)
                x_like(i, 1)
                for s in range(STEPS):
                    if s < N:
                        x_like(i, s + 2)
                    if s == 1:
                        key_query(i)
                        turn_cum(i)
                    if 0 <= s - LAG_HEADS < N:
                        spread_cum(i, 2 * (s - LAG_HEADS))
                    if s < N:
                        gate_like(i, s)
                    if 0 <= s - LAG_HEADS < N:
                        spread_cum(i, 2 * (s - LAG_HEADS) + 1)
                    if 0 <= s - 1 < N:
                        turn_x(i, s - 1)
                    if 0 <= s - LAG_OUT < N:
                        project_out(i, s - LAG_OUT)
                    if 0 <= s - LAG_Y < N:
                        mix(i, s - LAG_Y)
                pe.wait_ge(square_used, (i + 1) * N)
                pe.wait_ge(pt_free, i * (N + 2) + N + 1)
                nc.tensor.matmul(pt[:], net.ones[:], square_sum[:], start=True, stop=True) \
                    .then_inc(pt_ready, 1)

        @block.scalar
        def _(act):
            col = net.pp[0:HEADS, PP_ALOG:PP_ALOG + 1]
            nc.scalar.activation(col, col, ACT.Exp).then_inc(alog_exp, 1)
            tanh_h()

            def begin_conv(i, n):
                act.wait_ge(px_ready, i * (N + 2) + n + 1)
                act.wait_ge(xs_ready, i * (N + 2) + max(n - 1, 0))
                nc.scalar.activation(conv[:, n % 2, :], px[:], ACT.Identity,
                                     bias=net.pp[:, PP_CONVB + n:PP_CONVB + n + 1],
                                     scale=conv_w(n, TAPS - 1)).then_inc(conv_begun, 1)

            def tanh_conv(i, n):
                act.wait_ge(px_free, i * (N + 2) + n + 1)
                nc.scalar.activation(tanh_x[:, n % 2, :], conv[:, n % 2, :], ACT.Tanh, scale=0.5) \
                    .then_inc(tanh_x_ready, 1)

            def tanh_gate(i, s):
                act.wait_ge(pg_ready, i * (N + 1) + s + 2)
                act.wait_ge(pg_free, i * (N + 1) + s + 1)
                nc.scalar.activation(tanh_g[:], pg[:], ACT.Tanh, scale=0.5) \
                    .then_inc(tanh_g_ready, 1)

            def exp_decay(i, head):
                if head >= 4:
                    act.wait_ge(y_ready, i * N + (head - 4) // 2 + 1)
                for r in range(ST):
                    act.wait_ge(pcum_ready[r], i * (HEADS + 1) + head + 2)
                    for b in range(BB):
                        n = SEQ - r * P
                        at = (b * ST + r) * HEADS + head
                        op = nc.scalar.activation(
                            decays[:, head % 4, b, r * SEQ:r * SEQ + n],
                            pcum[r][:, b * n:(b + 1) * n], ACT.Exp, bias=neg_cum[:, at:at + 1])
                    op.then_inc(pcum_free[r], 1)

            def square_g(i, s):
                act.wait_ge(g_ready, i * N + s + 1)
                act.wait_ge(square_used, i * N + s)
                nc.scalar.activation(square[:], g[:, s % 2, :], ACT.Square) \
                    .then_inc(square_ready, 1)

            with nc.scalar.Fori(0, PAIRS) as i:
                act.wait_ge(soft_in, i + 1)
                nc.scalar.activation(soft, soft, ACT.Exp, scale=-1.0).then_inc(soft_exp, 1)
                act.wait_ge(soft_exp, i + 1)
                nc.scalar.activation(soft, soft, ACT.Ln, bias=1.0).then_inc(soft_ready, 1)
                for n in range(2):
                    begin_conv(i, n)
                    tanh_conv(i, n)
                for s in range(STEPS):
                    if s < N:
                        begin_conv(i, s + 2)
                    if s == LAG_HEADS:
                        act.wait_ge(row_cols_ready, i + 1)
                    if 0 <= s - LAG_HEADS < N:
                        exp_decay(i, 2 * (s - LAG_HEADS))
                    if s < N:
                        tanh_conv(i, s + 2)
                        tanh_gate(i, s)
                    if 0 <= s - LAG_HEADS < N:
                        exp_decay(i, 2 * (s - LAG_HEADS) + 1)
                    if 0 <= s - LAG_OUT < N:
                        square_g(i, s - LAG_OUT)
                    if s == 3:
                        unit.scalar(i + PAIRS)
                act.wait_ge(pt_ready, (i + 1) * (N + 2))
                nc.scalar.activation(root[:], pt[:], ACT.Ln, scale=0.25 / INNER,
                                     bias=net.pp[:, PP_EPS_MIXER:PP_EPS_MIXER + 1]) \
                    .then_inc(pt_free, 1)
                act.wait_ge(pt_free, (i + 1) * (N + 2))
                nc.scalar.activation(root[:], root[:], ACT.Exp, scale=-0.5,
                                     bias=net.pp[:, PP_LN_HALF:PP_LN_HALF + 1]) \
                    .then_inc(root_ready, 1)

        @block.gpsimd
        def _(pool):
            net.clear_last_stage(pool)
            pool.wait_ge(net.win_loaded[chunk_of(W_OUT0)], 16)
            for s in range(N):
                rows = w[:, W_OUT0 + s * D:W_OUT0 + (s + 1) * D]
                nc.gpsimd.tensor_scalar(rows, rows, net.pp[:, PP_NORM + s:PP_NORM + s + 1], None,
                                        ALU.mult).then_inc(norm_folded, 1)

            def scale_decay(i, head):
                pool.wait_ge(pcum_free[ST - 1], i * (HEADS + 1) + head + 2)
                nc.gpsimd.tensor_tensor(decays[:, head % 4], decays[:, head % 4], scores[:],
                                        ALU.mult).then_inc(decay_scaled, 1)

            def add_square(i, s):
                pool.wait_ge(square_ready, i * N + s + 1)
                if s == 0:
                    pool.wait_ge(pt_ready, i * (N + 2))
                    op = nc.gpsimd.tensor_tensor(square_sum[:], square[:],
                                                 net.ones[:, 0:1].to_broadcast([P, TOK]), ALU.mult)
                else:
                    pool.wait_ge(square_used, i * N + s)
                    op = nc.gpsimd.tensor_tensor(square_sum[:], square_sum[:], square[:], ALU.add)
                op.then_inc(square_used, 1)

            with nc.gpsimd.Fori(0, PAIRS) as i:
                unit.pool(i, i + PAIRS)
                for b in range(BB):
                    pool.wait_ge(pcum_free[b], i * (HEADS + 1) + 1)
                for s in range(LAG_HEADS, STEPS):
                    for hh in range(TILE_HEADS):
                        if s - LAG_HEADS < N:
                            scale_decay(i, TILE_HEADS * (s - LAG_HEADS) + hh)
                    if s >= LAG_OUT:
                        add_square(i, s - LAG_OUT)

        @block.vector
        def _(dve):
            v = nc.vector
            make_h()
            half_d = net.pp[:, PP_D:PP_D + N]
            v.tensor_scalar(half_d, half_d, 0.5, None, ALU.mult).then_inc(d_halved, 1)
            dve.wait_ge(d_halved, 1)
            dve.wait_ge(alog_exp, 1)

            def softplus_cum(i, link):
                dve.wait_ge(pg_ready, i * (N + 1) + 1)
                dve.wait_ge(y_ready, i * N)
                v.tensor_scalar(z, pg[0:HEADS, :], net.pp[0:HEADS, PP_DTB:PP_DTB + 1], None,
                                ALU.add).then_inc(pg_free, 1)
                dve.wait_ge(pg_free, i * (N + 1) + 1)
                v.scalar_tensor_tensor(soft, z, -1.0, z, ALU.mult, ALU.max).then_inc(soft_in, 1)

            def cum_parts(i, link):
                dve.wait_ge(soft_ready, i + 1)
                link(v.scalar_tensor_tensor(dt, z, 0.0, soft, ALU.max, ALU.add))
                link(v.tensor_scalar(z, dt, net.pp[0:HEADS, PP_ALOG:PP_ALOG + 1], -1.0, ALU.mult,
                                     ALU.mult))
                for b in range(BB):
                    s = slice(b * SEQ, (b + 1) * SEQ)
                    link(v.tensor_tensor_scan(cum[:, s], ones_row, z[:, s], 0.0, ALU.mult,
                                              ALU.add))
                v.tensor_copy(parts[0:HEADS, :], cum).then_inc(cum_ready, 1)
                dve.wait_ge(cum_ready, i + 1)
                link(v.tensor_tensor(rest, cum, parts[0:HEADS, :], ALU.subtract))
                link(v.tensor_copy(part[:], rest))
                v.tensor_copy(parts[HEADS:2 * HEADS, :], part[:])
                link(v.tensor_tensor(rest, rest, part[:], ALU.subtract))
                v.tensor_copy(parts[2 * HEADS:3 * HEADS, :], rest).then_inc(parts_ready, 1)

            def taps(i, n, link):
                dve.wait_ge(conv_begun, i * (N + 2) + n + 1)
                for k in range(1, TAPS):
                    out = conv[:, n % 2, :].rearrange("p (b t) -> p b t", b=BB)[:, :, k:SEQ]
                    src = px[:].rearrange("p (b t) -> p b t", b=BB)[:, :, 0:SEQ - k]
                    op = v.scalar_tensor_tensor(out, src, conv_w(n, TAPS - 1 - k), out, ALU.mult,
                                                ALU.add)
                    if k < TAPS - 1:
                        link(op)
                op.then_inc(px_free, 1)

            def silu_x(i, n):
                dve.wait_ge(tanh_x_ready, i * (N + 2) + n + 1)
                out = bc[:, n, :] if n < 2 else xs[:, (n - 2) % 4, :]
                v.scalar_tensor_tensor(out, tanh_x[:, n % 2, :], 1.0, conv[:, n % 2, :], ALU.add,
                                       ALU.mult).then_inc(xs_ready, 1)

            def silu_gate(i, s):
                dve.wait_ge(tanh_g_ready, i * N + s + 1)
                v.scalar_tensor_tensor(gate[:, s % 4, :], tanh_g[:], 1.0, pg[:], ALU.add,
                                       ALU.mult).then_inc(pg_free, 1)

            def row_cols(i):
                dve.wait_ge(pt_ready, i * (N + 2) + 1)
                n = BB * ST * HEADS
                v.tensor_scalar(neg_cum[:], pt[:, 0:n], -1.0, None, ALU.mult) \
                    .then_inc(row_cols_ready, 1)
                v.tensor_scalar(dt_tok[:], pt[:, n:2 * n], 0.5, None, ALU.mult) \
                    .then_inc(pt_free, 1)
                for b in range(BB):
                    dve.wait_ge(pcum_ready[b], i * (HEADS + 1) + 1)
                    v.tensor_scalar(scores[:, b, :], pcum[b][:, 0:TRI], 0.25, None, ALU.mult) \
                        .then_inc(pcum_free[b], 1)

            def take_x(i, s):
                dve.wait_ge(pt_ready, i * (N + 2) + s + 2)
                if s == 0:
                    dve.wait_ge(pt_free, i * (N + 2) + 1)
                if s >= 3:
                    dve.wait_ge(y_ready, i * N + s - 2)
                heads = dt_tok[:].rearrange("p (r h) -> p r h", h=HEADS)[
                    :, :, s * TILE_HEADS:(s + 1) * TILE_HEADS]
                v.tensor_tensor(
                    x_tok[:, s % 3].rearrange("p r (h d) -> p r h d", h=TILE_HEADS),
                    pt[:].rearrange("p (r h d) -> p r h d", r=BB * ST, h=TILE_HEADS),
                    heads[:, :, :, None].to_broadcast([P, BB * ST, TILE_HEADS, HEAD]),
                    ALU.mult).then_inc(pt_free, 1)

            def gated(i, s, link):
                dve.wait_ge(y_ready, i * N + s + 1)
                v.scalar_tensor_tensor(y[:], xs[:, s % 4, :], net.pp[:, PP_D + s:PP_D + s + 1],
                                       py[:], ALU.mult, ALU.add).then_inc(y_free, 1)
                dve.wait_ge(y_free, i * N + s + 1)
                dve.wait_ge(out_used, i * N + max(s - 1, 0))
                dve.wait_ge(square_ready, i * N + max(s - 1, 0))
                dve.wait_ge(pg_free, i * (N + 1) + s + 2)
                v.tensor_tensor(g[:, s % 2, :], y[:], gate[:, s % 4, :], ALU.mult) \
                    .then_inc(g_ready, 1)

            def add_to_x(i, link):
                dve.wait_ge(root_ready, i + 1)
                dve.wait_ge(out_used, (i + 1) * N)
                for k in range(KT):
                    out = net.x[:, ds(i * PAIR + k * TOK, TOK)]
                    link(v.tensor_tensor(g[:, k, :], pout[k][:], root[:], ALU.mult))
                    op = v.tensor_tensor(out, out, g[:, k, :], ALU.add)
                op.then_inc(out_free, 1)

            with nc.vector.Fori(0, PAIRS) as i:
                link = Links(dve, links, i, MIXER_LINKS)
                cond = unit.vector(link, i, i + PAIRS)
                softplus_cum(i, link)
                taps(i, 0, link)
                cum_parts(i, link)
                silu_x(i, 0)
                taps(i, 1, link)
                silu_x(i, 1)
                for s in range(STEPS):
                    if s < N:
                        taps(i, s + 2, link)
                    if s == 1:
                        row_cols(i)
                    if 0 <= s - LAG_Y < N:
                        gated(i, s - LAG_Y, link)
                    if s < N:
                        silu_x(i, s + 2)
                    if 0 <= s - 1 < N:
                        take_x(i, s - 1)
                    if s < N:
                        silu_gate(i, s)
                    if s >= 2 and cond:
                        cond.pop(0)()
                assert not cond
                add_to_x(i, link)
                link.check()



class Experts:

    def __init__(self, tag, experts, top, shared, tiles, gate_product):
        self.tag, self.experts, self.top = tag, experts, top
        self.shared, self.tiles, self.gate_product = shared, tiles, gate_product
        self.part_rows = 32


MOE0 = Experts("0", E0, K0, SHARED_TILES, MOE0_TILES, True)
MOE1 = Experts("1", E1, K1, 0, MOE1_TILES, False)
TOK_TILES = BATCH * SEQ // P


def stage_moe(net, cfg, weights, prepare, cond):
    nc = net.nc
    E, N, S = cfg.experts, cfg.tiles, cfg.shared
    PR = cfg.part_rows
    R = 3 * PR
    per = (0 if cfg.gate_product else N) + (CondUnit.VECTOR_LINKS if cond is not None else 0)
    net.next_stage()
    with ExitStack() as mem:
        def sb(name, shape, dt=F32):
            return mem.enter_context(nc.sbuf_tensor(name + cfg.tag, shape, dt))

        def sem(name):
            return net.stage_sem(mem, name + cfg.tag)

        def ps(name):
            return mem.enter_context(nc.psum_tensor(name + cfg.tag, [P, 512], F32))

        weight_tile, w_loaded, loads = weights(sb)
        sel = sb("expert_sel", [R, (N - S) * P], BF16)
        gate_wt = sb("gate_wt", [P, KT * E])
        score = sb("score", [P, TOK_TILES, E])
        pick = sb("pick", [P, 3, TOK_TILES, E])
        seg = sb("seg", [P, TOK_TILES, E])
        top8 = sb("top8", [P, TOK_TILES, 8])
        col = sb("col", [P, 2, TOK_TILES])
        route = sb("route", [E, PAIRS * TOK])
        part = sb("route_part", [E, PAIRS * TOK], BF16)
        parts = sb("route_parts", [R, PAIRS * TOK], BF16)
        up = sb("up", [P, 2, TOK])
        mid = sb("mid", [P, 2, TOK])
        act_out = sb("act_out", [P, 2, TOK])
        hidden = sb("hidden", [P, 2, TOK])

        ph1 = [ps(f"ph1_{n}_") for n in range(2)]
        ph3 = [ps(f"ph3_{n}_") for n in range(2)]
        pw = [ps(f"pw_{n}_") for n in range(2)]
        pout = [ps(f"pmoe_{n}_") for n in range(KT)]
        plogit, proute = pout[0], pw

        small_loaded = sem("small_loaded")
        logit_ready, score_ready = sem("logit_ready"), sem("score_ready")
        exp_ready, exp_in = sem("exp_ready"), sem("exp_in")
        route_cols_ready, route_turned = sem("route_cols_ready"), sem("route_turned")
        parts_ready = sem("route_parts_ready")
        h_up_ready, w_ready = sem("h_up_ready"), sem("w_ready")
        up_copied, mid_ready = sem("up_copied"), sem("mid_ready")
        act_ready, hidden_ready = sem("act_ready"), sem("hidden_ready")
        down_done, x_added = sem("down_done"), sem("x_added")
        zeroed, links, route_links = sem("zeroed"), sem("moe_links"), sem("route_links")
        unit = CondUnit(net, cond, net.cond_sems) if cond is not None else None
        turn0 = PAIRS * cond if cond is not None else 0
        tanh_h, make_h, h_ready = prepare or (lambda: None, lambda: None, None)
        routed = N - S

        block = mem.enter_context(nc.Block())

        @block.sync
        def _(sp):
            tag = cfg.tag
            sp.dma_start(gate_wt[:], net.dram[f"gate{tag}"]).then_inc(small_loaded, 16)
            sp.dma_start(sel[:], net.dram[f"sel{tag}"]).then_inc(small_loaded, 16)
            for dst, src, done in loads:
                sp.dma_start(dst, src).then_inc(done, 16)

        @block.tensor
        def _(pe):
            pe.wait_ge(small_loaded, 32)
            if h_ready:
                pe.wait_ge(h_ready, PAIRS)
            for n in range(TOK_TILES):
                pair, at = n // (BB * ST), n % (BB * ST) * P
                for k in range(KT):
                    op = nc.tensor.matmul(plogit[:, n * E:(n + 1) * E],
                                          net.h[:, pair * PAIR + k * TOK + at:][:, 0:P],
                                          gate_wt[:, k * E:(k + 1) * E], start=(k == 0),
                                          stop=(k == KT - 1))
            op.then_inc(logit_ready, 1)
            pe.wait_ge(route_cols_ready, 1)
            for n in range(TOK_TILES):
                op = nc.tensor.transpose(proute[n // 4][0:E, n % 4 * P:(n % 4 + 1) * P],
                                         pick[:, 0, n, :], net.ident[:])
            op.then_inc(route_turned, 1)

            def up_project(i, m):
                pe.wait_ge(w_loaded(m), 16)
                pe.wait_ge(hidden_ready, i * N + max(m - 1, 0))
                wt = weight_tile(m)
                for n, out in enumerate((ph1[m % 2], ph3[m % 2])):
                    for k in range(KT):
                        op = nc.tensor.matmul(out[:], wt[:, n * D + k * P:n * D + (k + 1) * P],
                                              net.h[:, ds(i * PAIR + k * TOK, TOK)],
                                              start=(k == 0), stop=(k == KT - 1))
                op.then_inc(h_up_ready, 1)
                if m >= S:
                    r = m - S
                    pe.wait_ge(parts_ready, 1)
                    nc.tensor.matmul(pw[r % 2][:], sel[:, r * P:(r + 1) * P],
                                     parts[:, ds(i * TOK, TOK)], start=True, stop=True) \
                        .then_inc(w_ready, 1)

            def down_project(i, m):
                pe.wait_ge(hidden_ready, i * N + m + 1)
                if m == 0:
                    pe.wait_ge(x_added, i)
                wt = weight_tile(m)
                for k in range(KT):
                    op = nc.tensor.matmul(pout[k][:], wt[:, 2 * D + k * P:2 * D + (k + 1) * P],
                                          hidden[:, m % 2, :], start=(m == 0), stop=(m == N - 1))
                op.then_inc(down_done, 1)

            with nc.tensor.Fori(0, PAIRS) as i:
                for m in range(N + 1):
                    if m < N:
                        up_project(i, m)
                    if m >= 1:
                        down_project(i, m - 1)

        @block.scalar
        def _(act):
            tanh_h()
            if cfg.gate_product:
                act.wait_ge(logit_ready, 1)
                nc.scalar.activation(score[:].rearrange("p n e -> p (n e)"),
                                     plogit[:, 0:TOK_TILES * E], ACT.Tanh, scale=0.5) \
                    .then_inc(score_ready, 1)
            else:
                act.wait_ge(exp_in, 1)
                nc.scalar.activation(score[:], score[:], ACT.Exp).then_inc(exp_ready, 1)

            def silu(i, m):
                act.wait_ge(hidden_ready, i * N + max(m - 1, 0))
                if m >= S and cfg.gate_product:
                    src = mid[:, m % 2, :]
                    act.wait_ge(mid_ready, i * routed + m - S + 1)
                else:
                    src = ph1[m % 2][:]
                    act.wait_ge(h_up_ready, i * N + m + 1)
                nc.scalar.activation(act_out[:, m % 2, :], src, ACT.Silu).then_inc(act_ready, 1)

            def copy_up(i, m):
                act.wait_ge(h_up_ready, i * N + m + 1)
                act.wait_ge(mid_ready, i * routed + max(m - S - 1, 0))
                nc.scalar.activation(up[:, m % 2, :], ph1[m % 2][:], ACT.Copy) \
                    .then_inc(up_copied, 1)

            with nc.scalar.Fori(0, PAIRS) as i:
                for m in range(N):
                    if m >= S and cfg.gate_product:
                        copy_up(i, m)
                    silu(i, m)
                    if m == 2 and unit:
                        unit.scalar(i + turn0)

        @block.gpsimd
        def _(pool):
            net.clear_last_stage(pool)
            nc.gpsimd.memset(seg[:], 1.0).then_inc(zeroed, 1)
            nc.gpsimd.memset(parts[:], 0.0).then_inc(zeroed, 1)
            pool.wait_ge(zeroed, 2)
            nc.gpsimd.memset(seg[:, :, 0:1], 0.0).then_inc(zeroed, 1)
            if unit:
                with nc.gpsimd.Fori(0, PAIRS) as i:
                    unit.pool(i, i + turn0)

        @block.vector
        def _(dve):
            v = nc.vector
            make_h()
            link = Links(dve, route_links)
            wide = [P, TOK_TILES, E]
            one, two, three = (pick[:, n] for n in range(3))

            def per_token(x):
                return x[:, :, None].to_broadcast(wide)

            if cfg.gate_product:
                dve.wait_ge(score_ready, 1)
                link(v.tensor_scalar(score[:], score[:], 0.5, 0.5, ALU.mult, ALU.add))
                bias = net.pp[:, PP_GATEB:PP_GATEB + E][:, None, :].to_broadcast(wide)
                link(v.tensor_tensor(score[:], score[:], bias, ALU.add))
            else:
                dve.wait_ge(logit_ready, 1)
                logits = plogit[:, 0:TOK_TILES * E].rearrange("p (n e) -> p n e", e=E)
                link(v.tensor_reduce(col[:, 0], logits, AX_X, ALU.max))
                v.tensor_tensor(score[:], logits, per_token(col[:, 0]), ALU.subtract) \
                    .then_inc(exp_in, 1)
                dve.wait_ge(exp_ready, 1)
                link(v.tensor_reduce(col[:, 0], score[:], AX_X, ALU.add))
                link(v.reciprocal(col[:, 1], col[:, 0]))
                link(v.tensor_tensor(score[:], score[:], per_token(col[:, 1]), ALU.mult))
            for n in range(TOK_TILES):
                op = v.max(top8[:, n, :], score[:, n, :])
            link(op)
            last = per_token(top8[:, :, cfg.top - 1])
            link(v.tensor_tensor(one, score[:], last, ALU.is_gt))
            link(v.tensor_tensor(two, score[:], last, ALU.is_equal))
            link(v.tensor_reduce(col[:, 0], one, AX_X, ALU.add))
            link(v.tensor_scalar(col[:, 0], col[:, 0], -1.0, float(cfg.top), ALU.mult, ALU.add))
            dve.wait_ge(zeroed, 3)
            flat = lambda x: x.rearrange("p n e -> p (n e)")
            link(v.tensor_tensor_scan(flat(three), flat(seg[:]), flat(two), 0.0, ALU.mult,
                                      ALU.add))
            link(v.tensor_tensor(three, three, per_token(col[:, 0]), ALU.is_le))
            link(v.tensor_tensor(two, two, three, ALU.mult))
            link(v.tensor_tensor(one, one, two, ALU.add))
            link(v.tensor_tensor(one, one, score[:], ALU.mult))
            link(v.tensor_reduce(col[:, 0], one, AX_X, ALU.add))
            if not cfg.gate_product:
                link(v.tensor_scalar(col[:, 0], col[:, 0], 1e-9, None, ALU.add))
            link(v.reciprocal(col[:, 1], col[:, 0]))
            v.tensor_tensor(one, one, per_token(col[:, 1]), ALU.mult) \
                .then_inc(route_cols_ready, 1)
            dve.wait_ge(route_turned, 1)
            for p in range(PAIRS):
                op = v.tensor_copy(route[:, p * TOK:(p + 1) * TOK], proute[p][0:E, :])
            link(op)
            link(v.tensor_copy(parts[0:E, :], route[:]))
            link(v.tensor_tensor(route[:], route[:], parts[0:E, :], ALU.subtract))
            link(v.tensor_copy(part[:], route[:]))
            v.tensor_copy(parts[PR:PR + E, :], part[:])
            link(v.tensor_tensor(route[:], route[:], part[:], ALU.subtract))
            v.tensor_copy(parts[2 * PR:2 * PR + E, :], route[:]).then_inc(parts_ready, 1)

            def times_up(i, m):
                dve.wait_ge(up_copied, i * routed + m - S + 1)
                v.tensor_tensor(mid[:, m % 2, :], up[:, m % 2, :], ph3[m % 2][:], ALU.mult) \
                    .then_inc(mid_ready, 1)

            def weigh(i, m, src):
                r = m - S
                dve.wait_ge(w_ready, i * routed + r + 1)
                dve.wait_ge(down_done, i * N + max(m - 1, 0))
                v.tensor_tensor(hidden[:, m % 2, :], src, pw[r % 2][:], ALU.mult) \
                    .then_inc(hidden_ready, 1)

            with nc.vector.Fori(0, PAIRS) as i:
                link = Links(dve, links, i, per)
                steps = unit.vector(link, i, i + turn0) if unit else []
                for m in range(N):
                    if m >= S and cfg.gate_product:
                        times_up(i, m)
                        dve.wait_ge(act_ready, i * N + m + 1)
                        weigh(i, m, act_out[:, m % 2, :])
                    elif m < S:
                        dve.wait_ge(act_ready, i * N + m + 1)
                        dve.wait_ge(down_done, i * N + max(m - 1, 0))
                        v.tensor_tensor(hidden[:, m % 2, :], act_out[:, m % 2, :], ph3[m % 2][:],
                                        ALU.mult).then_inc(hidden_ready, 1)
                    else:
                        dve.wait_ge(act_ready, i * N + m + 1)
                        link(v.tensor_tensor(mid[:, m % 2, :], act_out[:, m % 2, :],
                                             ph3[m % 2][:], ALU.mult))
                        weigh(i, m, mid[:, m % 2, :])
                    if steps:
                        steps.pop(0)()
                assert not steps
                dve.wait_ge(down_done, (i + 1) * N)
                for k in range(KT):
                    out = net.x[:, ds(i * PAIR + k * TOK, TOK)]
                    op = v.tensor_tensor(out, out, pout[k][:], ALU.add)
                op.then_inc(x_added, 1)
                link.check()



DEPTH = 4


class Attend:

    LINKS = 1

    def __init__(self, net, mem, tag, heads, per_bank, rows_of):
        nc = net.nc
        self.net, self.heads, self.per_bank, self.rows_of = net, heads, per_bank, rows_of
        self.units = BB * heads
        self.banks = self.units // per_bank

        def sb(name, shape, dt=F32):
            return mem.enter_context(nc.sbuf_tensor(name + tag, shape, dt))

        def ps(name):
            return mem.enter_context(nc.psum_tensor(name + tag, [P, 512], F32))

        def sem(name):
            return net.stage_sem(mem, name + tag)

        self.prob = sb("prob", [P, DEPTH, TRI])
        self.turned = sb("turned", [P, 2, TRI])
        self.neg_max = sb("neg_max", [P, DEPTH, ST])
        self.total = sb("total", [P, DEPTH, ST])
        self.inverse = sb("inverse", [P, DEPTH, ST])
        self.ps = [ps(f"ps{n}_") for n in range(2)]
        self.pt = [ps(f"pturn{n}_") for n in range(2)]
        self.po = [ps(f"po{n}_") for n in range(2)]
        self.s_ready, self.max_ready = sem("s_ready"), sem("max_ready")
        self.exp_ready, self.prob_ready = sem("exp_ready"), sem("prob_ready")
        self.pt_ready = sem("probs_turned")
        self.pt_taken = [sem(f"pt_taken{n}") for n in range(2)]
        self.mixed, self.o_ready, self.o_taken = sem("mixed"), sem("o_ready"), sem("o_taken")


    def scores(self, i, u, query, keys):
        nc, cb, out = self.net.nc, self.net.cb, self.ps[u % 2]
        ident = cb[:, CB_IDENT:CB_IDENT + P]
        nc.tensor.wait_ge(self.exp_ready, i * self.units + max(u - 1, 0))
        nc.tensor.matmul(out[:, 0:SEQ], ident, cb[:, CB_MASK_QK:CB_MASK_QK + SEQ], start=True,
                         stop=False)
        nc.tensor.matmul(out[:, 0:P], query(0), keys(P), start=False, stop=True)
        nc.tensor.matmul(out[:, SEQ:2 * SEQ], query(1), keys(SEQ), start=True, stop=False)
        nc.tensor.matmul(out[:, SEQ + P:2 * SEQ], ident, cb[:, CB_MASK_QK:CB_MASK_QK + P],
                         start=False, stop=True).then_inc(self.s_ready, 1)

    def turn(self, i, u):
        nc = self.net.nc
        nc.tensor.wait_ge(self.prob_ready, i * self.units + u + 1)
        nc.tensor.wait_ge(self.pt_taken[u % 2], i * (self.units // 2) + u // 2)
        for n in range(3):
            op = nc.tensor.transpose(self.pt[u % 2][:, n * P:(n + 1) * P],
                                     self.prob[:, u % DEPTH, n * P:(n + 1) * P],
                                     self.net.ident[:])
        op.then_inc(self.pt_ready, 1)

    def mix(self, i, u, values):
        nc = self.net.nc
        bank, place = u // self.per_bank, u % self.per_bank
        if place == 0:
            nc.tensor.wait_ge(self.o_taken, i * self.banks + max(bank - 1, 0))
        nc.tensor.wait_ge(self.pt_taken[u % 2], i * (self.units // 2) + u // 2 + 1)
        rows, at = self.rows_of(place)
        out = self.po[bank % 2]
        nc.tensor.matmul(out[rows, at:at + SEQ], values(0), self.turned[:, u % 2, 0:SEQ],
                         start=True, stop=False)
        op = nc.tensor.matmul(out[rows, at + P:at + SEQ], values(1),
                              self.turned[:, u % 2, SEQ:TRI], start=False, stop=True)
        if place == self.per_bank - 1:
            op.then_inc(self.o_ready, 1)
        else:
            op.then_inc(self.mixed, 1)

    def mixed_up_to(self, i, u):
        bank, place = u // self.per_bank, u % self.per_bank
        if place == self.per_bank - 1:
            return self.o_ready, i * self.banks + bank + 1
        return self.mixed, (i * self.banks + bank) * (self.per_bank - 1) + place + 1


    def maximum(self, i, u):
        nc = self.net.nc
        nc.vector.wait_ge(self.s_ready, i * self.units + u + 1)
        nc.vector.tensor_reduce(self.neg_max[:, u % DEPTH, :],
                                self.ps[u % 2][:].rearrange("p (t k) -> p t k", t=ST), AX_X,
                                ALU.max, negate=True).then_inc(self.max_ready, 1)

    def normalise(self, i, u, link):
        nc, slot = self.net.nc, u % DEPTH
        nc.vector.wait_ge(self.exp_ready, i * self.units + u + 1)
        link(nc.vector.reciprocal(self.inverse[:, slot, :], self.total[:, slot, :]))
        for t in range(ST):
            cols = slice(0, P) if t == 0 else slice(P, TRI)
            op = nc.vector.tensor_scalar(self.prob[:, slot, cols], self.prob[:, slot, cols],
                                         self.inverse[:, slot, t:t + 1], None, ALU.mult)
        op.then_inc(self.prob_ready, 1)


    def exponential(self, i, u):
        nc, slot = self.net.nc, u % DEPTH
        nc.scalar.wait_ge(self.max_ready, i * self.units + u + 1)
        nc.scalar.wait_ge(self.pt_ready, i * self.units + max(u - DEPTH + 1, 0))
        for t in range(ST):
            cols = slice(0, P) if t == 0 else slice(P, TRI)
            n = P * (t + 1)
            op = nc.scalar.activation(self.prob[:, slot, cols],
                                      self.ps[u % 2][:, t * SEQ:t * SEQ + n], ACT.Exp,
                                      bias=self.neg_max[:, slot, t:t + 1],
                                      accum_out=self.total[:, slot, t:t + 1])
        op.then_inc(self.exp_ready, 1)


    def take_turned(self, i, u):
        nc = self.net.nc
        engine = nc.scalar if u % 2 else nc.vector
        engine.wait_ge(self.pt_ready, i * self.units + u + 1)
        if u >= 2:
            engine.wait_ge(*self.mixed_up_to(i, u - 2))
        else:
            engine.wait_ge(self.o_ready, i * self.banks)
        out, src = self.turned[:, u % 2, :], self.pt[u % 2][:, 0:TRI]
        op = nc.scalar.copy(out, src) if u % 2 else nc.vector.tensor_copy(out, src)
        op.then_inc(self.pt_taken[u % 2], 1)



A_HEADS, A_HEAD, LATENT = 16, 16, 64
SLOT = 32
A_GROUPS = A_HEADS * SLOT // P
(WA_DOWN, WA_Q, WA_K, WA_V, WA_O, WA_END) = np.cumsum(
    [0, KT * P, D, D, A_HEADS * SLOT, A_GROUPS * D]).tolist()


def stage_latent_attention(net):
    nc = net.nc
    U = BB * A_HEADS
    LINKS = CondUnit.VECTOR_LINKS + U * Attend.LINKS
    net.next_stage()
    with ExitStack() as mem:
        def sb(name, shape, dt=F32):
            return mem.enter_context(nc.sbuf_tensor(name, shape, dt))

        def sem(name):
            return net.stage_sem(mem, name)

        w = net.weights[:, W_MIXER - WA_END:W_MIXER]
        latent = sb("latent", [P, TOK_TILES, 2, LATENT])
        latent_sq = sb("latent_sq", [P, TOK_TILES, 2, LATENT])
        stat = sb("stat", [P, 2, TOK_TILES, 2])
        c_t = latent_sq[:].rearrange("p n h c -> p (n h c)")
        keys = sb("keys", [P, KT, PAIRS * TOK])
        values = sb("values", [P, BB * ST, A_HEADS * SLOT])
        query = sb("query", [P, A_HEADS, TOK])
        o = sb("o", [P, A_GROUPS, TOK])

        def rows_of(place):
            return slice(place * SLOT, (place + 1) * SLOT), 0

        att = Attend(net, mem, "_latent", A_HEADS, P // SLOT, rows_of)
        pp = [mem.enter_context(nc.psum_tensor(f"latent_out{n}", [P, 512], F32))
              for n in range(2)]

        w_loaded = sem("w_latent_loaded")
        down_ready, centred, logs = sem("down_ready"), sem("centred"), sem("latent_logs")
        rstd_ready, normed = sem("rstd_ready"), sem("latent_normed")
        c_turned, c_ready = sem("c_turned"), sem("c_ready")
        k_projected, k_ready = sem("k_projected"), sem("k_ready")
        q_projected, q_taken = sem("q_projected"), sem("q_taken")
        v_projected, v_taken = sem("v_projected"), sem("v_taken")
        c_pair_ready = sem("c_pair_ready")
        o_projected, x_added = sem("o_projected"), sem("x_added_latent")
        links, once = sem("latent_links"), sem("latent_once")
        unit = CondUnit(net, 3, net.cond_sems)
        tanh_h, make_h, h_ready = condition_input(net, "_latent")
        c_pair = sb("c_pair", [P, TOK])

        block = mem.enter_context(nc.Block())

        @block.sync
        def _(sp):
            sp.dma_start(w, net.dram["w_latent"]).then_inc(w_loaded, 16)
            for dst, src, done in net.gqa_early:
                sp.dma_start(dst, src).then_inc(done, 16)

        @block.tensor
        def _(pe):
            pe.wait_ge(w_loaded, 16)
            pe.wait_ge(h_ready, PAIRS)
            for n in range(TOK_TILES):
                pair, at = n // (BB * ST), n % (BB * ST) * P
                for k in range(KT):
                    op = nc.tensor.matmul(pp[pair][:, at:at + P],
                                          net.h[:, pair * PAIR + k * TOK + at:][:, 0:P],
                                          w[:, WA_DOWN + k * P:WA_DOWN + (k + 1) * P],
                                          start=(k == 0), stop=(k == KT - 1))
            op.then_inc(down_ready, 1)
            pe.wait_ge(normed, 1)
            for n in range(TOK_TILES):
                pair, at = n // (BB * ST), n % (BB * ST) * P
                op = nc.tensor.transpose(pp[pair][:, at:at + P],
                                         latent[:, n].rearrange("p h c -> p (h c)"),
                                         net.ident[:])
            op.then_inc(c_turned, 1)
            for pair in range(PAIRS):
                pe.wait_ge(c_ready, pair + 1)
                for g in range(KT):
                    out = (att.ps + att.pt)[pair * KT + g]
                    at = WA_K + g * P
                    nc.tensor.matmul(out[:], w[:, at:at + P], c_t[:, pair * TOK:(pair + 1) * TOK],
                                     start=True, stop=True).then_inc(k_projected, 1)

            def project_qv(i):
                pe.wait_ge(c_pair_ready, i + 1)
                pe.wait_ge(x_added, i)
                for n in range(BB * ST):
                    if n >= 2:
                        pe.wait_ge(v_taken, i * BB * ST + n - 1)
                    nc.tensor.matmul(pp[n % 2][:], c_pair[:, n * P:(n + 1) * P],
                                     w[:, WA_V:WA_V + A_HEADS * SLOT], start=True, stop=True) \
                        .then_inc(v_projected, 1)
                for g in range(KT):
                    pe.wait_ge(v_taken, i * BB * ST + BB * ST - 1 + g)
                    nc.tensor.matmul(pp[g][:], w[:, WA_Q + g * P:WA_Q + (g + 1) * P], c_pair[:],
                                     start=True, stop=True).then_inc(q_projected, 1)

            pe.wait_ge(k_ready, PAIRS * KT)
            with nc.tensor.Fori(0, PAIRS) as i:
                project_qv(i)
                for u in range(U + 3):
                    if u < U:
                        b, head = divmod(u, A_HEADS)
                        pe.wait_ge(q_taken, i * A_HEADS + head + 1) if u < A_HEADS else None
                        att.scores(
                            i, u,
                            lambda t: query[:, head, b * SEQ + t * P:][:, 0:P],
                            lambda n: keys[:, head // 8, ds(i * TOK + b * SEQ, n)])
                    if 0 <= u - 2 < U:
                        att.turn(i, u - 2)
                    if 0 <= u - 3 < U:
                        b, head = divmod(u - 3, A_HEADS)
                        att.mix(i, u - 3, lambda k: values[:, b * ST + k,
                                                           head * SLOT:(head + 1) * SLOT])
                pe.wait_ge(att.o_taken, (i + 1) * att.banks)
                for k in range(KT):
                    for g in range(A_GROUPS):
                        at = WA_O + g * D + k * P
                        op = nc.tensor.matmul(pp[k][:], w[:, at:at + P], o[:, g, :],
                                              start=(g == 0), stop=(g == A_GROUPS - 1))
                op.then_inc(o_projected, 1)

        @block.scalar
        def _(act):
            tanh_h()
            act.wait_ge(centred, 3)
            nc.scalar.activation(stat[:, 1], stat[:, 1], ACT.Ln, scale=1.0 / LATENT,
                                 bias=net.pp[:, PP_EPS_LN:PP_EPS_LN + 1]).then_inc(logs, 1)
            act.wait_ge(logs, 1)
            nc.scalar.activation(stat[:, 1], stat[:, 1], ACT.Exp, scale=-0.5) \
                .then_inc(rstd_ready, 1)
            act.wait_ge(c_turned, 1)
            for pair in range(PAIRS):
                nc.scalar.activation(c_t[:, pair * TOK:(pair + 1) * TOK], pp[pair][:],
                                     ACT.Identity, scale=net.pp[:, PP_LNG:PP_LNG + 1],
                                     bias=net.pp[:, PP_LNB:PP_LNB + 1]).then_inc(c_ready, 1)
            for n in range(PAIRS * KT):
                pair, g = divmod(n, KT)
                act.wait_ge(k_projected, n + 1)
                nc.scalar.copy(keys[:, g, pair * TOK:(pair + 1) * TOK], (att.ps + att.pt)[n][:]) \
                    .then_inc(k_ready, 1)

            def take_query(i, h):
                act.wait_ge(q_projected, i * KT + h // 8 + 1)
                nc.scalar.activation(query[:, h, :], pp[h // 8][:], ACT.Copy,
                                     scale=net.pp[:, PP_HEADMASK + h % 8:][:, 0:1]) \
                    .then_inc(q_taken, 1)

            with nc.scalar.Fori(0, PAIRS) as i:
                for n in range(BB * ST):
                    act.wait_ge(v_projected, i * BB * ST + n + 1)
                    nc.scalar.copy(values[:, n, :], pp[n % 2][:]).then_inc(v_taken, 1)
                for h in range(A_HEADS):
                    take_query(i, h)
                for u in range(U + 3):
                    if u < U:
                        att.exponential(i, u)
                    if 0 <= u - 2 < U and u % 2:
                        att.take_turned(i, u - 2)
                    if 0 <= u - 3 < U and (u - 3) % att.per_bank == att.per_bank - 1:
                        bank = (u - 3) // att.per_bank
                        b, g = divmod(bank, A_GROUPS)
                        act.wait_ge(att.o_ready, i * att.banks + bank + 1)
                        act.wait_ge(o_projected, i)
                        nc.scalar.copy(o[:, g, b * SEQ:(b + 1) * SEQ],
                                       att.po[bank % 2][:, 0:SEQ]).then_inc(att.o_taken, 1)
                    if u == 4:
                        unit.scalar(i + 3 * PAIRS)

        @block.gpsimd
        def _(pool):
            net.clear_last_stage(pool)
            with nc.gpsimd.Fori(0, PAIRS) as i:
                unit.pool(i, i + 3 * PAIRS)

        @block.vector
        def _(dve):
            v = nc.vector
            make_h()
            link = Links(dve, once)
            dve.wait_ge(down_ready, 1)
            for pair in range(PAIRS):
                n = BB * ST
                src = pp[pair][:].rearrange("p (n h c) -> p n h c", n=n, h=2)
                op = v.tensor_reduce(stat[:, 0, pair * n:(pair + 1) * n, :], src, AX_X, ALU.add)
            link(op)
            link(v.tensor_scalar(stat[:, 0], stat[:, 0], 1.0 / LATENT, None, ALU.mult))
            wide = [P, TOK_TILES, 2, LATENT]
            for pair in range(PAIRS):
                n = slice(pair * BB * ST, (pair + 1) * BB * ST)
                src = pp[pair][:].rearrange("p (n h c) -> p n h c", n=BB * ST, h=2)
                mean = stat[:, 0, n, :, None].to_broadcast([P, BB * ST, 2, LATENT])
                v.tensor_tensor(latent[:, n], src, mean, ALU.subtract).then_inc(centred, 1)
            dve.wait_ge(centred, 2)
            link(v.tensor_tensor(latent_sq[:], latent[:], latent[:], ALU.mult))
            v.tensor_reduce(stat[:, 1], latent_sq[:], AX_X, ALU.add).then_inc(centred, 1)
            dve.wait_ge(rstd_ready, 1)
            v.tensor_tensor(latent[:], latent[:], stat[:, 1, :, :, None].to_broadcast(wide),
                            ALU.mult).then_inc(normed, 1)
            dve.wait_ge(c_ready, PAIRS)

            with nc.vector.Fori(0, PAIRS) as i:
                link = Links(dve, links, i, LINKS)
                steps = unit.vector(link, i, i + 3 * PAIRS)
                dve.wait_ge(q_projected, i * KT)
                v.tensor_copy(c_pair[:], c_t[:, ds(i * TOK, TOK)]).then_inc(c_pair_ready, 1)
                for u in range(U + 3):
                    if u < U:
                        att.maximum(i, u)
                    if 0 <= u - 1 < U:
                        att.normalise(i, u - 1, link)
                    if 0 <= u - 2 < U and u % 2 == 0:
                        att.take_turned(i, u - 2)
                    if steps and u >= 2:
                        steps.pop(0)()
                assert not steps
                dve.wait_ge(o_projected, i + 1)
                for k in range(KT):
                    out = net.x[:, ds(i * PAIR + k * TOK, TOK)]
                    op = v.tensor_tensor(out, out, pp[k][:], ALU.add)
                op.then_inc(x_added, 1)
                link.check()



Q_HEADS, KV_HEADS, Q_HEAD = 16, 4, 128
CHUNK = 512
CHUNKS = (Q_HEADS + 2 * KV_HEADS) * Q_HEAD // CHUNK
QK_CHUNKS = CHUNKS - 1
WG_QKV, WG_O, WG_END = np.cumsum([0, KT * CHUNKS * CHUNK, Q_HEADS * D]).tolist()
HALF = Q_HEAD // 2
RT_COS, RT_SIN, RT_QW, RT_KW, RT_END = np.cumsum([0, ST * HALF, ST * HALF, Q_HEAD, Q_HEAD]).tolist()


def stage_gqa(net):
    nc = net.nc
    U = BB * Q_HEADS
    TILES = BB * ST
    STEPS = TILES * CHUNKS
    QK = TILES * QK_CHUNKS
    LAG = 3
    LINKS = U * Attend.LINKS + QK + 2
    net.next_stage()
    with ExitStack() as mem:
        def sb(name, shape, dt=F32):
            return mem.enter_context(nc.sbuf_tensor(name, shape, dt))

        def sem(name):
            return net.stage_sem(mem, name)

        w = net.weights
        tail = w[:, WG_END:]
        rope = tail[:, 0:RT_END]
        table = tail[:, RT_END:RT_END + 8 * Q_HEAD].rearrange("p (a t c d) -> p a t c d", a=2, t=ST,
                                                            c=2)
        at = RT_END + 8 * Q_HEAD
        chunk_sq = tail[:, at:at + 2 * CHUNK].rearrange("p (n d) -> p n d", n=2)
        spare = net.m[:].rearrange("p (n d) -> p n d", d=CHUNK)
        normed, by_cos = spare[:, 0:2], spare[:, 2:4]
        by_sin = sb("by_sin", [P, CHUNK])
        rotated = sb("rotated", [P, 2, CHUNK])
        h_norm = sb("h_norm", [P, PAIR])
        hidden = h_norm
        h_sq = sb("h_sq", [P, PAIR])
        q_t = sb("q_t", [P, Q_HEADS, TOK])
        k_t = sb("k_t", [P, KV_HEADS, TOK])
        values = sb("values_gqa", [P, TILES, CHUNK])
        root = sb("root_gqa", [P, TOK])
        scale = sb("scale_gqa", [P, TILES])
        head_scale = sb("head_scale", [P, 4, 4])

        def rows_of(place):
            return slice(0, P), place * SEQ

        att = Attend(net, mem, "_gqa", Q_HEADS, 2, rows_of)
        pp = [mem.enter_context(nc.psum_tensor(f"gqa_out{n}", [P, 512], F32)) for n in range(2)]
        ring = att.ps + pp

        rope_loaded, table_ready = sem("rope_loaded"), sem("table_ready")
        h_norm_ready, h_squared = sem("h_norm_ready"), sem("h_squared")
        norm_summed, scale_log, scale_ready = (sem("norm_summed"), sem("scale_log"),
                                               sem("scale_ready"))
        chunk_ready, qk_taken, v_taken = sem("chunk_ready"), sem("qk_taken"), sem("v_taken_gqa")
        chunk_squared, chunk_summed = sem("chunk_squared"), sem("chunk_summed")
        head_log, head_scale_ready = sem("head_log"), sem("head_scale_ready")
        cos_ready, sin_ready, rotated_ready = sem("cos_ready"), sem("sin_ready"), sem("rotated_ready")
        qk_turned, qk_stored = sem("qk_turned"), sem("qk_stored")
        o_projected, hidden_ready = sem("o_projected_gqa"), sem("hidden_ready_gqa")
        hidden_squared, hidden_summed = sem("hidden_squared"), sem("hidden_summed")
        root_log, root_ready, normed_ready = sem("root_log"), sem("root_ready_gqa"), sem("normed")
        links, once = sem("gqa_links"), sem("gqa_once")
        tanh_h, make_h, h_ready = condition_input(net, "_gqa")

        def chunk_of(step):
            n, c = divmod(step, CHUNKS)
            return n, c, n * QK_CHUNKS + c

        block = mem.enter_context(nc.Block())

        @block.sync
        def _(sp):
            sp.dma_start(rope, net.dram["rope"]).then_inc(rope_loaded, 16)
            for dst, src, done in net.moe1_loads:
                sp.dma_start(dst, src).then_inc(done, 16)

        @block.tensor
        def _(pe):
            for s in net.gqa_loaded:
                pe.wait_ge(s, 16)

            def project(i, step):
                n, c, _ = chunk_of(step)
                if step >= 4:
                    _, c4, j4 = chunk_of(step - 4)
                    if c4 < QK_CHUNKS:
                        pe.wait_ge(qk_taken, i * QK + j4 + 1)
                    else:
                        pe.wait_ge(v_taken, i * TILES + step // CHUNKS)
                out = ring[step % 4]
                for k in range(KT):
                    cols = WG_QKV + (k * CHUNKS + c) * CHUNK
                    op = nc.tensor.matmul(out[:], h_norm[:, k * TOK + n * P:][:, 0:P],
                                          w[:, cols:cols + CHUNK], start=(k == 0),
                                          stop=(k == KT - 1))
                op.then_inc(chunk_ready, 1)

            def turn_chunk(i, step):
                _, c, j = chunk_of(step)
                if c == QK_CHUNKS:
                    return
                pe.wait_ge(rotated_ready, i * QK + j + 1)
                pe.wait_ge(qk_stored, i * QK + max(j - 1, 0))
                for hd in range(4):
                    op = nc.tensor.transpose(att.pt[j % 2][:, hd * P:(hd + 1) * P],
                                             rotated[:, j % 2, hd * P:(hd + 1) * P],
                                             net.ident[:])
                op.then_inc(qk_turned, 1)

            with nc.tensor.Fori(0, PAIRS) as i:
                pe.wait_ge(h_norm_ready, i + 1)
                pe.wait_ge(h_squared, i + 1)
                pe.wait_ge(normed_ready, i)
                for n in range(TILES):
                    for k in range(KT):
                        op = nc.tensor.matmul(att.po[1][:, n:n + 1],
                                              h_sq[:, k * TOK + n * P:][:, 0:P],
                                              net.ones[:, 0:1], start=(k == 0),
                                              stop=(k == KT - 1))
                op.then_inc(norm_summed, 1)
                for step in range(STEPS + LAG):
                    if step < STEPS:
                        project(i, step)
                    if step >= LAG:
                        turn_chunk(i, step - LAG)
                pe.wait_ge(qk_stored, (i + 1) * QK)
                pe.wait_ge(v_taken, (i + 1) * TILES)
                for u in range(U + 3):
                    if u < U:
                        b, head = divmod(u, Q_HEADS)
                        att.scores(i, u, lambda t: q_t[:, head, b * SEQ + t * P:][:, 0:P],
                                   lambda n: k_t[:, head // 4, b * SEQ:b * SEQ + n])
                    if 0 <= u - 2 < U:
                        att.turn(i, u - 2)
                    if 0 <= u - 3 < U:
                        b, head = divmod(u - 3, Q_HEADS)
                        kv = slice(head // 4 * Q_HEAD, (head // 4 + 1) * Q_HEAD)
                        att.mix(i, u - 3, lambda k: values[:, b * ST + k, kv])
                pe.wait_ge(att.o_taken, (i + 1) * att.banks)
                for k in range(KT):
                    for head in range(Q_HEADS):
                        cols = WG_O + head * D + k * P
                        op = nc.tensor.matmul(pp[k][:], w[:, cols:cols + P], q_t[:, head, :],
                                              start=(head == 0), stop=(head == Q_HEADS - 1))
                op.then_inc(o_projected, 1)
                pe.wait_ge(hidden_squared, i + 1)
                for k in range(KT):
                    op = nc.tensor.matmul(att.po[0][:], net.ones[:],
                                          h_sq[:, k * TOK:(k + 1) * TOK], start=(k == 0),
                                          stop=(k == KT - 1))
                op.then_inc(hidden_summed, 1)

        @block.scalar
        def _(act):
            tanh_h()
            eps = net.pp[:, PP_EPS_RMS:PP_EPS_RMS + 1]

            def square_chunk(i, step):
                n, c, j = chunk_of(step)
                act.wait_ge(chunk_ready, i * STEPS + step + 1)
                src = ring[step % 4][:]
                if c == QK_CHUNKS:
                    nc.scalar.activation(values[:, n, :], src, ACT.Copy, scale=scale[:, n:n + 1]) \
                        .then_inc(v_taken, 1)
                    return
                act.wait_ge(chunk_summed, i * QK + max(j - 1, 0))
                nc.scalar.activation(chunk_sq[:, j % 2], src, ACT.Square,
                                     scale=scale[:, n:n + 1]).then_inc(chunk_squared, 1)

            def scale_heads(i, step):
                _, c, j = chunk_of(step)
                if c == QK_CHUNKS:
                    return
                s = head_scale[:, j % 4]
                act.wait_ge(chunk_summed, i * QK + j + 1)
                nc.scalar.activation(s, s, ACT.Ln, scale=1.0 / Q_HEAD, bias=eps) \
                    .then_inc(head_log, 1)
                act.wait_ge(head_log, i * QK + j + 1)
                nc.scalar.activation(s, s, ACT.Exp, scale=-0.5).then_inc(head_scale_ready, 1)

            def store_chunk(i, step):
                n, c, j = chunk_of(step)
                if c == QK_CHUNKS:
                    return
                act.wait_ge(qk_turned, i * QK + j + 1)
                out = q_t[:, 4 * c:4 * c + 4] if c < QK_CHUNKS - 1 else k_t[:]
                nc.scalar.copy(out[:, :, n * P:(n + 1) * P],
                               att.pt[j % 2][:].rearrange("p (h t) -> p h t", h=4)) \
                    .then_inc(qk_stored, 1)

            with nc.scalar.Fori(0, PAIRS) as i:
                act.wait_ge(hidden_summed, i)
                act.wait_ge(h_ready, PAIRS)
                nc.scalar.activation(h_sq[:], net.h[:, ds(i * PAIR, PAIR)], ACT.Square) \
                    .then_inc(h_squared, 1)
                act.wait_ge(norm_summed, i + 1)
                nc.scalar.activation(scale[:], att.po[1][:, 0:TILES], ACT.Ln, scale=1.0 / D,
                                     bias=eps).then_inc(scale_log, 1)
                act.wait_ge(scale_log, i + 1)
                nc.scalar.activation(scale[:], scale[:], ACT.Exp, scale=-0.5) \
                    .then_inc(scale_ready, 1)
                act.wait_ge(scale_ready, i + 1)
                for step in range(STEPS + LAG + 1):
                    if step < STEPS:
                        square_chunk(i, step)
                    if 0 <= step - 1 < STEPS:
                        scale_heads(i, step - 1)
                    if step >= LAG + 1:
                        store_chunk(i, step - LAG - 1)
                for u in range(U + 3):
                    if u < U:
                        att.exponential(i, u)
                    if 0 <= u - 2 < U and u % 2:
                        att.take_turned(i, u - 2)
                    if 0 <= u - 3 < U and (u - 3) % 2:
                        bank = (u - 3) // 2
                        b, pair_of_heads = divmod(bank, Q_HEADS // 2)
                        act.wait_ge(att.o_ready, i * att.banks + bank + 1)
                        nc.scalar.copy(
                            q_t[:, 2 * pair_of_heads:2 * pair_of_heads + 2,
                                b * SEQ:(b + 1) * SEQ],
                            att.po[bank % 2][:].rearrange("p (h t) -> p h t", h=2)) \
                            .then_inc(att.o_taken, 1)
                act.wait_ge(hidden_ready, i + 1)
                nc.scalar.activation(h_sq[:], hidden[:], ACT.Square) \
                    .then_inc(hidden_squared, 1)
                act.wait_ge(hidden_summed, i + 1)
                nc.scalar.activation(root[:], att.po[0][:], ACT.Ln, scale=1.0 / D, bias=eps) \
                    .then_inc(root_log, 1)
                act.wait_ge(root_log, i + 1)
                nc.scalar.activation(root[:], root[:], ACT.Exp, scale=-0.5) \
                    .then_inc(root_ready, 1)

        @block.gpsimd
        def _(pool):
            net.clear_last_stage(pool)
            with nc.gpsimd.Fori(0, PAIRS) as i:
                for step in range(STEPS):
                    n, c, j = chunk_of(step)
                    if c == QK_CHUNKS:
                        continue
                    src = normed[:, j % 2].rearrange("p (h s d) -> p h s d", h=4, s=2)
                    sin = table[:, int(c == QK_CHUNKS - 1), n % ST, 1].rearrange(
                        "p (s d) -> p s d", s=2)
                    pool.wait_ge(qk_taken, i * QK + j + 1)
                    pool.wait_ge(rotated_ready, i * QK + j)
                    out = by_sin[:].rearrange("p (h s d) -> p h s d", h=4, s=2)
                    for s in range(2):
                        op = nc.gpsimd.tensor_tensor(
                            out[:, :, s, :], src[:, :, 1 - s, :],
                            sin[:, None, s, :].to_broadcast([P, 4, HALF]), ALU.mult)
                    op.then_inc(sin_ready, 1)
                    pool.wait_ge(sin_ready, i * QK + j + 1)
                    pool.wait_ge(cos_ready, i * QK + j + 1)
                    pool.wait_ge(qk_turned, i * QK + max(j - 1, 0))
                    nc.gpsimd.tensor_tensor(rotated[:, j % 2], by_cos[:, j % 2], by_sin[:],
                                            ALU.add).then_inc(rotated_ready, 1)

        @block.vector
        def _(dve):
            v = nc.vector
            make_h()
            link = Links(dve, once)
            dve.wait_ge(rope_loaded, 16)
            qw = rope[:, RT_QW:RT_QW + Q_HEAD]
            link(v.tensor_scalar(qw, qw, Q_HEAD ** -0.5, None, ALU.mult))
            for a, at in enumerate((RT_QW, RT_KW)):
                for t in range(ST):
                    weight = rope[:, at:at + Q_HEAD]
                    cos = rope[:, RT_COS + t * HALF:RT_COS + (t + 1) * HALF]
                    sin = rope[:, RT_SIN + t * HALF:RT_SIN + (t + 1) * HALF]
                    for s in range(2):
                        own = slice(s * HALF, (s + 1) * HALF)
                        other = slice((1 - s) * HALF, (2 - s) * HALF)
                        v.tensor_tensor(table[:, a, t, 0, own], weight[:, own], cos, ALU.mult)
                        op = v.scalar_tensor_tensor(table[:, a, t, 1, own], weight[:, other],
                                                    1.0 if s else -1.0, sin, ALU.mult, ALU.mult)
            op.then_inc(table_ready, 1)
            dve.wait_ge(table_ready, 1)

            def sum_chunk(i, step):
                _, c, j = chunk_of(step)
                if c == QK_CHUNKS:
                    return
                dve.wait_ge(chunk_squared, i * QK + j + 1)
                v.tensor_reduce(head_scale[:, j % 4],
                                chunk_sq[:, j % 2].rearrange("p (h d) -> p h d", h=4), AX_X,
                                ALU.add).then_inc(chunk_summed, 1)

            def norm_chunk(i, step, link):
                n, c, j = chunk_of(step)
                if c == QK_CHUNKS:
                    return
                dve.wait_ge(head_scale_ready, i * QK + j + 1)
                s = head_scale[:, j % 4]
                link(v.tensor_scalar(s, s, scale[:, n:n + 1], None, ALU.mult))
                dve.wait_ge(rotated_ready, i * QK + max(j - 1, 0))
                v.tensor_tensor(normed[:, j % 2].rearrange("p (h d) -> p h d", h=4),
                                ring[step % 4][:].rearrange("p (h d) -> p h d", h=4),
                                s[:, :, None].to_broadcast([P, 4, Q_HEAD]), ALU.mult) \
                    .then_inc(qk_taken, 1)
                dve.wait_ge(qk_taken, i * QK + j + 1)
                cos = table[:, int(c == QK_CHUNKS - 1), n % ST, 0]
                v.tensor_tensor(by_cos[:, j % 2].rearrange("p (h d) -> p h d", h=4),
                                normed[:, j % 2].rearrange("p (h d) -> p h d", h=4),
                                cos[:, None, :].to_broadcast([P, 4, Q_HEAD]), ALU.mult) \
                    .then_inc(cos_ready, 1)

            with nc.vector.Fori(0, PAIRS) as i:
                link = Links(dve, links, i, LINKS)
                dve.wait_ge(chunk_ready, i * STEPS)
                dve.wait_ge(normed_ready, i)
                for k in range(KT):
                    op = v.tensor_scalar(h_norm[:, k * TOK:(k + 1) * TOK],
                                         net.h[:, ds(i * PAIR + k * TOK, TOK)],
                                         net.pp[:, PP_ATTN_NORM + k:PP_ATTN_NORM + k + 1], None,
                                         ALU.mult)
                op.then_inc(h_norm_ready, 1)
                for step in range(STEPS + 1):
                    if step < STEPS:
                        sum_chunk(i, step)
                    if step >= 1:
                        norm_chunk(i, step - 1, link)
                for u in range(U + 3):
                    if u < U:
                        att.maximum(i, u)
                    if 0 <= u - 1 < U:
                        att.normalise(i, u - 1, link)
                    if 0 <= u - 2 < U and u % 2 == 0:
                        att.take_turned(i, u - 2)
                dve.wait_ge(o_projected, i + 1)
                hs = [net.h[:, ds(i * PAIR + k * TOK, TOK)] for k in range(KT)]
                cur = [hidden[:, k * TOK:(k + 1) * TOK] for k in range(KT)]
                for k in range(KT):
                    op = v.tensor_tensor(cur[k], hs[k], pp[k][:], ALU.add)
                op.then_inc(hidden_ready, 1)
                dve.wait_ge(hidden_ready, i + 1)
                for k in range(KT):
                    out = net.x[:, ds(i * PAIR + k * TOK, TOK)]
                    link(v.tensor_tensor(out, out, cur[k], ALU.add))
                dve.wait_ge(root_ready, i + 1)
                for k in range(KT):
                    weight = net.pp[:, PP_FFN_NORM + k:PP_FFN_NORM + k + 1]
                    op = v.scalar_tensor_tensor(hs[k], cur[k], weight, root[:], ALU.mult, ALU.mult)
                op.then_inc(normed_ready, 1)
                link.check()



_OUT = [P, PAIRS * PAIR]


def _moe0_weights(net):
    early = W_OUT0 // MOE_COLS
    late = early + (W_MIXER - W_OUT0) // MOE_COLS
    groups = [(0, 4), (4, 8), (8, early), (early, late), (late, late + 4), (late + 4, MOE0_TILES)]
    sems = [net.sem(f"moe0_loaded{n}") for n in range(len(groups))]
    src = net.dram["w_moe0"]

    def load(n, dst):
        a, b = groups[n]
        return dst, src[:, a * MOE_COLS:b * MOE_COLS], sems[n]

    def place(a, b):
        at = a * MOE_COLS if a < early else W_OUT0 + (a - early) * MOE_COLS
        return net.weights[:, at:at + (b - a) * MOE_COLS]

    net.moe0_early = [load(n, place(*groups[n])) for n in range(3)]

    def weights(sb):
        rest = sb("moe_rest", [P, (MOE0_TILES - late) * MOE_COLS])

        def at(a, b):
            return place(a, b) if a < late else rest[:, (a - late) * MOE_COLS:(b - late) * MOE_COLS]

        loads = [load(n, at(*groups[n])) for n in range(3, len(groups))]
        return (lambda m: at(m, m + 1),
                lambda m: next(s for s, (a, b) in zip(sems, groups) if a <= m < b), loads)

    return weights


def _moe1_weights(net):
    places, loads, m = [], [], 0
    for buffer in (net.f, net.e, net.e_pair, net.ev_pair, net.decay, net.num, net.num_b, net.den, net.den_b):
        n = min(buffer.shape[1] // MOE_COLS, MOE1_TILES - m)
        if n > 0:
            done = net.sem(f"moe1_loaded{len(loads)}")
            loads.append((buffer[:, 0:n * MOE_COLS],
                          net.dram["w_moe1"][:, m * MOE_COLS:(m + n) * MOE_COLS], done))
            places += [(buffer[:, k * MOE_COLS:(k + 1) * MOE_COLS], done) for k in range(n)]
            m += n
    assert m == MOE1_TILES
    net.moe1_loads = loads
    return lambda sb: (lambda m: places[m][0], lambda m: places[m][1], [])


def _network(nc, dram, out):
    with ExitStack() as stack:
        net = Net(nc, stack, dram)
        net.weights = stack.enter_context(nc.sbuf_tensor("weights", [P, W_MIXER], F32))
        net.win_chunks = [(0, W_BCXG + 6 * KT * P), (W_BCXG + 6 * KT * P, W_BCXG + 18 * KT * P),
                          (W_BCXG + 18 * KT * P, W_OUT0), (W_OUT0, W_MIXER)]
        moe0_weights, moe1_weights = _moe0_weights(net), _moe1_weights(net)
        net.gqa_loaded = [net.sem(f"gqa_loaded{n}") for n in range(2)]
        net.gqa_early = [(net.weights[:, a:b], dram["w_gqa"][:, a:b], s)
                         for a, b, s in zip((0, WG_O), (WG_O, WG_END), net.gqa_loaded)]
        stage_condition(net)
        stage_mixer(net)
        stage_moe(net, MOE0, moe0_weights, condition_input(net, "_moe0"), 2)
        stage_latent_attention(net)
        stage_gqa(net)
        stage_moe(net, MOE1, moe1_weights, None, None)
        with nc.Block() as block:
            @block.sync
            def _(sp):
                sp.wait_ge(net.x_loaded, 16)
                sp.dma_start(out, net.x[:]).then_inc(net.out_stored, 16)
                sp.wait_ge(net.out_stored, 16)


def _channels(a):
    return np.ascontiguousarray(
        a.reshape(PAIRS, TOK, KT, P).transpose(3, 0, 2, 1).reshape(P, PAIRS * PAIR))


def _stationary(w):
    return w.reshape(-1, P, w.shape[1]).transpose(1, 0, 2).reshape(P, -1)


def _column(v, tiles):
    return v.reshape(tiles, P).T


def _padded(v, rows=P):
    out = np.zeros((rows, 1), np.float32)
    out[:len(v), 0] = v
    return out


def _params(i):
    conv_tiles = [XT_TILES, XT_TILES + 1, *range(XT_TILES)]
    w = i["L0_attn_conv_w"].reshape(CONV_TILES, P, TAPS)[conv_tiles]
    full = lambda x: np.full((P, 1), x, np.float32)
    zero = full(0.0)
    heads = np.zeros((P, 8), np.float32)
    heads[np.arange(P), np.arange(P) // A_HEAD] = A_HEAD ** -0.5
    cols = [
        np.concatenate([_column(i[n], KT) for n in ("L0_cond_w", "L0_cond2_w", "L1_cond_w",
                                                    "L1_cond2_w")], 1),
        np.concatenate([_column(i[n], KT) for n in ("L0_cond_u", "L0_cond2_u", "L1_cond_u",
                                                    "L1_cond2_u")], 1),
        w.transpose(1, 0, 2).reshape(P, -1),
        i["L0_attn_conv_b"].reshape(CONV_TILES, P)[conv_tiles].T,
        _padded(i["L0_attn_dt_bias"]), _padded(i["L0_attn_A_log"]),
        np.repeat(i["L0_attn_D_param"], HEAD).reshape(XT_TILES, P).T,
        _column(i["L0_attn_norm_w"], XT_TILES),
        full(EPS_MIXER), full(np.log(0.5)),
        np.concatenate([i["L1_attn_q_ln_g"], i["L1_attn_kv_ln_g"]])[:, None],
        np.concatenate([i["L1_attn_q_ln_b"], i["L1_attn_kv_ln_b"]])[:, None],
        full(1e-5), _column(i["L1_ffn_attn_norm_w"], KT), _column(i["L1_ffn_ffn_norm_w"], KT),
        full(1e-6), heads,
        np.broadcast_to(i["cond_512"].reshape(1, -1), (P, BATCH * 64)),
        np.broadcast_to(i["L0_ffn_gate_b"], (P, E0)),
        i["L1_ffn_q_norm_w"][:, None], i["L1_ffn_k_norm_w"][:, None],
    ]
    out = np.concatenate(cols, 1)
    assert out.shape[1] == PP_END
    return np.ascontiguousarray(out)


def _bf16_constants():
    out = np.zeros((P, CB_END), np.float32)
    r = np.arange(P)
    out[r, CB_IDENT + r] = 1.0
    out[:, CB_MASK_QK:CB_MASK_QK + P][r[None, :] > r[:, None]] = -1e30
    out[:, CB_MASK_QK + P:CB_MASK_QK + SEQ] = -1e30
    out[:, CB_MASK_ST:CB_MASK_ST + P][r[None, :] < r[:, None]] = -1e30
    for part in range(3):
        for h in range(HEADS):
            out[part * HEADS + h, CB_SEL + h * P:CB_SEL + (h + 1) * P] = 1.0
    return out.astype(mybir.dt.np(BF16))


def _mixer_weights(i):
    w = i["L0_attn_W_in"]
    tile = lambda row: _stationary(w[row:row + P].T)
    tiles = [_stationary(w[2 * INNER + 2 * STATE:].T), tile(2 * INNER), tile(2 * INNER + P)]
    for s in range(XT_TILES):
        tiles += [tile(INNER + s * P), tile(s * P)]
    tiles.append(_stationary(i["L0_attn_W_out"].T))
    return np.ascontiguousarray(np.concatenate(tiles, 1))


def _moe_tiles(w1, w3, w2):
    tiles = []
    for m in range(w2.shape[0] // P):
        c = slice(m * P, (m + 1) * P)
        tiles += [_stationary(w1[:, c]), _stationary(w3[:, c]), w2[c]]
    return np.ascontiguousarray(np.concatenate(tiles, 1))


def _moe0(i):
    pad = SHARED_TILES * P - FF
    wide = [np.concatenate([np.pad(i[f"L0_ffn_{n}_shared"], ((0, 0), (0, pad))),
                            i[f"L0_ffn_{n}_routed"].transpose(1, 0, 2).reshape(D, -1)], 1)
            for n in ("w1", "w3")]
    down = np.concatenate([np.pad(i["L0_ffn_w2_shared"], ((0, pad), (0, 0))),
                           i["L0_ffn_w2_routed"].reshape(-1, D)])
    return _moe_tiles(*wide, down)


def _moe1(i):
    return _moe_tiles(i["L1_ffn_wg"].reshape(-1, D).T, i["L1_ffn_wu"].reshape(-1, D).T,
                      i["L1_ffn_wd"].transpose(0, 2, 1).reshape(-1, D))


def _latent_weights(i):
    zeros = np.zeros((LATENT, D), np.float32)
    ukv = i["L1_attn_W_ukv"]
    v = np.pad(ukv[:, D:].reshape(LATENT, A_HEADS, A_HEAD),
               ((LATENT, 0), (0, 0), (0, SLOT - A_HEAD))).reshape(P, -1)
    o = np.pad(i["L1_attn_W_o"].T.reshape(A_HEADS, A_HEAD, D),
               ((0, 0), (0, SLOT - A_HEAD), (0, 0))).reshape(-1, D)
    down = np.concatenate([i["L1_attn_W_dq"], i["L1_attn_W_dkv"]], 1)
    parts = [_stationary(down), np.concatenate([i["L1_attn_W_uq"], zeros]),
             np.concatenate([zeros, ukv[:, :D]]), v, _stationary(o)]
    return np.ascontiguousarray(np.concatenate(parts, 1))


def _gqa_weights(i):
    qkv = np.concatenate([i["L1_ffn_q_w"], i["L1_ffn_k_w"], i["L1_ffn_v_w"]]).T
    return np.ascontiguousarray(
        np.concatenate([_stationary(qkv), _stationary(i["L1_ffn_o_w"].T)], 1))


def _rope(i):
    freqs = 1.0 / 1e6 ** (np.arange(0, Q_HEAD, 2, dtype=np.float32) / np.float32(Q_HEAD))
    angle = np.outer(np.arange(SEQ, dtype=np.float32), freqs.astype(np.float32))
    angle = angle.astype(np.float32).reshape(ST, P, HALF).transpose(1, 0, 2).reshape(P, -1)
    rows = [np.broadcast_to(i[n], (P, Q_HEAD)) for n in ("L1_ffn_q_norm_w", "L1_ffn_k_norm_w")]
    return np.concatenate([np.cos(angle), np.sin(angle), *rows], 1).astype(np.float32)


def _expert_sel(experts, rows=32):
    out = np.zeros((3 * rows, experts * FF), np.float32)
    for part in range(3):
        for e in range(experts):
            out[part * rows + e, e * FF:(e + 1) * FF] = 1.0
    return out.astype(mybir.dt.np(BF16))


def kernel(**inputs):
    import concourse.bacc as bacc
    from concourse.bass_utils import run_bass_kernel_spmd

    i = {n: np.asarray(a) for n, a in inputs.items()}
    arrays = {
        "x": _channels(i["x"].reshape(-1, D)),
        "f": _channels(i["fside_BxSxS_0"].reshape(-1, D)),
        "pp": _params(i),
        "cb": _bf16_constants(),
        "ident": np.eye(P, dtype=np.float32),
        "w_mixer": _mixer_weights(i),
        "w_latent": _latent_weights(i),
        "w_gqa": _gqa_weights(i), "rope": _rope(i),
        "w_moe0": _moe0(i), "gate0": np.ascontiguousarray(_stationary(i["L0_ffn_gate_w"].T)),
        "sel0": _expert_sel(E0),
        "w_moe1": _moe1(i), "gate1": np.ascontiguousarray(_stationary(i["L1_ffn_gate_w"].T)),
        "sel1": _expert_sel(E1),
    }
    nc = bacc.Bacc("TRN2", target_bir_lowering=False, num_devices=1)
    dram = {n: nc.dram_tensor(f"in_{n}", a.shape, mybir.dt.from_np(a.dtype), kind="ExternalInput").ap()
            for n, a in arrays.items()}
    out = nc.dram_tensor("out", _OUT, F32, kind="ExternalOutput").ap()
    _network(nc, dram, out)
    result = run_bass_kernel_spmd(nc, [{f"in_{n}": a for n, a in arrays.items()}], core_ids=[0])
    y = result.results[0]["out"]
    return y.reshape(P, PAIRS, KT, TOK).transpose(1, 3, 2, 0).reshape(BATCH, SEQ, D)
```

```python
from contextlib import ExitStack
from functools import partial

import concourse.bass as bass
import numpy as np
from concourse import mybir

F32 = mybir.dt.float32
BF16 = mybir.dt.bfloat16
ALU = mybir.AluOpType
ACT = mybir.ActivationFunctionType
AX_X = mybir.AxisListType.X
ds = bass.ds

P = 128
BATCH, SEQ, D = 4, 256, 256
KT = D // P
PAIRS = 2
BB = BATCH // PAIRS
TOK = BB * SEQ
PAIR = KT * TOK
SEG = SEQ + 1
UNIT = KT * BB * SEG
ST = SEQ // P

HEADS, HEAD, STATE, TAPS = 32, 64, 128, 4
INNER = HEADS * HEAD
XT_TILES = INNER // P
CONV_TILES = XT_TILES + 2
TILE_HEADS = P // HEAD
TRI = SEQ + P
EPS_MIXER = 1e-5

FF = 176
E0, K0 = 16, 4
E1, K1 = 8, 2
SHARED_TILES = 2
MOE0_TILES = SHARED_TILES + E0 * FF // P
MOE1_TILES = E1 * FF // P
MOE_COLS = 3 * D

(PP_W, PP_U, PP_CONVW, PP_CONVB, PP_DTB, PP_ALOG, PP_D, PP_NORM, PP_EPS_MIXER, PP_LN_HALF, PP_LNG,
 PP_LNB, PP_EPS_LN, PP_ATTN_NORM, PP_FFN_NORM, PP_EPS_RMS, PP_HEADMASK, PP_COND, PP_GATEB,
 PP_QNORM, PP_KNORM, PP_GATE0, PP_GATE1, PP_END) = np.cumsum(
    [0, 4 * KT, 4 * KT, CONV_TILES * TAPS, CONV_TILES, 1, 1, XT_TILES, XT_TILES, 1, 1, 1, 1, 1,
     KT, KT, 1, 8, BATCH * 64, E0, 1, 1, KT * E0, KT * E1]).tolist()

CB_IDENT, CB_MASK_QK, CB_MASK_ST, CB_SEL, CB_END = np.cumsum([0, P, SEQ, P, HEADS * P]).tolist()

W_DT, W_BCXG, W_OUT0 = np.cumsum([0, KT * HEADS, (2 * XT_TILES + 2) * KT * P]).tolist()
W_MIXER = W_OUT0 + XT_TILES * D


STAGE_SEMS = 44


class Links:

    def __init__(self, engine, sem, i=0, per=0):
        self.engine, self.sem, self.i, self.per, self.n = engine, sem, i, per, 0

    def __call__(self, instruction):
        self.n += 1
        instruction.then_inc(self.sem, 1)
        self.engine.wait_ge(self.sem, self.i * self.per + self.n)
        return instruction

    def mark(self, instruction):
        self.n += 1
        instruction.then_inc(self.sem, 1)
        return self.sem, self.i * self.per + self.n

    def check(self):
        assert self.n == self.per, self.n


class Net:

    def __init__(self, nc, stack, dram):
        self.nc, self.stack, self.dram = nc, stack, dram

        def sb(name, shape, dt=F32):
            return stack.enter_context(nc.sbuf_tensor(name, shape, dt))

        self.x = sb("x_res", [P, PAIRS * PAIR])
        self.h = sb("h", [P, PAIRS * PAIR])
        self.m = sb("m", [P, PAIRS * PAIR])
        self.f = sb("f", [P, PAIRS * UNIT])
        self.e = sb("e", [P, PAIRS * UNIT])
        self.e_pair = sb("e_pair", [P, UNIT])
        self.ev_pair = sb("ev_pair", [P, UNIT])
        self.f_pair = sb("f_pair", [P, UNIT])
        self.decay = sb("decay", [P, UNIT])
        self.num = sb("num", [P, UNIT])
        self.num_b = sb("num_b", [P, UNIT])
        self.den = sb("den", [P, UNIT])
        self.den_b = sb("den_b", [P, UNIT])
        self.euk = sb("euk", [P, UNIT])
        self.pp = sb("pp", [P, PP_END])
        self.cb = sb("cb", [P, CB_SEL], BF16)
        self.ident = sb("ident", [P, P])
        self.ones = sb("ones", [P, P])
        self.dcol = sb("dcol", [P, 4 * KT * BATCH])
        self.scol = sb("scol", [P, BATCH])
        self.tf = sb("tf", [P, 3 * BATCH])

        def sem(name):
            return stack.enter_context(nc.semaphore(name))

        self.sem = sem
        self.stage, self.named = 0, 0
        ids = [nc.alloc_semaphore(f"stage_sem{n}") for n in range(2 * STAGE_SEMS)]
        for handle in ids:
            nc.release_semaphore(handle)
        self.banks = [[handle.num for handle in ids[n * STAGE_SEMS:(n + 1) * STAGE_SEMS]]
                      for n in range(2)]
        self.params_loaded = sem("params_loaded")
        self.x_loaded = sem("x_loaded")
        self.f_loaded = [sem(f"f_loaded{n}") for n in range(PAIRS)]
        self.consts_loaded = sem("consts_loaded")
        self.win_loaded = [sem(f"win_loaded{n}") for n in range(4)]
        self.out_stored = sem("out_stored")
        self.consts_made = sem("consts_made")


    def next_stage(self):
        self.stage, self.named = self.stage + 1, 0

    def stage_sem(self, mem, name):
        self.named += 1
        return mem.enter_context(
            self.nc.semaphore(name, num=self.banks[self.stage % 2][self.named - 1]))

    def clear_last_stage(self, pool):
        if self.stage > 1:
            bank = self.banks[(self.stage - 1) % 2]
            pool.sem_clear(range(bank[0], bank[-1] + 1))



INVERT_PARTS = 8


class CondUnit:

    VECTOR_LINKS = 9 * KT - 1 + 1

    def __init__(self, net, c, sems):
        self.net, self.c = net, c
        (self.u_ready, self.euk_ready, self.operand_ready, self.scans_done, self.own_ready,
         self.factor_made, self.f_copied) = sems

    def pool_operands(self, pair, turn):
        net, nc = self.net, self.net.nc
        nc.gpsimd.wait_ge(self.scans_done, turn)
        for kt in range(KT):
            src = net.dcol[:, ds((self.c * KT + kt) * BATCH + pair * BB, BB)]
            last = nc.gpsimd.tensor_tensor(
                net.decay[:, kt * BB * SEG:(kt + 1) * BB * SEG].rearrange(
                    "p (b t) -> p b t", b=BB)[:, :, 1:SEG],
                src[:, :, None].to_broadcast([P, BB, SEQ]),
                net.ones[:, 0:1, None].to_broadcast([P, BB, SEQ]), ALU.mult)
            last.then_inc(self.operand_ready, 1)
        nc.gpsimd.wait_ge(self.factor_made, turn)
        unit = ds(pair * UNIT, UNIT)
        nc.gpsimd.tensor_tensor(net.ev_pair[:], net.e[:, unit], net.f[:, unit], ALU.mult) \
            .then_inc(self.operand_ready, 1)
        nc.gpsimd.tensor_tensor(net.e_pair[:], net.e[:, unit],
                                net.ones[:, 0:1].to_broadcast([P, UNIT]), ALU.mult) \
            .then_inc(self.operand_ready, 1)

    def pool_own(self, turn):
        net, nc = self.net, self.net.nc
        nc.gpsimd.wait_ge(self.operand_ready, 4 * turn + 4)
        nc.gpsimd.wait_ge(self.euk_ready, turn + 1)
        nc.gpsimd.tensor_tensor(net.euk[:], net.euk[:], net.e_pair[:], ALU.subtract) \
            .then_inc(self.own_ready, 1)

    def pool_own_f(self, turn):
        net, nc = self.net, self.net.nc
        nc.gpsimd.wait_ge(self.own_ready, 2 * turn + 1)
        nc.gpsimd.wait_ge(self.scans_done, turn + 1)
        nc.gpsimd.wait_ge(self.f_copied, turn + 1)
        nc.gpsimd.tensor_tensor(net.ev_pair[:], net.euk[:], net.f_pair[:], ALU.mult) \
            .then_inc(self.own_ready, 1)

    def scalar(self, pair, turn):
        net, nc = self.net, self.net.nc
        nc.scalar.wait_ge(self.u_ready, turn + 1)
        nc.scalar.activation(net.euk[:], net.euk[:], ACT.Exp).then_inc(self.euk_ready, 1)
        nc.scalar.activation(net.f_pair[:], net.f[:, ds(pair * UNIT, UNIT)], ACT.Copy) \
            .then_inc(self.f_copied, 1)

    def vector(self, link, pair, turn):
        net, nc, c = self.net, self.net.nc, self.c
        v = nc.vector
        n = BB * SEG

        def columns(k):
            return slice(k * n, (k + 1) * n), ds(pair * UNIT + k * n, n)

        done = [None] * KT

        def on(k, op):
            done[k] = link.mark(op)

        def after(k):
            if done[k] is not None:
                v.wait_ge(*done[k])

        def add_u(k):
            here, both = columns(k)
            op = v.tensor_scalar(net.euk[:, here], net.f[:, both],
                                 net.pp[:, PP_U + c * KT + k:PP_U + c * KT + k + 1], 30.0,
                                 ALU.add, ALU.min)
            if k == KT - 1:
                op.then_inc(self.u_ready, 1)

        def scan(out, x, operands, reverse=False):
            def step(k):
                here, both = columns(k)
                v.wait_ge(self.operand_ready, 4 * turn + operands)
                data = x[:, both if x is net.e else here]
                order = slice(None, None, -1) if reverse else slice(None)
                op = v.tensor_tensor_scan(out[:, here][:, order], net.decay[:, here][:, order],
                                          data[:, order] if reverse else data, 0.0, ALU.mult,
                                          ALU.add)
                if out is net.den_b and k == KT - 1:
                    op.then_inc(self.scans_done, 1)
                    done[k] = self.scans_done, turn + 1
                else:
                    on(k, op)
            return step

        def combine(a, b):
            def step(k):
                here, _ = columns(k)
                after(k)
                on(k, v.tensor_tensor(a[:, here], a[:, here], b[:, here], ALU.add))
            return step

        def add_own(a, b, ready):
            def step(k):
                v.wait_ge(self.own_ready, 2 * turn + ready)
                combine(a, b)(k)
            return step

        def bound(k):
            here, _ = columns(k)
            after(k)
            on(k, v.tensor_scalar(net.den[:, here], net.den[:, here], 1e-8, None, ALU.max))

        def invert(part):
            cols = slice(part * UNIT // INVERT_PARTS, (part + 1) * UNIT // INVERT_PARTS)
            if part % (INVERT_PARTS // KT) == 0:
                after(part * KT // INVERT_PARTS)
            op = v.reciprocal(net.den[:, cols], net.den[:, cols])
            if part == INVERT_PARTS - 1:
                link(op)

        def factor(b):
            shape = dict(k=KT, b=BB)
            num = net.num[:].rearrange("p (k b t) -> p k b t", **shape)[:, :, b, 1:SEG]
            den = net.den[:].rearrange("p (k b t) -> p k b t", **shape)[:, :, b, 1:SEG]
            m = net.m[:, ds(pair * PAIR, PAIR)].rearrange("p (k b t) -> p k b t", **shape)
            op = v.scalar_tensor_tensor(m[:, :, b, :], num, net.scol[:, ds(pair * BB + b, 1)],
                                        den, ALU.mult, ALU.mult)
            if b == BB - 1:
                op.then_inc(self.factor_made, 1)
                v.wait_ge(self.factor_made, turn + 1)

        stages = [
            add_u,
            scan(net.den, net.e, 2), scan(net.num, net.ev_pair, 3),
            scan(net.num_b, net.ev_pair, 3, True), scan(net.den_b, net.e_pair, 4, True),
            combine(net.num, net.num_b), combine(net.den, net.den_b),
            add_own(net.den, net.euk, 1), add_own(net.num, net.ev_pair, 2), bound,
        ]
        return [partial(stage, k) for stage in stages for k in range(KT)] \
            + [partial(invert, part) for part in range(INVERT_PARTS)] \
            + [partial(factor, b) for b in range(BB)]


def take(steps, share):
    for step in steps[:share]:
        step()
    del steps[:share]


def stage_condition(net):
    nc, dram = net.nc, net.dram
    sem = net.sem
    e0_exp, e_padded = sem("e0_exp"), sem("e_padded")
    min_ready = sem("min_ready")
    tf_sum, tf_tanh, w_exp = sem("tf_sum"), sem("tf_tanh"), sem("w_exp")
    cols_ready = sem("cols_ready")
    pads_ready, links = sem("pads_ready"), sem("cond_links")
    net.cond_sems = [sem(n) for n in ("u_ready", "euk_ready", "operand_ready", "scans_done",
                                         "own_ready", "factor_made", "f_copied")]
    unit = CondUnit(net, 0, net.cond_sems)
    tanh_h, make_h, _ = condition_input(net, "_mixer")

    with nc.Block() as block:
        @block.sync
        def _(sp):
            sp.dma_start(net.pp[:], dram["pp"]).then_inc(net.params_loaded, 16)
            for p in range(PAIRS):
                rows = net.f[:, p * UNIT:(p + 1) * UNIT].rearrange("p (r t) -> p r t", t=SEG)
                src = dram["f"][:, p * PAIR:(p + 1) * PAIR].rearrange("p (r t) -> p r t", t=SEQ)
                sp.dma_start(rows[:, :, 1:SEG], src).then_inc(net.f_loaded[p], 16)
            sp.dma_start(net.x[:], dram["x"]).then_inc(net.x_loaded, 16)
            sp.dma_start(net.cb[:], dram["cb"][:, 0:CB_SEL]).then_inc(net.consts_loaded, 16)
            sp.dma_start(net.ident[:], dram["ident"]).then_inc(net.consts_loaded, 16)
            for n, (a, b) in enumerate(net.win_chunks):
                sp.dma_start(net.weights[:, a:b], dram["w_mixer"][:, a:b]).then_inc(
                    net.win_loaded[n], 16)

        @block.gpsimd
        def _(pool):
            nc.gpsimd.memset(net.ones[:], 1.0).then_inc(net.consts_made, 1)
            pool.wait_ge(net.consts_made, 1)
            nc.gpsimd.memset(net.f[:].rearrange("p (r t) -> p r t", t=SEG)[:, :, 0:1], 0.0) \
                .then_inc(pads_ready, 1)
            nc.gpsimd.memset(net.decay[:].rearrange("p (r t) -> p r t", t=SEG)[:, :, 0:1], 0.0) \
                .then_inc(pads_ready, 1)
            pool.wait_ge(cols_ready, 3)
            for pair in range(PAIRS):
                pool.wait_ge(e_padded, pair + 1)
                unit.pool_operands(pair, pair)
                unit.pool_own(pair)
                unit.pool_own_f(pair)

        @block.scalar
        def _(act):
            act.wait_ge(net.params_loaded, 16)
            w = net.pp[:, PP_W:PP_W + 4 * KT]
            nc.scalar.activation(w, w, ACT.Exp).then_inc(w_exp, 1)
            act.wait_ge(w_exp, 1)
            nc.scalar.activation(w, w, ACT.Exp, scale=-1.0).then_inc(w_exp, 1)
            act.wait_ge(tf_sum, 1)
            nc.scalar.activation(net.tf[:, 0:BATCH], net.tf[:, 0:BATCH], ACT.Tanh, scale=0.5) \
                .then_inc(tf_tanh, 1)
            for pair in range(PAIRS):
                e = net.e[:, pair * UNIT:(pair + 1) * UNIT]
                act.wait_ge(min_ready, pair + 1)
                nc.scalar.activation(e, e, ACT.Exp).then_inc(e0_exp, 1)
            unit.scalar(0, 0)
            tanh_h()
            unit.scalar(1, 1)

        @block.vector
        def _(dve):
            v = nc.vector
            link = Links(dve, links)
            dve.wait_ge(net.params_loaded, 16)
            cond = net.pp[:, PP_COND:PP_COND + BATCH * 64].rearrange("p (b c) -> p b c", b=BATCH)
            v.tensor_reduce(net.tf[:, 0:BATCH], cond, AX_X, ALU.add).then_inc(tf_sum, 1)
            dve.wait_ge(tf_tanh, 1)
            v.tensor_scalar(net.tf[:, BATCH:2 * BATCH], net.tf[:, 0:BATCH], 0.25, 0.75, ALU.mult,
                            ALU.add).then_inc(cols_ready, 1)
            v.tensor_scalar(net.scol[:], net.tf[:, 0:BATCH], 0.05, 0.45, ALU.mult,
                            ALU.add).then_inc(cols_ready, 1)
            dve.wait_ge(w_exp, 2)
            dve.wait_ge(cols_ready, 2)
            v.tensor_tensor(
                net.dcol[:].rearrange("p (c b) -> p c b", b=BATCH),
                net.pp[:, PP_W:PP_W + 4 * KT][:, :, None].to_broadcast([P, 4 * KT, BATCH]),
                net.tf[:, BATCH:2 * BATCH][:, None, :].to_broadcast([P, 4 * KT, BATCH]),
                ALU.mult).then_inc(cols_ready, 1)
            dve.wait_ge(pads_ready, 2)
            for pair in range(PAIRS):
                unit_cols = slice(pair * UNIT, (pair + 1) * UNIT)
                dve.wait_ge(net.f_loaded[pair], 16)
                v.tensor_scalar(net.e[:, unit_cols], net.f[:, unit_cols], 30.0, None, ALU.min) \
                    .then_inc(min_ready, 1)
            for pair in range(PAIRS):
                e = net.e[:, pair * UNIT:(pair + 1) * UNIT].rearrange("p (r t) -> p r t", t=SEG)
                dve.wait_ge(e0_exp, pair + 1)
                v.memset(e[:, :, 0:1], 0.0).then_inc(e_padded, 1)
            dve.wait_ge(e_padded, PAIRS)
            for pair in range(PAIRS):
                for step in unit.vector(link, pair, pair):
                    step()
                make_h(pair)


def condition_input(net, tag):
    nc = net.nc
    half_tanh, h_ready = net.sem(f"half_tanh{tag}"), net.sem(f"h_ready{tag}")

    def scalar():
        nc.scalar.wait_ge(net.x_loaded, 16)
        for pair in range(PAIRS):
            s = slice(pair * PAIR, (pair + 1) * PAIR)
            nc.scalar.activation(net.h[:, s], net.x[:, s], ACT.Tanh, scale=0.5) \
                .then_inc(half_tanh, 1)

    def vector(*pairs):
        nc.vector.wait_ge(net.x_loaded, 16)
        for pair in pairs or range(PAIRS):
            s = slice(pair * PAIR, (pair + 1) * PAIR)
            nc.vector.wait_ge(half_tanh, pair + 1)
            nc.vector.scalar_tensor_tensor(net.h[:, s], net.h[:, s], 1.0, net.m[:, s], ALU.add,
                                           ALU.mult).then_inc(h_ready, 1)

    return scalar, vector, h_ready



LAG_HEADS, LAG_Y, LAG_OUT = 2, 3, 4
MIXER_LINKS = CondUnit.VECTOR_LINKS + 45


def stage_mixer(net):
    nc = net.nc
    N = XT_TILES
    STEPS = N + LAG_OUT
    net.next_stage()
    with ExitStack() as mem:
        def sb(name, shape, dt=F32):
            return mem.enter_context(nc.sbuf_tensor(name, shape, dt))

        def ps(name):
            return mem.enter_context(nc.psum_tensor(name, [P, 512], F32))

        def sem(name):
            return net.stage_sem(mem, name)

        w = net.weights
        sel = sb("sel", [3 * HEADS, HEADS * P], BF16)
        conv = sb("conv", [P, 2, TOK])
        tanh_x = sb("tanh_x", [P, 2, TOK])
        tanh_g = sb("tanh_g", [P, TOK])
        bc = sb("bc", [P, 2, TOK])
        xs = sb("xs", [P, 4, TOK])
        gate = sb("gate", [P, 4, TOK])
        x_tok = sb("x_tok", [P, 3, BB * ST, P])
        scores = sb("scores", [P, BB, TRI])
        decays = sb("decays", [P, 4, BB, TRI])
        y = sb("y", [P, TOK])
        g = sb("g", [P, 2, TOK])
        square = sb("square", [P, TOK])
        square_sum = sb("square_sum", [P, TOK])
        parts = sb("parts", [3 * HEADS, TOK], BF16)
        part = sb("part", [HEADS, TOK], BF16)
        neg_cum = sb("neg_cum", [P, BB * ST * HEADS])
        dt_tok = sb("dt_tok", [P, BB * ST * HEADS])
        z, soft, dt, cum = (gate[0:HEADS, n, :] for n in range(4))
        rest = y[0:HEADS, :]
        ones_row = net.ones[0:HEADS, 0:1].to_broadcast([HEADS, SEQ])
        root = y

        px, pg, py, pt = ps("px"), ps("pg"), ps("py"), ps("pt")
        pcum = [ps(f"pcum{n}") for n in range(ST)]
        pout = [ps(f"pout{n}") for n in range(KT)]

        sel_loaded = sem("sel_loaded")
        norm_folded, alog_exp, d_halved = sem("norm_folded"), sem("alog_exp"), sem("d_halved")
        px_ready, px_free = sem("px_ready"), sem("px_free")
        pg_ready, pg_free = sem("pg_ready"), sem("pg_free")
        conv_begun, tanh_x_ready, xs_ready = sem("conv_begun"), sem("tanh_x_ready"), sem("xs_ready")
        soft_in, soft_exp, soft_ready = sem("soft_in"), sem("soft_exp"), sem("soft_ready")
        cum_ready, parts_ready = sem("cum_ready"), sem("parts_ready")
        pt_ready, pt_free = sem("pt_ready"), sem("pt_free")
        pcum_ready = [sem(f"pcum_ready{n}") for n in range(ST)]
        pcum_free = [sem(f"pcum_free{n}") for n in range(ST)]
        row_cols_ready = sem("row_cols_ready")
        tanh_g_ready, gate_ready = sem("tanh_g_ready"), sem("gate_ready")
        decay_scaled = sem("decay_scaled")
        y_ready, y_free, g_ready = sem("y_ready"), sem("y_free"), sem("g_ready")
        square_ready, square_used = sem("square_ready"), sem("square_used")
        out_used, out_ready, out_free = sem("out_used"), sem("out_ready"), sem("out_free")
        root_ready = sem("root_ready")
        links = sem("mixer_links")
        unit = CondUnit(net, 1, net.cond_sems)

        def conv_w(n, k):
            return net.pp[:, PP_CONVW + n * TAPS + k:PP_CONVW + n * TAPS + k + 1]

        def chunk_of(col):
            return next(n for n, (a, b) in enumerate(net.win_chunks) if a <= col < b)

        block = mem.enter_context(nc.Block())

        @block.sync
        def _(sp):
            sp.dma_start(sel[:], net.dram["cb"][0:3 * HEADS, CB_SEL:CB_SEL + HEADS * P]) \
                .then_inc(sel_loaded, 16)
            sp.wait_ge(px_ready, PAIRS * (N + 2))
            sp.wait_ge(pg_ready, PAIRS * (N + 1))
            for dst, src, done in net.moe0_early:
                sp.dma_start(dst, src).then_inc(done, 16)

        @block.tensor
        def _(pe):
            def project(out, m, col, i, free, ready, count):
                pe.wait_ge(net.win_loaded[chunk_of(col)], 16)
                if count is not None:
                    pe.wait_ge(free, count)
                for k in range(KT):
                    op = nc.tensor.matmul(out[0:m, :], w[:, col + k * m:col + (k + 1) * m],
                                          net.h[:, ds(i * PAIR + k * TOK, TOK)],
                                          start=(k == 0), stop=(k == KT - 1))
                op.then_inc(ready, 1)

            def x_like(i, n):
                col = W_BCXG + (n if n < 2 else 2 + 2 * (n - 2)) * KT * P
                project(px, P, col, i, px_free, px_ready, i * (N + 2) + n)

            def gate_like(i, s):
                m, col = (HEADS, W_DT) if s < 0 else (P, W_BCXG + (3 + 2 * s) * KT * P)
                project(pg, m, col, i, pg_free, pg_ready, i * (N + 1) + s + 1)

            def turn_cum(i):
                for n, src in enumerate((cum, dt)):
                    for r in range(BB * ST):
                        at = (n * BB * ST + r) * HEADS
                        op = nc.tensor.transpose(pt[:, at:at + HEADS], src[:, r * P:(r + 1) * P],
                                                 net.ident[0:HEADS, 0:HEADS])
                op.then_inc(pt_ready, 1)

            def key_query(i):
                pe.wait_ge(cum_ready, i + 1)
                pe.wait_ge(pt_free, i * (N + 2))
                pe.wait_ge(xs_ready, i * (N + 2) + 2)
                for b in range(BB):
                    pe.wait_ge(pcum_free[b], i * (HEADS + 1))
                    at = b * SEQ
                    nc.tensor.matmul(pcum[b][:, 0:SEQ], bc[:, 0, at:at + P],
                                     bc[:, 1, at:at + SEQ], start=True, stop=True)
                    nc.tensor.matmul(pcum[b][:, SEQ:TRI], bc[:, 0, at + P:at + SEQ],
                                     bc[:, 1, at + P:at + SEQ], start=True, stop=True) \
                        .then_inc(pcum_ready[b], 1)

            def spread_cum(i, head):
                pe.wait_ge(parts_ready, i + 1)
                for r in range(ST):
                    pe.wait_ge(pcum_free[r], i * (HEADS + 1) + head + 1)
                    rows = parts[:].rearrange("p (b t) -> p b t", b=BB)[:, :, r * P:SEQ]
                    out = pcum[r][:, 0:BB * (SEQ - r * P)].rearrange("p (b t) -> p b t", b=BB)
                    nc.tensor.matmul(out, sel[:, head * P:(head + 1) * P], rows, start=True,
                                     stop=False)
                    nc.tensor.matmul(out[:, :, 0:P], net.cb[:, CB_IDENT:CB_IDENT + P],
                                     net.cb[:, CB_MASK_ST:CB_MASK_ST + P][:, None, :]
                                     .to_broadcast([P, BB, P]), start=False, stop=True) \
                        .then_inc(pcum_ready[r], 1)

            def turn_x(i, s):
                pe.wait_ge(xs_ready, i * (N + 2) + s + 3)
                pe.wait_ge(pt_free, i * (N + 2) + s + 1)
                for r in range(BB * ST):
                    op = nc.tensor.transpose(pt[:, r * P:(r + 1) * P],
                                             xs[:, s % 4, r * P:(r + 1) * P], net.ident[:])
                op.then_inc(pt_ready, 1)

            def mix(i, s):
                pe.wait_ge(pt_free, i * (N + 2) + s + 2)
                pe.wait_ge(y_free, i * N + s)
                for hh in range(TILE_HEADS):
                    head = s * TILE_HEADS + hh
                    pe.wait_ge(decay_scaled, i * HEADS + head + 1)
                    rows = slice(hh * HEAD, (hh + 1) * HEAD)
                    for b in range(BB):
                        for r in range(ST):
                            cols = slice(0, SEQ) if r == 0 else slice(SEQ, TRI)
                            op = nc.tensor.matmul(
                                py[rows, b * SEQ + r * P:(b + 1) * SEQ],
                                x_tok[:, s % 3, b * ST + r, rows],
                                decays[:, head % 4, b, cols], start=(r == 0), stop=(r == ST - 1))
                op.then_inc(y_ready, 1)

            def project_out(i, s):
                pe.wait_ge(g_ready, i * N + s + 1)
                if s == 0:
                    pe.wait_ge(norm_folded, N)
                    pe.wait_ge(out_free, i)
                for k in range(KT):
                    at = W_OUT0 + s * D + k * P
                    op = nc.tensor.matmul(pout[k][:], w[:, at:at + P], g[:, s % 2, :],
                                          start=(s == 0), stop=(s == N - 1))
                op.then_inc(out_used, 1)

            pe.wait_ge(sel_loaded, 16)
            pe.wait_ge(net.consts_loaded, 32)
            with nc.tensor.Fori(0, PAIRS) as i:
                gate_like(i, -1)
                x_like(i, 0)
                x_like(i, 1)
                for s in range(STEPS):
                    if s < N:
                        x_like(i, s + 2)
                    if s == 1:
                        key_query(i)
                        turn_cum(i)
                    if 0 <= s - LAG_HEADS < N:
                        spread_cum(i, 2 * (s - LAG_HEADS))
                    if s < N:
                        gate_like(i, s)
                    if 0 <= s - LAG_HEADS < N:
                        spread_cum(i, 2 * (s - LAG_HEADS) + 1)
                    if 0 <= s - 1 < N:
                        turn_x(i, s - 1)
                    if 0 <= s - LAG_OUT < N:
                        project_out(i, s - LAG_OUT)
                    if 0 <= s - LAG_Y < N:
                        mix(i, s - LAG_Y)
                pe.wait_ge(square_used, (i + 1) * N)
                pe.wait_ge(pt_free, i * (N + 2) + N + 1)
                nc.tensor.matmul(pt[:], net.ones[:], square_sum[:], start=True, stop=True) \
                    .then_inc(pt_ready, 1)

        @block.scalar
        def _(act):
            col = net.pp[0:HEADS, PP_ALOG:PP_ALOG + 1]
            nc.scalar.activation(col, col, ACT.Exp).then_inc(alog_exp, 1)

            def begin_conv(i, n):
                act.wait_ge(px_ready, i * (N + 2) + n + 1)
                act.wait_ge(xs_ready, i * (N + 2) + max(n - 1, 0))
                nc.scalar.activation(conv[:, n % 2, :], px[:], ACT.Identity,
                                     bias=net.pp[:, PP_CONVB + n:PP_CONVB + n + 1],
                                     scale=conv_w(n, TAPS - 1)).then_inc(conv_begun, 1)

            def tanh_conv(i, n):
                act.wait_ge(px_free, i * (N + 2) + n + 1)
                nc.scalar.activation(tanh_x[:, n % 2, :], conv[:, n % 2, :], ACT.Tanh, scale=0.5) \
                    .then_inc(tanh_x_ready, 1)

            def tanh_gate(i, s):
                act.wait_ge(pg_ready, i * (N + 1) + s + 2)
                act.wait_ge(gate_ready, i * N + s)
                if s >= 4:
                    act.wait_ge(g_ready, i * N + s - 3)
                elif s == 0:
                    act.wait_ge(parts_ready, i + 1)
                else:
                    act.wait_ge(pt_ready, i * (N + 2) + 1)
                nc.scalar.activation(tanh_g[:], pg[:], ACT.Tanh, scale=0.5) \
                    .then_inc(tanh_g_ready, 1)
                nc.scalar.activation(gate[:, s % 4, :], pg[:], ACT.Copy).then_inc(pg_free, 1)

            def exp_decay(i, head):
                if head >= 4:
                    act.wait_ge(y_ready, i * N + (head - 4) // 2 + 1)
                for r in range(ST):
                    act.wait_ge(pcum_ready[r], i * (HEADS + 1) + head + 2)
                    for b in range(BB):
                        n = SEQ - r * P
                        at = (b * ST + r) * HEADS + head
                        op = nc.scalar.activation(
                            decays[:, head % 4, b, r * SEQ:r * SEQ + n],
                            pcum[r][:, b * n:(b + 1) * n], ACT.Exp, bias=neg_cum[:, at:at + 1])
                    op.then_inc(pcum_free[r], 1)

            def square_g(i, s):
                act.wait_ge(g_ready, i * N + s + 1)
                act.wait_ge(square_used, i * N + s)
                nc.scalar.activation(square[:], g[:, s % 2, :], ACT.Square) \
                    .then_inc(square_ready, 1)

            with nc.scalar.Fori(0, PAIRS) as i:
                begin_conv(i, 0)
                nc.scalar.preload_act_table_set("natural_log_exp_and_others")
                act.wait_ge(soft_in, i + 1)
                nc.scalar.activation(soft, soft, ACT.Exp, scale=-1.0).then_inc(soft_exp, 1)
                act.wait_ge(soft_exp, i + 1)
                nc.scalar.activation(soft, soft, ACT.Ln, bias=1.0).then_inc(soft_ready, 1)
                begin_conv(i, 1)
                tanh_conv(i, 0)
                tanh_conv(i, 1)
                for s in range(STEPS):
                    if s < N:
                        begin_conv(i, s + 2)
                    if s == LAG_HEADS:
                        act.wait_ge(row_cols_ready, i + 1)
                    if 0 <= s - LAG_HEADS < N:
                        exp_decay(i, 2 * (s - LAG_HEADS))
                    if s < N:
                        tanh_conv(i, s + 2)
                        tanh_gate(i, s)
                    if 0 <= s - LAG_HEADS < N:
                        exp_decay(i, 2 * (s - LAG_HEADS) + 1)
                    if 0 <= s - LAG_OUT < N:
                        square_g(i, s - LAG_OUT)
                    if s == 3:
                        unit.scalar(i, i + PAIRS)
                nc.scalar.preload_act_table_set("natural_log_exp_and_others")
                act.wait_ge(pt_ready, (i + 1) * (N + 2))
                nc.scalar.activation(root[:], pt[:], ACT.Ln, scale=0.25 / INNER,
                                     bias=net.pp[:, PP_EPS_MIXER:PP_EPS_MIXER + 1]) \
                    .then_inc(pt_free, 1)
                act.wait_ge(pt_free, (i + 1) * (N + 2))
                nc.scalar.activation(root[:], root[:], ACT.Exp, scale=-0.5,
                                     bias=net.pp[:, PP_LN_HALF:PP_LN_HALF + 1]) \
                    .then_inc(root_ready, 1)

            nc.scalar.preload_act_table_set("exp_and_others")

        @block.gpsimd
        def _(pool):
            net.clear_last_stage(pool)
            pool.wait_ge(net.win_loaded[chunk_of(W_OUT0)], 16)
            for s in range(N):
                rows = w[:, W_OUT0 + s * D:W_OUT0 + (s + 1) * D]
                nc.gpsimd.tensor_scalar(rows, rows, net.pp[:, PP_NORM + s:PP_NORM + s + 1], None,
                                        ALU.mult).then_inc(norm_folded, 1)

            def scale_decay(i, head):
                pool.wait_ge(pcum_free[ST - 1], i * (HEADS + 1) + head + 2)
                nc.gpsimd.tensor_tensor(decays[:, head % 4], decays[:, head % 4], scores[:],
                                        ALU.mult).then_inc(decay_scaled, 1)

            def add_square(i, s):
                pool.wait_ge(square_ready, i * N + s + 1)
                if s == 0:
                    pool.wait_ge(pt_ready, i * (N + 2))
                    op = nc.gpsimd.tensor_tensor(square_sum[:], square[:],
                                                 net.ones[:, 0:1].to_broadcast([P, TOK]), ALU.mult)
                else:
                    pool.wait_ge(square_used, i * N + s)
                    op = nc.gpsimd.tensor_tensor(square_sum[:], square_sum[:], square[:], ALU.add)
                op.then_inc(square_used, 1)

            with nc.gpsimd.Fori(0, PAIRS) as i:
                unit.pool_operands(i, i + PAIRS)
                for b in range(BB):
                    pool.wait_ge(pcum_free[b], i * (HEADS + 1) + 1)
                for s in range(LAG_HEADS, STEPS):
                    for hh in range(TILE_HEADS):
                        if s - LAG_HEADS < N:
                            scale_decay(i, TILE_HEADS * (s - LAG_HEADS) + hh)
                    if s >= LAG_OUT:
                        add_square(i, s - LAG_OUT)
                    if s == 5:
                        unit.pool_own(i + PAIRS)
                    if s == 8:
                        unit.pool_own_f(i + PAIRS)

        @block.vector
        def _(dve):
            v = nc.vector
            half_d = net.pp[:, PP_D:PP_D + N]
            v.tensor_scalar(half_d, half_d, 0.5, None, ALU.mult).then_inc(d_halved, 1)
            dve.wait_ge(d_halved, 1)
            dve.wait_ge(alog_exp, 1)

            def softplus_cum(i, link):
                dve.wait_ge(pg_ready, i * (N + 1) + 1)
                dve.wait_ge(y_ready, i * N)
                v.tensor_scalar(z, pg[0:HEADS, :], net.pp[0:HEADS, PP_DTB:PP_DTB + 1], None,
                                ALU.add).then_inc(pg_free, 1)
                dve.wait_ge(pg_free, i * (N + 1) + 1)
                v.scalar_tensor_tensor(soft, z, -1.0, z, ALU.mult, ALU.max).then_inc(soft_in, 1)

            def cum_parts(i, link):
                dve.wait_ge(soft_ready, i + 1)
                link(v.scalar_tensor_tensor(dt, z, 0.0, soft, ALU.max, ALU.add))
                link(v.tensor_scalar(z, dt, net.pp[0:HEADS, PP_ALOG:PP_ALOG + 1], -1.0, ALU.mult,
                                     ALU.mult))
                for b in range(BB):
                    s = slice(b * SEQ, (b + 1) * SEQ)
                    link(v.tensor_tensor_scan(cum[:, s], ones_row, z[:, s], 0.0, ALU.mult,
                                              ALU.add))
                v.tensor_copy(parts[0:HEADS, :], cum).then_inc(cum_ready, 1)
                dve.wait_ge(cum_ready, i + 1)
                link(v.tensor_tensor(rest, cum, parts[0:HEADS, :], ALU.subtract))
                link(v.tensor_copy(part[:], rest))
                v.tensor_copy(parts[HEADS:2 * HEADS, :], part[:])
                link(v.tensor_tensor(rest, rest, part[:], ALU.subtract))
                v.tensor_copy(parts[2 * HEADS:3 * HEADS, :], rest).then_inc(parts_ready, 1)

            def taps(i, n, link):
                dve.wait_ge(conv_begun, i * (N + 2) + n + 1)
                for k in range(1, TAPS):
                    out = conv[:, n % 2, :].rearrange("p (b t) -> p b t", b=BB)[:, :, k:SEQ]
                    src = px[:].rearrange("p (b t) -> p b t", b=BB)[:, :, 0:SEQ - k]
                    op = v.scalar_tensor_tensor(out, src, conv_w(n, TAPS - 1 - k), out, ALU.mult,
                                                ALU.add)
                    if k < TAPS - 1:
                        link(op)
                op.then_inc(px_free, 1)

            def silu_x(i, n):
                dve.wait_ge(tanh_x_ready, i * (N + 2) + n + 1)
                out = bc[:, n, :] if n < 2 else xs[:, (n - 2) % 4, :]
                v.scalar_tensor_tensor(out, tanh_x[:, n % 2, :], 1.0, conv[:, n % 2, :], ALU.add,
                                       ALU.mult).then_inc(xs_ready, 1)

            def silu_gate(i, s):
                dve.wait_ge(tanh_g_ready, i * N + s + 1)
                dve.wait_ge(pg_free, i * (N + 1) + s + 2)
                v.scalar_tensor_tensor(gate[:, s % 4, :], tanh_g[:], 1.0, gate[:, s % 4, :],
                                       ALU.add, ALU.mult).then_inc(gate_ready, 1)

            def row_cols(i):
                dve.wait_ge(pt_ready, i * (N + 2) + 1)
                n = BB * ST * HEADS
                v.tensor_scalar(neg_cum[:], pt[:, 0:n], -1.0, None, ALU.mult) \
                    .then_inc(row_cols_ready, 1)
                v.tensor_scalar(dt_tok[:], pt[:, n:2 * n], 0.5, None, ALU.mult) \
                    .then_inc(pt_free, 1)
                for b in range(BB):
                    dve.wait_ge(pcum_ready[b], i * (HEADS + 1) + 1)
                    v.tensor_scalar(scores[:, b, :], pcum[b][:, 0:TRI], 0.25, None, ALU.mult) \
                        .then_inc(pcum_free[b], 1)

            def take_x(i, s):
                dve.wait_ge(pt_ready, i * (N + 2) + s + 2)
                if s == 0:
                    dve.wait_ge(pt_free, i * (N + 2) + 1)
                if s >= 3:
                    dve.wait_ge(y_ready, i * N + s - 2)
                heads = dt_tok[:].rearrange("p (r h) -> p r h", h=HEADS)[
                    :, :, s * TILE_HEADS:(s + 1) * TILE_HEADS]
                v.tensor_tensor(
                    x_tok[:, s % 3].rearrange("p r (h d) -> p r h d", h=TILE_HEADS),
                    pt[:].rearrange("p (r h d) -> p r h d", r=BB * ST, h=TILE_HEADS),
                    heads[:, :, :, None].to_broadcast([P, BB * ST, TILE_HEADS, HEAD]),
                    ALU.mult).then_inc(pt_free, 1)

            def gated(i, s, link):
                dve.wait_ge(y_ready, i * N + s + 1)
                v.scalar_tensor_tensor(y[:], xs[:, s % 4, :], net.pp[:, PP_D + s:PP_D + s + 1],
                                       py[:], ALU.mult, ALU.add).then_inc(y_free, 1)
                dve.wait_ge(y_free, i * N + s + 1)
                dve.wait_ge(out_used, i * N + max(s - 1, 0))
                dve.wait_ge(square_ready, i * N + max(s - 1, 0))
                dve.wait_ge(gate_ready, i * N + s + 1)
                v.tensor_tensor(g[:, s % 2, :], y[:], gate[:, s % 4, :], ALU.mult) \
                    .then_inc(g_ready, 1)

            def add_to_x(i, link):
                dve.wait_ge(root_ready, i + 1)
                dve.wait_ge(out_used, (i + 1) * N)
                for k in range(KT):
                    out = net.x[:, ds(i * PAIR + k * TOK, TOK)]
                    link(v.tensor_tensor(g[:, k, :], pout[k][:], root[:], ALU.mult))
                    op = v.tensor_tensor(out, out, g[:, k, :], ALU.add)
                op.then_inc(out_free, 1)

            with nc.vector.Fori(0, PAIRS) as i:
                link = Links(dve, links, i, MIXER_LINKS)
                cond = unit.vector(link, i, i + PAIRS)
                taps(i, 0, link)
                softplus_cum(i, link)
                taps(i, 1, link)
                silu_x(i, 0)
                cum_parts(i, link)
                silu_x(i, 1)
                for s in range(STEPS):
                    if s < N:
                        taps(i, s + 2, link)
                    if s == 1:
                        row_cols(i)
                    if 0 <= s - LAG_Y < N:
                        gated(i, s - LAG_Y, link)
                    if s < N:
                        silu_x(i, s + 2)
                    if 0 <= s - 1 < N:
                        take_x(i, s - 1)
                    if s < N:
                        silu_gate(i, s)
                    if s >= 2:
                        take(cond, 2)
                assert not cond
                add_to_x(i, link)
                link.check()



class Experts:

    def __init__(self, tag, experts, top, shared, tiles, gate_product, gate_at):
        self.tag, self.experts, self.top = tag, experts, top
        self.shared, self.tiles, self.gate_product = shared, tiles, gate_product
        self.gate_at = gate_at
        self.part_rows = 32


MOE0 = Experts("0", E0, K0, SHARED_TILES, MOE0_TILES, True, PP_GATE0)
MOE1 = Experts("1", E1, K1, 0, MOE1_TILES, False, PP_GATE1)
TOK_TILES = BATCH * SEQ // P


def stage_moe(net, cfg, weights, prepare, cond, later=(0, ())):
    nc = net.nc
    E, N, S = cfg.experts, cfg.tiles, cfg.shared
    PR = cfg.part_rows
    R = 3 * PR
    per = (0 if cfg.gate_product else N) + (CondUnit.VECTOR_LINKS if cond is not None else 0)
    net.next_stage()
    with ExitStack() as mem:
        def sb(name, shape, dt=F32):
            return mem.enter_context(nc.sbuf_tensor(name + cfg.tag, shape, dt))

        def sem(name):
            return net.stage_sem(mem, name + cfg.tag)

        def ps(name):
            return mem.enter_context(nc.psum_tensor(name + cfg.tag, [P, 512], F32))

        weight_tile, w_loaded, loads = weights(sb)
        sel = sb("expert_sel", [R, (N - S) * P], BF16)
        gate_wt = net.pp[:, cfg.gate_at:cfg.gate_at + KT * E]
        score = sb("score", [P, TOK_TILES, E])
        pick = sb("pick", [P, 3, TOK_TILES, E])
        seg = sb("seg", [P, TOK_TILES, E])
        top8 = sb("top8", [P, TOK_TILES, 8])
        col = sb("col", [P, 2, TOK_TILES])
        route = sb("route", [E, PAIRS * TOK])
        part = sb("route_part", [E, PAIRS * TOK], BF16)
        parts = sb("route_parts", [R, PAIRS * TOK], BF16)
        up = sb("up", [P, 2, TOK])
        mid = sb("mid", [P, 2, TOK])
        act_out = sb("act_out", [P, 2, TOK])
        hidden = sb("hidden", [P, 2, TOK])

        ph1 = [ps(f"ph1_{n}_") for n in range(2)]
        ph3 = [ps(f"ph3_{n}_") for n in range(2)]
        pw = [ps(f"pw_{n}_") for n in range(2)]
        pout = [ps(f"pmoe_{n}_") for n in range(KT)]
        plogit, proute = pout[0], pw

        sel_loaded = sem("sel_loaded")
        logit_ready, score_ready = sem("logit_ready"), sem("score_ready")
        exp_ready, exp_in = sem("exp_ready"), sem("exp_in")
        route_cols_ready, route_turned = sem("route_cols_ready"), sem("route_turned")
        parts_ready = sem("route_parts_ready")
        h_up_ready, w_ready = sem("h_up_ready"), sem("w_ready")
        up_copied, mid_ready = sem("up_copied"), sem("mid_ready")
        act_ready, hidden_ready = sem("act_ready"), sem("hidden_ready")
        down_done, x_added = sem("down_done"), sem("x_added")
        zeroed, links, route_links = sem("zeroed"), sem("moe_links"), sem("route_links")
        unit = CondUnit(net, cond, net.cond_sems) if cond is not None else None
        turn0 = PAIRS * cond if cond is not None else 0
        tanh_h, make_h, h_ready = prepare or (lambda: None, lambda: None, None)
        routed = N - S

        block = mem.enter_context(nc.Block())

        @block.sync
        def _(sp):
            tag = cfg.tag
            sp.dma_start(sel[:], net.dram[f"sel{tag}"]).then_inc(sel_loaded, 16)
            for dst, src, done in loads:
                sp.dma_start(dst, src).then_inc(done, 16)
            tiles_used, later_loads = later
            for dst, src, done in later_loads:
                sp.wait_ge(down_done, (PAIRS - 1) * N + tiles_used)
                sp.dma_start(dst, src).then_inc(done, 16)

        @block.tensor
        def _(pe):
            pe.wait_ge(net.params_loaded, 16)
            for n in range(TOK_TILES):
                pair, at = n // (BB * ST), n % (BB * ST) * P
                if h_ready:
                    pe.wait_ge(h_ready, pair + 1)
                for k in range(KT):
                    op = nc.tensor.matmul(plogit[:, n * E:(n + 1) * E],
                                          net.h[:, pair * PAIR + k * TOK + at:][:, 0:P],
                                          gate_wt[:, k * E:(k + 1) * E], start=(k == 0),
                                          stop=(k == KT - 1))
            op.then_inc(logit_ready, 1)
            pe.wait_ge(route_cols_ready, 1)
            for n in range(TOK_TILES):
                op = nc.tensor.transpose(proute[n // 4][0:E, n % 4 * P:(n % 4 + 1) * P],
                                         pick[:, 0, n, :], net.ident[:])
            op.then_inc(route_turned, 1)

            def up_project(i, m):
                pe.wait_ge(w_loaded(m), 16)
                pe.wait_ge(hidden_ready, i * N + max(m - 1, 0))
                wt = weight_tile(m)
                for n, out in enumerate((ph1[m % 2], ph3[m % 2])):
                    for k in range(KT):
                        op = nc.tensor.matmul(out[:], wt[:, n * D + k * P:n * D + (k + 1) * P],
                                              net.h[:, ds(i * PAIR + k * TOK, TOK)],
                                              start=(k == 0), stop=(k == KT - 1))
                op.then_inc(h_up_ready, 1)
                if m >= S:
                    r = m - S
                    pe.wait_ge(sel_loaded, 16)
                    pe.wait_ge(parts_ready, 1)
                    nc.tensor.matmul(pw[r % 2][:], sel[:, r * P:(r + 1) * P],
                                     parts[:, ds(i * TOK, TOK)], start=True, stop=True) \
                        .then_inc(w_ready, 1)

            def down_project(i, m):
                pe.wait_ge(hidden_ready, i * N + m + 1)
                if m == 0:
                    pe.wait_ge(x_added, i)
                wt = weight_tile(m)
                for k in range(KT):
                    op = nc.tensor.matmul(pout[k][:], wt[:, 2 * D + k * P:2 * D + (k + 1) * P],
                                          hidden[:, m % 2, :], start=(m == 0), stop=(m == N - 1))
                op.then_inc(down_done, 1)

            with nc.tensor.Fori(0, PAIRS) as i:
                for m in range(N + 1):
                    if m < N:
                        up_project(i, m)
                    if m >= 1:
                        down_project(i, m - 1)

        @block.scalar
        def _(act):
            tanh_h()
            if cfg.gate_product:
                act.wait_ge(logit_ready, 1)
                nc.scalar.activation(score[:].rearrange("p n e -> p (n e)"),
                                     plogit[:, 0:TOK_TILES * E], ACT.Tanh, scale=0.5) \
                    .then_inc(score_ready, 1)
            else:
                act.wait_ge(exp_in, 1)
                nc.scalar.activation(score[:], score[:], ACT.Exp).then_inc(exp_ready, 1)

            def silu(i, m):
                act.wait_ge(hidden_ready, i * N + max(m - 1, 0))
                if m >= S and cfg.gate_product:
                    src = mid[:, m % 2, :]
                    act.wait_ge(mid_ready, i * routed + m - S + 1)
                else:
                    src = ph1[m % 2][:]
                    act.wait_ge(h_up_ready, i * N + m + 1)
                nc.scalar.activation(act_out[:, m % 2, :], src, ACT.Silu).then_inc(act_ready, 1)

            def copy_up(i, m):
                act.wait_ge(h_up_ready, i * N + m + 1)
                act.wait_ge(mid_ready, i * routed + max(m - S - 1, 0))
                nc.scalar.activation(up[:, m % 2, :], ph1[m % 2][:], ACT.Copy) \
                    .then_inc(up_copied, 1)

            with nc.scalar.Fori(0, PAIRS) as i:
                for m in range(N):
                    if m >= S and cfg.gate_product:
                        copy_up(i, m)
                    silu(i, m)
                    if m == 2 and unit:
                        unit.scalar(i, i + turn0)

        @block.gpsimd
        def _(pool):
            net.clear_last_stage(pool)
            nc.gpsimd.memset(seg[:], 1.0).then_inc(zeroed, 1)
            nc.gpsimd.memset(parts[:], 0.0).then_inc(zeroed, 1)
            pool.wait_ge(zeroed, 2)
            nc.gpsimd.memset(seg[:, :, 0:1], 0.0).then_inc(zeroed, 1)
            if unit:
                with nc.gpsimd.Fori(0, PAIRS) as i:
                    unit.pool_operands(i, i + turn0)
                    unit.pool_own(i + turn0)
                    unit.pool_own_f(i + turn0)

        @block.vector
        def _(dve):
            v = nc.vector
            make_h()
            link = Links(dve, route_links)
            wide = [P, TOK_TILES, E]
            one, two, three = (pick[:, n] for n in range(3))

            def per_token(x):
                return x[:, :, None].to_broadcast(wide)

            if cfg.gate_product:
                dve.wait_ge(score_ready, 1)
                link(v.tensor_scalar(score[:], score[:], 0.5, 0.5, ALU.mult, ALU.add))
                bias = net.pp[:, PP_GATEB:PP_GATEB + E][:, None, :].to_broadcast(wide)
                link(v.tensor_tensor(score[:], score[:], bias, ALU.add))
            else:
                dve.wait_ge(logit_ready, 1)
                logits = plogit[:, 0:TOK_TILES * E].rearrange("p (n e) -> p n e", e=E)
                link(v.tensor_reduce(col[:, 0], logits, AX_X, ALU.max))
                v.tensor_tensor(score[:], logits, per_token(col[:, 0]), ALU.subtract) \
                    .then_inc(exp_in, 1)
                dve.wait_ge(exp_ready, 1)
                link(v.tensor_reduce(col[:, 0], score[:], AX_X, ALU.add))
                link(v.reciprocal(col[:, 1], col[:, 0]))
                link(v.tensor_tensor(score[:], score[:], per_token(col[:, 1]), ALU.mult))
            for n in range(TOK_TILES):
                op = v.max(top8[:, n, :], score[:, n, :])
            link(op)
            last = per_token(top8[:, :, cfg.top - 1])
            link(v.tensor_tensor(one, score[:], last, ALU.is_gt))
            link(v.tensor_tensor(two, score[:], last, ALU.is_equal))
            link(v.tensor_reduce(col[:, 0], one, AX_X, ALU.add))
            link(v.tensor_scalar(col[:, 0], col[:, 0], -1.0, float(cfg.top), ALU.mult, ALU.add))
            dve.wait_ge(zeroed, 3)
            flat = lambda x: x.rearrange("p n e -> p (n e)")
            link(v.tensor_tensor_scan(flat(three), flat(seg[:]), flat(two), 0.0, ALU.mult,
                                      ALU.add))
            link(v.tensor_tensor(three, three, per_token(col[:, 0]), ALU.is_le))
            link(v.tensor_tensor(two, two, three, ALU.mult))
            link(v.tensor_tensor(one, one, two, ALU.add))
            link(v.tensor_tensor(one, one, score[:], ALU.mult))
            link(v.tensor_reduce(col[:, 0], one, AX_X, ALU.add))
            if not cfg.gate_product:
                link(v.tensor_scalar(col[:, 0], col[:, 0], 1e-9, None, ALU.add))
            link(v.reciprocal(col[:, 1], col[:, 0]))
            v.tensor_tensor(one, one, per_token(col[:, 1]), ALU.mult) \
                .then_inc(route_cols_ready, 1)
            dve.wait_ge(route_turned, 1)
            for p in range(PAIRS):
                op = v.tensor_copy(route[:, p * TOK:(p + 1) * TOK], proute[p][0:E, :])
            link(op)
            link(v.tensor_copy(parts[0:E, :], route[:]))
            link(v.tensor_tensor(route[:], route[:], parts[0:E, :], ALU.subtract))
            link(v.tensor_copy(part[:], route[:]))
            v.tensor_copy(parts[PR:PR + E, :], part[:])
            link(v.tensor_tensor(route[:], route[:], part[:], ALU.subtract))
            v.tensor_copy(parts[2 * PR:2 * PR + E, :], route[:]).then_inc(parts_ready, 1)

            def times_up(i, m):
                dve.wait_ge(up_copied, i * routed + m - S + 1)
                v.tensor_tensor(mid[:, m % 2, :], up[:, m % 2, :], ph3[m % 2][:], ALU.mult) \
                    .then_inc(mid_ready, 1)

            def weigh(i, m, src):
                r = m - S
                dve.wait_ge(w_ready, i * routed + r + 1)
                dve.wait_ge(down_done, i * N + max(m - 1, 0))
                v.tensor_tensor(hidden[:, m % 2, :], src, pw[r % 2][:], ALU.mult) \
                    .then_inc(hidden_ready, 1)

            with nc.vector.Fori(0, PAIRS) as i:
                link = Links(dve, links, i, per)
                steps = unit.vector(link, i, i + turn0) if unit else []
                for m in range(N):
                    if m >= S and cfg.gate_product:
                        times_up(i, m)
                        dve.wait_ge(act_ready, i * N + m + 1)
                        weigh(i, m, act_out[:, m % 2, :])
                    elif m < S:
                        dve.wait_ge(act_ready, i * N + m + 1)
                        dve.wait_ge(down_done, i * N + max(m - 1, 0))
                        v.tensor_tensor(hidden[:, m % 2, :], act_out[:, m % 2, :], ph3[m % 2][:],
                                        ALU.mult).then_inc(hidden_ready, 1)
                    else:
                        dve.wait_ge(act_ready, i * N + m + 1)
                        link(v.tensor_tensor(mid[:, m % 2, :], act_out[:, m % 2, :],
                                             ph3[m % 2][:], ALU.mult))
                        weigh(i, m, mid[:, m % 2, :])
                    take(steps, 2)
                assert not steps
                dve.wait_ge(down_done, (i + 1) * N)
                for k in range(KT):
                    out = net.x[:, ds(i * PAIR + k * TOK, TOK)]
                    op = v.tensor_tensor(out, out, pout[k][:], ALU.add)
                op.then_inc(x_added, 1)
                link.check()



DEPTH = 5
SCORE_BANKS = 3
LAG_TURN, LAG_MIX = 4, 5


class Attend:

    def __init__(self, net, mem, tag, heads, per_bank, rows_of, spare_bank, share):
        nc = net.nc
        self.net, self.heads, self.per_bank, self.rows_of = net, heads, per_bank, rows_of
        self.units, self.share = BB * heads, share
        self.banks = self.units // per_bank

        def sb(name, shape, dt=F32):
            return mem.enter_context(nc.sbuf_tensor(name + tag, shape, dt))

        def ps(name):
            return mem.enter_context(nc.psum_tensor(name + tag, [P, 512], F32))

        def sem(name):
            return net.stage_sem(mem, name + tag)

        self.prob = sb("prob", [P, DEPTH, TRI])
        self.turned = sb("turned", [P, 2, TRI])
        self.neg_max = sb("neg_max", [P, DEPTH, ST])
        self.total = sb("total", [P, DEPTH, ST])
        self.inverse = sb("inverse", [P, DEPTH, ST])
        self.ps = [ps("ps0_"), ps("ps1_"), spare_bank]
        self.pt = [ps(f"pturn{n}_") for n in range(2)]
        self.po = [ps(f"po{n}_") for n in range(2)]
        self.s_ready, self.max_ready = sem("s_ready"), sem("max_ready")
        self.exp_ready, self.prob_ready = sem("exp_ready"), sem("prob_ready")
        self.inverse_ready = sem("inverse_ready")
        self.pt_ready = sem("probs_turned")
        self.pt_taken = [sem(f"pt_taken{n}") for n in range(2)]
        self.mixed, self.o_ready, self.o_taken = sem("mixed"), sem("o_ready"), sem("o_taken")


    def scores(self, i, u, query, keys):
        nc, cb, out = self.net.nc, self.net.cb, self.ps[u % SCORE_BANKS]
        ident = cb[:, CB_IDENT:CB_IDENT + P]
        nc.tensor.wait_ge(self.exp_ready, i * self.units + max(u - SCORE_BANKS + 1, 0))
        nc.tensor.matmul(out[:, 0:SEQ], ident, cb[:, CB_MASK_QK:CB_MASK_QK + SEQ], start=True,
                         stop=False)
        nc.tensor.matmul(out[:, 0:P], query(0), keys(P), start=False, stop=True)
        nc.tensor.matmul(out[:, SEQ:2 * SEQ], query(1), keys(SEQ), start=True, stop=False)
        nc.tensor.matmul(out[:, SEQ + P:2 * SEQ], ident, cb[:, CB_MASK_QK:CB_MASK_QK + P],
                         start=False, stop=True).then_inc(self.s_ready, 1)

    def turn(self, i, u):
        nc = self.net.nc
        nc.tensor.wait_ge(self.prob_ready, i * self.units + u + 1)
        nc.tensor.wait_ge(self.pt_taken[u % 2], i * (self.units // 2) + u // 2)
        for n in range(3):
            op = nc.tensor.transpose(self.pt[u % 2][:, n * P:(n + 1) * P],
                                     self.prob[:, u % DEPTH, n * P:(n + 1) * P],
                                     self.net.ident[:])
        op.then_inc(self.pt_ready, 1)

    def mix(self, i, u, values):
        nc = self.net.nc
        bank, place = u // self.per_bank, u % self.per_bank
        if place == 0:
            nc.tensor.wait_ge(self.o_taken, i * self.banks + max(bank - 1, 0))
        nc.tensor.wait_ge(self.pt_taken[u % 2], i * (self.units // 2) + u // 2 + 1)
        rows, at = self.rows_of(place)
        out = self.po[bank % 2]
        nc.tensor.matmul(out[rows, at:at + SEQ], values(0), self.turned[:, u % 2, 0:SEQ],
                         start=True, stop=False)
        op = nc.tensor.matmul(out[rows, at + P:at + SEQ], values(1),
                              self.turned[:, u % 2, SEQ:TRI], start=False, stop=True)
        if place == self.per_bank - 1:
            op.then_inc(self.o_ready, 1)
        else:
            op.then_inc(self.mixed, 1)

    def mixed_up_to(self, i, u):
        bank, place = u // self.per_bank, u % self.per_bank
        if place == self.per_bank - 1:
            return self.o_ready, i * self.banks + bank + 1
        return self.mixed, (i * self.banks + bank) * (self.per_bank - 1) + place + 1


    def maximum(self, i, u):
        nc = self.net.nc
        nc.vector.wait_ge(self.s_ready, i * self.units + u + 1)
        nc.vector.tensor_reduce(self.neg_max[:, u % DEPTH, :],
                                self.ps[u % SCORE_BANKS][:].rearrange("p (t k) -> p t k", t=ST), AX_X,
                                ALU.max, negate=True).then_inc(self.max_ready, 1)

    def invert(self, i, u):
        nc, slot = self.net.nc, u % DEPTH
        nc.vector.wait_ge(self.exp_ready, i * self.units + u + 1)
        nc.vector.reciprocal(self.inverse[:, slot, :], self.total[:, slot, :]) \
            .then_inc(self.inverse_ready, 1)


    def normalise(self, i, u):
        nc, slot = self.net.nc, u % DEPTH
        nc.gpsimd.wait_ge(self.inverse_ready, i * self.units + u + 1)
        for t in range(ST):
            cols = slice(0, P) if t == 0 else slice(P, TRI)
            op = nc.gpsimd.tensor_tensor(
                self.prob[:, slot, cols], self.prob[:, slot, cols],
                self.inverse[:, slot, t:t + 1].to_broadcast([P, P * (t + 1)]), ALU.mult)
        op.then_inc(self.prob_ready, 1)


    def exponential(self, i, u):
        nc, slot = self.net.nc, u % DEPTH
        nc.scalar.wait_ge(self.max_ready, i * self.units + u + 1)
        nc.scalar.wait_ge(self.pt_ready, i * self.units + max(u - DEPTH + 1, 0))
        for t in range(ST):
            cols = slice(0, P) if t == 0 else slice(P, TRI)
            n = P * (t + 1)
            op = nc.scalar.activation(self.prob[:, slot, cols],
                                      self.ps[u % SCORE_BANKS][:, t * SEQ:t * SEQ + n], ACT.Exp,
                                      bias=self.neg_max[:, slot, t:t + 1],
                                      accum_out=self.total[:, slot, t:t + 1])
        op.then_inc(self.exp_ready, 1)


    def take_turned(self, engine, i, u):
        nc = self.net.nc
        if not 0 <= u < self.units or (engine is nc.vector) != (u % self.share == 0):
            return
        engine.wait_ge(self.pt_ready, i * self.units + u + 1)
        if u >= 2:
            engine.wait_ge(*self.mixed_up_to(i, u - 2))
        else:
            engine.wait_ge(self.o_ready, i * self.banks)
        out, src = self.turned[:, u % 2, :], self.pt[u % 2][:, 0:TRI]
        op = (nc.scalar.copy if engine is nc.scalar else nc.vector.tensor_copy)(out, src)
        op.then_inc(self.pt_taken[u % 2], 1)



A_HEADS, A_HEAD, LATENT = 16, 16, 64
Q_AHEAD = 4
SLOT = 32
A_GROUPS = A_HEADS * SLOT // P
(WA_DOWN, WA_Q, WA_K, WA_V, WA_O, WA_END) = np.cumsum(
    [0, KT * P, D, D, A_HEADS * SLOT, A_GROUPS * D]).tolist()


def stage_latent_attention(net):
    nc = net.nc
    U = BB * A_HEADS
    LINKS = CondUnit.VECTOR_LINKS
    net.next_stage()
    with ExitStack() as mem:
        def sb(name, shape, dt=F32):
            return mem.enter_context(nc.sbuf_tensor(name, shape, dt))

        def sem(name):
            return net.stage_sem(mem, name)

        w = net.weights[:, WG_END:WG_END + WA_END]
        latent = sb("latent", [P, TOK_TILES, 2, LATENT])
        latent_sq = sb("latent_sq", [P, TOK_TILES, 2, LATENT])
        stat = sb("stat", [P, 2, TOK_TILES, 2])
        c_t = latent_sq[:].rearrange("p n h c -> p (n h c)")
        keys = sb("keys", [P, KT, PAIRS * TOK])
        values = sb("values", [P, BB * ST, A_HEADS * SLOT])
        query = sb("query", [P, A_HEADS, TOK])
        o = sb("o", [P, A_GROUPS, TOK])

        def rows_of(place):
            return slice(place * SLOT, (place + 1) * SLOT), 0

        pp = [mem.enter_context(nc.psum_tensor(f"latent_out{n}", [P, 512], F32))
              for n in range(2)]
        att = Attend(net, mem, "_latent", A_HEADS, P // SLOT, rows_of, pp[0], 4)

        v_banks = [pp[0], att.po[0], *att.pt]
        q_banks = [att.po[1], pp[1]]
        k_banks = [*att.ps[0:2], *att.pt]

        down_ready, centred, logs = sem("down_ready"), sem("centred"), sem("latent_logs")
        rstd_ready, normed = sem("rstd_ready"), sem("latent_normed")
        c_turned, c_ready = sem("c_turned"), sem("c_ready")
        k_projected, k_ready = sem("k_projected"), sem("k_ready")
        q_projected, v_projected = sem("q_projected"), sem("v_projected")
        q_taken = [sem(f"q_taken{n}") for n in range(2)]
        v_taken = [sem(f"v_taken{n}") for n in range(2)]
        c_pair_ready = sem("c_pair_ready")
        o_projected, x_added = sem("o_projected"), sem("x_added_latent")
        links, once = sem("latent_links"), sem("latent_once")
        unit = CondUnit(net, 3, net.cond_sems)
        tanh_h, make_h, h_ready = condition_input(net, "_latent")
        c_pair = sb("c_pair", [P, TOK])

        block = mem.enter_context(nc.Block())

        @block.sync
        def _(sp):
            for dst, src, done in net.gqa_early:
                sp.dma_start(dst, src).then_inc(done, 16)

        @block.tensor
        def _(pe):
            pe.wait_ge(net.latent_loaded, 16)
            for n in range(TOK_TILES):
                pair, at = n // (BB * ST), n % (BB * ST) * P
                pe.wait_ge(h_ready, pair + 1)
                for k in range(KT):
                    op = nc.tensor.matmul(pp[pair][:, at:at + P],
                                          net.h[:, pair * PAIR + k * TOK + at:][:, 0:P],
                                          w[:, WA_DOWN + k * P:WA_DOWN + (k + 1) * P],
                                          start=(k == 0), stop=(k == KT - 1))
            op.then_inc(down_ready, 1)
            for pair in range(PAIRS):
                pe.wait_ge(normed, pair + 1)
                for n in range(BB * ST):
                    op = nc.tensor.transpose(
                        pp[pair][:, n * P:(n + 1) * P],
                        latent[:, pair * BB * ST + n].rearrange("p h c -> p (h c)"),
                        net.ident[:])
                op.then_inc(c_turned, 1)
            for pair in range(PAIRS):
                pe.wait_ge(c_ready, pair + 1)
                for g in range(KT):
                    out = k_banks[pair * KT + g]
                    at = WA_K + g * P
                    nc.tensor.matmul(out[:], w[:, at:at + P], c_t[:, pair * TOK:(pair + 1) * TOK],
                                     start=True, stop=True).then_inc(k_projected, 1)

            def project_qv(i):
                pe.wait_ge(c_pair_ready, i + 1)
                pe.wait_ge(x_added, i)
                for g in range(KT):
                    nc.tensor.matmul(q_banks[g][:], w[:, WA_Q + g * P:WA_Q + (g + 1) * P], c_pair[:],
                                     start=True, stop=True).then_inc(q_projected, 1)
                for n in range(BB * ST):
                    nc.tensor.matmul(v_banks[n][:], c_pair[:, n * P:(n + 1) * P],
                                     w[:, WA_V:WA_V + A_HEADS * SLOT], start=True, stop=True) \
                        .then_inc(v_projected, 1)

            pe.wait_ge(k_ready, PAIRS * KT)
            with nc.tensor.Fori(0, PAIRS) as i:
                project_qv(i)
                for u in range(U + LAG_MIX):
                    if u == 2:
                        for n in range(2):
                            pe.wait_ge(v_taken[n], (i + 1) * BB * ST // 2)
                    if u < U:
                        b, head = divmod(u, A_HEADS)
                        if u < A_HEADS:
                            pe.wait_ge(q_taken[head // 8], i * 8 + head % 8 + 1)
                        att.scores(
                            i, u,
                            lambda t: query[:, head, b * SEQ + t * P:][:, 0:P],
                            lambda n: keys[:, head // 8, ds(i * TOK + b * SEQ, n)])
                    if 0 <= u - LAG_TURN < U:
                        att.turn(i, u - LAG_TURN)
                    if 0 <= u - LAG_MIX < U:
                        b, head = divmod(u - LAG_MIX, A_HEADS)
                        att.mix(i, u - LAG_MIX, lambda k: values[:, b * ST + k,
                                                           head * SLOT:(head + 1) * SLOT])
                pe.wait_ge(att.o_taken, (i + 1) * att.banks)
                for k in range(KT):
                    for g in range(A_GROUPS):
                        at = WA_O + g * D + k * P
                        op = nc.tensor.matmul(pp[k][:], w[:, at:at + P], o[:, g, :],
                                              start=(g == 0), stop=(g == A_GROUPS - 1))
                op.then_inc(o_projected, 1)

        @block.scalar
        def _(act):
            tanh_h()
            nc.scalar.preload_act_table_set("natural_log_exp_and_others")
            act.wait_ge(centred, 3)
            nc.scalar.activation(stat[:, 1], stat[:, 1], ACT.Ln, scale=1.0 / LATENT,
                                 bias=net.pp[:, PP_EPS_LN:PP_EPS_LN + 1]).then_inc(logs, 1)
            act.wait_ge(logs, 1)
            nc.scalar.activation(stat[:, 1], stat[:, 1], ACT.Exp, scale=-0.5) \
                .then_inc(rstd_ready, 1)
            for pair in range(PAIRS):
                act.wait_ge(c_turned, pair + 1)
                nc.scalar.activation(c_t[:, pair * TOK:(pair + 1) * TOK], pp[pair][:],
                                     ACT.Identity, scale=net.pp[:, PP_LNG:PP_LNG + 1],
                                     bias=net.pp[:, PP_LNB:PP_LNB + 1]).then_inc(c_ready, 1)
            for n in range(PAIRS * KT):
                pair, g = divmod(n, KT)
                act.wait_ge(k_projected, n + 1)
                nc.scalar.copy(keys[:, g, pair * TOK:(pair + 1) * TOK], k_banks[n][:]) \
                    .then_inc(k_ready, 1)

            def take_query(i, h):
                act.wait_ge(q_projected, i * KT + 1)
                nc.scalar.activation(query[:, h, :], q_banks[0][:], ACT.Copy,
                                     scale=net.pp[:, PP_HEADMASK + h:][:, 0:1]) \
                    .then_inc(q_taken[0], 1)

            with nc.scalar.Fori(0, PAIRS) as i:
                for h in range(Q_AHEAD):
                    take_query(i, h)
                for n in range(0, BB * ST, 2):
                    act.wait_ge(v_projected, i * BB * ST + n + 1)
                    nc.scalar.copy(values[:, n, :], v_banks[n][:]).then_inc(v_taken[0], 1)
                for u in range(U + LAG_MIX):
                    if u < 8 - Q_AHEAD:
                        take_query(i, u + Q_AHEAD)
                    att.take_turned(nc.scalar, i, u - LAG_TURN)
                    if u < U:
                        att.exponential(i, u)
                    if 0 <= u - LAG_MIX < U and (u - LAG_MIX) % att.per_bank == att.per_bank - 1:
                        bank = (u - LAG_MIX) // att.per_bank
                        b, g = divmod(bank, A_GROUPS)
                        act.wait_ge(att.o_ready, i * att.banks + bank + 1)
                        act.wait_ge(o_projected, i)
                        nc.scalar.copy(o[:, g, b * SEQ:(b + 1) * SEQ],
                                       att.po[bank % 2][:, 0:SEQ]).then_inc(att.o_taken, 1)
                    if u == 4:
                        unit.scalar(i, i + 3 * PAIRS)

            nc.scalar.preload_act_table_set("exp_and_others")

        @block.gpsimd
        def _(pool):
            net.clear_last_stage(pool)
            with nc.gpsimd.Fori(0, PAIRS) as i:
                unit.pool_operands(i, i + 3 * PAIRS)
                for u in range(U):
                    att.normalise(i, u)
                    if u == 6:
                        unit.pool_own(i + 3 * PAIRS)
                    if u == 11:
                        unit.pool_own_f(i + 3 * PAIRS)

        @block.vector
        def _(dve):
            v = nc.vector
            make_h()
            link = Links(dve, once)
            dve.wait_ge(down_ready, 1)
            for pair in range(PAIRS):
                n = BB * ST
                src = pp[pair][:].rearrange("p (n h c) -> p n h c", n=n, h=2)
                op = v.tensor_reduce(stat[:, 0, pair * n:(pair + 1) * n, :], src, AX_X, ALU.add)
            link(op)
            link(v.tensor_scalar(stat[:, 0], stat[:, 0], 1.0 / LATENT, None, ALU.mult))
            for pair in range(PAIRS):
                n = slice(pair * BB * ST, (pair + 1) * BB * ST)
                src = pp[pair][:].rearrange("p (n h c) -> p n h c", n=BB * ST, h=2)
                mean = stat[:, 0, n, :, None].to_broadcast([P, BB * ST, 2, LATENT])
                v.tensor_tensor(latent[:, n], src, mean, ALU.subtract).then_inc(centred, 1)
            dve.wait_ge(centred, 2)
            link(v.tensor_tensor(latent_sq[:], latent[:], latent[:], ALU.mult))
            v.tensor_reduce(stat[:, 1], latent_sq[:], AX_X, ALU.add).then_inc(centred, 1)
            dve.wait_ge(rstd_ready, 1)
            for pair in range(PAIRS):
                n = slice(pair * BB * ST, (pair + 1) * BB * ST)
                rstd = stat[:, 1, n, :, None].to_broadcast([P, BB * ST, 2, LATENT])
                v.tensor_tensor(latent[:, n], latent[:, n], rstd, ALU.mult).then_inc(normed, 1)
            dve.wait_ge(c_ready, PAIRS)

            with nc.vector.Fori(0, PAIRS) as i:
                link = Links(dve, links, i, LINKS)
                steps = unit.vector(link, i, i + 3 * PAIRS)
                dve.wait_ge(q_projected, i * KT)
                v.tensor_copy(c_pair[:], c_t[:, ds(i * TOK, TOK)]).then_inc(c_pair_ready, 1)
                for n in range(1, BB * ST, 2):
                    dve.wait_ge(v_projected, i * BB * ST + n + 1)
                    v.tensor_copy(values[:, n, :], v_banks[n][:]).then_inc(v_taken[1], 1)
                for u in range(U + LAG_MIX):
                    att.take_turned(nc.vector, i, u - LAG_TURN)
                    if u < U:
                        att.maximum(i, u)
                    if u < 8:
                        dve.wait_ge(q_projected, i * KT + 2)
                        v.tensor_scalar(query[:, 8 + u, :], q_banks[1][:],
                                        net.pp[:, PP_HEADMASK + u:][:, 0:1], None, ALU.mult) \
                            .then_inc(q_taken[1], 1)
                    if 0 <= u - 1 < U:
                        att.invert(i, u - 1)
                    take(steps, 1)
                assert not steps
                dve.wait_ge(o_projected, i + 1)
                for k in range(KT):
                    out = net.x[:, ds(i * PAIR + k * TOK, TOK)]
                    op = v.tensor_tensor(out, out, pp[k][:], ALU.add)
                op.then_inc(x_added, 1)
                link.check()



Q_HEADS, KV_HEADS, Q_HEAD = 16, 4, 128
CHUNK = 512
CHUNKS = (Q_HEADS + 2 * KV_HEADS) * Q_HEAD // CHUNK
QK_CHUNKS = CHUNKS - 1
WG_QKV, WG_O, WG_END = np.cumsum([0, KT * CHUNKS * CHUNK, Q_HEADS * D]).tolist()
HALF = Q_HEAD // 2
RT_QW, RT_KW, RT_END = np.cumsum([2 * ST * 2 * Q_HEAD, Q_HEAD, Q_HEAD]).tolist()


def stage_gqa(net):
    nc = net.nc
    U = BB * Q_HEADS
    TILES = BB * ST
    STEPS = TILES * CHUNKS
    QK = TILES * QK_CHUNKS
    LAG, ROTATED = 5, 3
    LINKS = QK + 2
    net.next_stage()
    with ExitStack() as mem:
        def sb(name, shape, dt=F32):
            return mem.enter_context(nc.sbuf_tensor(name, shape, dt))

        def sem(name):
            return net.stage_sem(mem, name)

        w = net.weights
        tail = w[:, WG_END:]
        rope = tail[:, 0:RT_END]
        table = rope[:, 0:RT_QW].rearrange("p (a t c d) -> p a t c d", a=2, t=ST, c=2)
        at = RT_END
        chunk_sq = tail[:, at:at + 2 * CHUNK].rearrange("p (n h d) -> p n h d", n=2, h=4)
        spare = net.m[:].rearrange("p (n d) -> p n d", d=CHUNK)
        normed, by_cos = spare[:, 0:2], spare[:, 2:4]
        by_sin = net.f_pair[:, 0:2 * CHUNK].rearrange("p (n d) -> p n d", n=2)
        rotated = sb("rotated", [P, ROTATED, CHUNK])
        h_norm = sb("h_norm", [P, PAIR])
        hidden = h_norm
        h_sq = sb("h_sq", [P, PAIR])
        q_t = sb("q_t", [P, Q_HEADS, TOK])
        k_t = sb("k_t", [P, KV_HEADS, TOK])
        values = sb("values_gqa", [P, TILES, CHUNK])
        root = sb("root_gqa", [P, TOK])
        scale = sb("scale_gqa", [P, TILES])
        head_scale = sb("head_scale", [P, 4, 4])

        def rows_of(place):
            return slice(0, P), place * SEQ

        pp = [mem.enter_context(nc.psum_tensor(f"gqa_out{n}", [P, 512], F32)) for n in range(2)]
        att = Attend(net, mem, "_gqa", Q_HEADS, 2, rows_of, pp[0], 2)
        ring = att.ps[0:2] + pp

        rope_loaded, table_ready = sem("rope_loaded"), sem("table_ready")
        h_norm_ready, h_squared = sem("h_norm_ready"), sem("h_squared")
        norm_summed, scale_log, scale_ready = (sem("norm_summed"), sem("scale_log"),
                                               sem("scale_ready"))
        chunk_ready, qk_taken, v_taken = sem("chunk_ready"), sem("qk_taken"), sem("v_taken_gqa")
        chunk_summed = sem("chunk_summed")
        head_log, head_scale_ready = sem("head_log"), sem("head_scale_ready")
        cos_ready, sin_ready, rotated_ready = sem("cos_ready"), sem("sin_ready"), sem("rotated_ready")
        qk_turned, qk_stored = sem("qk_turned"), sem("qk_stored")
        o_projected, hidden_ready = sem("o_projected_gqa"), sem("hidden_ready_gqa")
        hidden_squared, hidden_summed = sem("hidden_squared"), sem("hidden_summed")
        root_log, root_ready, normed_ready = sem("root_log"), sem("root_ready_gqa"), sem("normed")
        links = sem("gqa_links")
        tanh_h, make_h, h_ready = condition_input(net, "_gqa")

        def chunk_of(step):
            n, c = divmod(step, CHUNKS)
            return n, c, n * QK_CHUNKS + c

        block = mem.enter_context(nc.Block())

        @block.sync
        def _(sp):
            sp.dma_start(rope, net.dram["rope"]).then_inc(rope_loaded, 16)
            for dst, src, done in net.moe1_loads:
                sp.dma_start(dst, src).then_inc(done, 16)

        @block.tensor
        def _(pe):
            for s in net.gqa_loaded:
                pe.wait_ge(s, 16)

            def project(i, step):
                n, c, _ = chunk_of(step)
                if step >= 4:
                    _, c4, j4 = chunk_of(step - 4)
                    if c4 < QK_CHUNKS:
                        pe.wait_ge(qk_taken, i * QK + j4 + 1)
                    else:
                        pe.wait_ge(v_taken, i * TILES + step // CHUNKS)
                out = ring[step % 4]
                for k in range(KT):
                    cols = WG_QKV + (k * CHUNKS + c) * CHUNK
                    op = nc.tensor.matmul(out[:], h_norm[:, k * TOK + n * P:][:, 0:P],
                                          w[:, cols:cols + CHUNK], start=(k == 0),
                                          stop=(k == KT - 1))
                op.then_inc(chunk_ready, 1)

            def turn_chunk(i, step):
                _, c, j = chunk_of(step)
                if c == QK_CHUNKS:
                    return
                pe.wait_ge(rotated_ready, i * QK + j + 1)
                pe.wait_ge(qk_stored, i * QK + max(j - 1, 0))
                for hd in range(4):
                    op = nc.tensor.transpose(att.pt[j % 2][:, hd * P:(hd + 1) * P],
                                             rotated[:, j % ROTATED, hd * P:(hd + 1) * P],
                                             net.ident[:])
                op.then_inc(qk_turned, 1)

            with nc.tensor.Fori(0, PAIRS) as i:
                pe.wait_ge(h_norm_ready, i + 1)
                pe.wait_ge(h_squared, i + 1)
                pe.wait_ge(normed_ready, i)
                for n in range(TILES):
                    for k in range(KT):
                        op = nc.tensor.matmul(att.po[1][:, n:n + 1],
                                              h_sq[:, k * TOK + n * P:][:, 0:P],
                                              net.ones[:, 0:1], start=(k == 0),
                                              stop=(k == KT - 1))
                op.then_inc(norm_summed, 1)
                for step in range(STEPS + LAG):
                    if step < STEPS:
                        project(i, step)
                    if step >= LAG:
                        turn_chunk(i, step - LAG)
                pe.wait_ge(qk_stored, (i + 1) * QK)
                pe.wait_ge(v_taken, (i + 1) * TILES)
                for u in range(U + LAG_MIX):
                    if u < U:
                        b, head = divmod(u, Q_HEADS)
                        att.scores(i, u, lambda t: q_t[:, head, b * SEQ + t * P:][:, 0:P],
                                   lambda n: k_t[:, head // 4, b * SEQ:b * SEQ + n])
                    if 0 <= u - LAG_TURN < U:
                        att.turn(i, u - LAG_TURN)
                    if 0 <= u - LAG_MIX < U:
                        b, head = divmod(u - LAG_MIX, Q_HEADS)
                        kv = slice(head // 4 * Q_HEAD, (head // 4 + 1) * Q_HEAD)
                        att.mix(i, u - LAG_MIX, lambda k: values[:, b * ST + k, kv])
                pe.wait_ge(att.o_taken, (i + 1) * att.banks)
                for k in range(KT):
                    for head in range(Q_HEADS):
                        cols = WG_O + head * D + k * P
                        op = nc.tensor.matmul(pp[k][:], w[:, cols:cols + P], q_t[:, head, :],
                                              start=(head == 0), stop=(head == Q_HEADS - 1))
                    op.then_inc(o_projected, 1)
                for k in range(KT):
                    pe.wait_ge(hidden_squared, i * KT + k + 1)
                    op = nc.tensor.matmul(att.po[0][:], net.ones[:],
                                          h_sq[:, k * TOK:(k + 1) * TOK], start=(k == 0),
                                          stop=(k == KT - 1))
                op.then_inc(hidden_summed, 1)

        @block.scalar
        def _(act):
            tanh_h()
            eps = net.pp[:, PP_EPS_RMS:PP_EPS_RMS + 1]

            def square_chunk(i, step):
                n, c, j = chunk_of(step)
                act.wait_ge(chunk_ready, i * STEPS + step + 1)
                src = ring[step % 4][:]
                if c == QK_CHUNKS:
                    nc.scalar.activation(values[:, n, :], src, ACT.Copy, scale=scale[:, n:n + 1]) \
                        .then_inc(v_taken, 1)
                    return
                act.wait_ge(qk_taken, i * QK + max(j - 3, 0))
                for head in range(4):
                    cols = slice(head * Q_HEAD, (head + 1) * Q_HEAD)
                    op = nc.scalar.activation(chunk_sq[:, j % 2, head], src[:, cols], ACT.Square,
                                              scale=scale[:, n:n + 1],
                                              accum_out=head_scale[:, j % 4, head:head + 1])
                op.then_inc(chunk_summed, 1)

            def scale_heads(i, step):
                _, c, j = chunk_of(step)
                if c == QK_CHUNKS:
                    return
                s = head_scale[:, j % 4]
                act.wait_ge(chunk_summed, i * QK + j + 1)
                nc.scalar.activation(s, s, ACT.Ln, scale=1.0 / Q_HEAD, bias=eps) \
                    .then_inc(head_log, 1)
                act.wait_ge(head_log, i * QK + j + 1)
                nc.scalar.activation(s, s, ACT.Exp, scale=-0.5).then_inc(head_scale_ready, 1)

            def store_chunk(i, step):
                n, c, j = chunk_of(step)
                if c == QK_CHUNKS:
                    return
                act.wait_ge(qk_turned, i * QK + j + 1)
                out = q_t[:, 4 * c:4 * c + 4] if c < QK_CHUNKS - 1 else k_t[:]
                nc.scalar.copy(out[:, :, n * P:(n + 1) * P],
                               att.pt[j % 2][:].rearrange("p (h t) -> p h t", h=4)) \
                    .then_inc(qk_stored, 1)

            nc.scalar.preload_act_table_set("natural_log_exp_and_others")
            with nc.scalar.Fori(0, PAIRS) as i:
                act.wait_ge(hidden_summed, i)
                act.wait_ge(h_ready, PAIRS)
                nc.scalar.activation(h_sq[:], net.h[:, ds(i * PAIR, PAIR)], ACT.Square) \
                    .then_inc(h_squared, 1)
                act.wait_ge(norm_summed, i + 1)
                nc.scalar.activation(scale[:], att.po[1][:, 0:TILES], ACT.Ln, scale=1.0 / D,
                                     bias=eps).then_inc(scale_log, 1)
                act.wait_ge(scale_log, i + 1)
                nc.scalar.activation(scale[:], scale[:], ACT.Exp, scale=-0.5) \
                    .then_inc(scale_ready, 1)
                act.wait_ge(scale_ready, i + 1)
                for step in range(STEPS + LAG + 1):
                    if step < STEPS:
                        square_chunk(i, step)
                    if 0 <= step - 1 < STEPS:
                        scale_heads(i, step - 1)
                    if step >= LAG + 1:
                        store_chunk(i, step - LAG - 1)
                for u in range(U + LAG_MIX):
                    att.take_turned(nc.scalar, i, u - LAG_TURN)
                    if u < U:
                        att.exponential(i, u)
                    if 0 <= u - LAG_MIX < U and (u - LAG_MIX) % 2:
                        bank = (u - LAG_MIX) // 2
                        b, pair_of_heads = divmod(bank, Q_HEADS // 2)
                        act.wait_ge(att.o_ready, i * att.banks + bank + 1)
                        nc.scalar.copy(
                            q_t[:, 2 * pair_of_heads:2 * pair_of_heads + 2,
                                b * SEQ:(b + 1) * SEQ],
                            att.po[bank % 2][:].rearrange("p (h t) -> p h t", h=2)) \
                            .then_inc(att.o_taken, 1)
                for k in range(KT):
                    act.wait_ge(hidden_ready, i * KT + k + 1)
                    cols = slice(k * TOK, (k + 1) * TOK)
                    nc.scalar.activation(h_sq[:, cols], hidden[:, cols], ACT.Square) \
                        .then_inc(hidden_squared, 1)
                act.wait_ge(hidden_summed, i + 1)
                nc.scalar.activation(root[:], att.po[0][:], ACT.Ln, scale=1.0 / D, bias=eps) \
                    .then_inc(root_log, 1)
                act.wait_ge(root_log, i + 1)
                nc.scalar.activation(root[:], root[:], ACT.Exp, scale=-0.5) \
                    .then_inc(root_ready, 1)

        @block.gpsimd
        def _(pool):
            net.clear_last_stage(pool)
            pool.wait_ge(rope_loaded, 16)
            for a, at in enumerate((RT_QW, RT_KW)):
                for c, out, weight in ((0, slice(0, Q_HEAD), slice(0, Q_HEAD)),
                                       (1, slice(0, HALF), slice(HALF, Q_HEAD)),
                                       (1, slice(HALF, Q_HEAD), slice(0, HALF))):
                    t = table[:, a, :, c, out]
                    op = nc.gpsimd.tensor_tensor(
                        t, t, rope[:, at:at + Q_HEAD][:, None, weight].to_broadcast(
                            [P, ST, out.stop - out.start]), ALU.mult)
            op.then_inc(table_ready, 1)
            pool.wait_ge(table_ready, 1)
            with nc.gpsimd.Fori(0, PAIRS) as i:
                for step in range(STEPS):
                    n, c, j = chunk_of(step)
                    if c == QK_CHUNKS:
                        continue
                    src = normed[:, j % 2].rearrange("p (h s d) -> p h s d", h=4, s=2)
                    sin = table[:, int(c == QK_CHUNKS - 1), n % ST, 1].rearrange(
                        "p (s d) -> p s d", s=2)
                    pool.wait_ge(qk_taken, i * QK + j + 1)
                    pool.wait_ge(rotated_ready, i * QK + max(j - 1, 0))
                    out = by_sin[:, j % 2].rearrange("p (h s d) -> p h s d", h=4, s=2)
                    for s in range(2):
                        op = nc.gpsimd.tensor_tensor(
                            out[:, :, s, :], src[:, :, 1 - s, :],
                            sin[:, None, s, :].to_broadcast([P, 4, HALF]), ALU.mult)
                    op.then_inc(sin_ready, 1)
                for u in range(U):
                    att.normalise(i, u)

        @block.vector
        def _(dve):
            v = nc.vector
            make_h()

            def norm_chunk(i, step, link):
                n, c, j = chunk_of(step)
                if c == QK_CHUNKS:
                    return
                dve.wait_ge(head_scale_ready, i * QK + j + 1)
                s = head_scale[:, j % 4]
                link(v.tensor_scalar(s, s, scale[:, n:n + 1], None, ALU.mult))
                dve.wait_ge(rotated_ready, i * QK + max(j - 1, 0))
                v.tensor_tensor(normed[:, j % 2].rearrange("p (h d) -> p h d", h=4),
                                ring[step % 4][:].rearrange("p (h d) -> p h d", h=4),
                                s[:, :, None].to_broadcast([P, 4, Q_HEAD]), ALU.mult) \
                    .then_inc(qk_taken, 1)
                dve.wait_ge(qk_taken, i * QK + j + 1)
                cos = table[:, int(c == QK_CHUNKS - 1), n % ST, 0]
                v.tensor_tensor(by_cos[:, j % 2].rearrange("p (h d) -> p h d", h=4),
                                normed[:, j % 2].rearrange("p (h d) -> p h d", h=4),
                                cos[:, None, :].to_broadcast([P, 4, Q_HEAD]), ALU.mult) \
                    .then_inc(cos_ready, 1)

            def rotate(i, step):
                _, c, j = chunk_of(step)
                if c == QK_CHUNKS:
                    return
                dve.wait_ge(sin_ready, i * QK + j + 1)
                dve.wait_ge(cos_ready, i * QK + j + 1)
                dve.wait_ge(qk_turned, i * QK + max(j - ROTATED + 1, 0))
                v.tensor_tensor(rotated[:, j % ROTATED], by_cos[:, j % 2], by_sin[:, j % 2],
                                ALU.add).then_inc(rotated_ready, 1)

            with nc.vector.Fori(0, PAIRS) as i:
                link = Links(dve, links, i, LINKS)
                dve.wait_ge(chunk_ready, i * STEPS)
                dve.wait_ge(normed_ready, i)
                dve.wait_ge(h_ready, PAIRS)
                for k in range(KT):
                    op = v.tensor_scalar(h_norm[:, k * TOK:(k + 1) * TOK],
                                         net.h[:, ds(i * PAIR + k * TOK, TOK)],
                                         net.pp[:, PP_ATTN_NORM + k:PP_ATTN_NORM + k + 1], None,
                                         ALU.mult)
                op.then_inc(h_norm_ready, 1)
                dve.wait_ge(table_ready, 1)
                for step in range(STEPS + 1):
                    if step < STEPS:
                        norm_chunk(i, step, link)
                    if step >= 1:
                        rotate(i, step - 1)
                for u in range(U + LAG_MIX):
                    att.take_turned(nc.vector, i, u - LAG_TURN)
                    if u < U:
                        att.maximum(i, u)
                    if 0 <= u - 1 < U:
                        att.invert(i, u - 1)
                hs = [net.h[:, ds(i * PAIR + k * TOK, TOK)] for k in range(KT)]
                cur = [hidden[:, k * TOK:(k + 1) * TOK] for k in range(KT)]
                for k in range(KT):
                    dve.wait_ge(o_projected, i * KT + k + 1)
                    v.tensor_tensor(cur[k], hs[k], pp[k][:], ALU.add).then_inc(hidden_ready, 1)
                dve.wait_ge(hidden_ready, (i + 1) * KT)
                for k in range(KT):
                    out = net.x[:, ds(i * PAIR + k * TOK, TOK)]
                    link(v.tensor_tensor(out, out, cur[k], ALU.add))
                dve.wait_ge(root_ready, i + 1)
                for k in range(KT):
                    weight = net.pp[:, PP_FFN_NORM + k:PP_FFN_NORM + k + 1]
                    op = v.scalar_tensor_tensor(hs[k], cur[k], weight, root[:], ALU.mult, ALU.mult)
                op.then_inc(normed_ready, 1)
                link.check()



_OUT = [P, PAIRS * PAIR]


def _moe0_weights(net):
    early = W_OUT0 // MOE_COLS
    late = early + (W_MIXER - W_OUT0) // MOE_COLS
    groups = [(0, 4), (4, 8), (8, early), (early, late), (late, late + 4), (late + 4, MOE0_TILES)]
    sems = [net.sem(f"moe0_loaded{n}") for n in range(len(groups))]
    src = net.dram["w_moe0"]

    def load(n, dst):
        a, b = groups[n]
        return dst, src[:, a * MOE_COLS:b * MOE_COLS], sems[n]

    def place(a, b):
        at = a * MOE_COLS if a < early else W_OUT0 + (a - early) * MOE_COLS
        return net.weights[:, at:at + (b - a) * MOE_COLS]

    net.moe0_early = [load(n, place(*groups[n])) for n in range(3)]

    def weights(sb):
        rest = sb("moe_rest", [P, (MOE0_TILES - late) * MOE_COLS])

        def at(a, b):
            return place(a, b) if a < late else rest[:, (a - late) * MOE_COLS:(b - late) * MOE_COLS]

        loads = [load(n, at(*groups[n])) for n in range(3, len(groups))]
        return (lambda m: at(m, m + 1),
                lambda m: next(s for s, (a, b) in zip(sems, groups) if a <= m < b), loads)

    return weights


def _moe1_weights(net):
    places, loads, m = [], [], 0
    for buffer in (net.f, net.e, net.e_pair, net.ev_pair, net.decay, net.num, net.num_b, net.den, net.den_b):
        n = min(buffer.shape[1] // MOE_COLS, MOE1_TILES - m)
        if n > 0:
            done = net.sem(f"moe1_loaded{len(loads)}")
            loads.append((buffer[:, 0:n * MOE_COLS],
                          net.dram["w_moe1"][:, m * MOE_COLS:(m + n) * MOE_COLS], done))
            places += [(buffer[:, k * MOE_COLS:(k + 1) * MOE_COLS], done) for k in range(n)]
            m += n
    assert m == MOE1_TILES
    net.moe1_loads = loads
    return lambda sb: (lambda m: places[m][0], lambda m: places[m][1], [])


def _network(nc, dram, out):
    with ExitStack() as stack:
        net = Net(nc, stack, dram)
        net.weights = stack.enter_context(nc.sbuf_tensor("weights", [P, W_MIXER], F32))
        net.win_chunks = [(0, W_BCXG + 6 * KT * P), (W_BCXG + 6 * KT * P, W_BCXG + 18 * KT * P),
                          (W_BCXG + 18 * KT * P, W_OUT0), (W_OUT0, W_MIXER)]
        moe0_weights, moe1_weights = _moe0_weights(net), _moe1_weights(net)
        net.gqa_loaded = [net.sem(f"gqa_loaded{n}") for n in range(2)]
        net.gqa_early = [(net.weights[:, a:b], dram["w_gqa"][:, a:b], s)
                         for a, b, s in zip((0, WG_O), (WG_O, WG_END), net.gqa_loaded)]
        net.latent_loaded = net.sem("latent_loaded")
        tiles_used = W_OUT0 // MOE_COLS + (WG_END + WA_END - W_OUT0 + MOE_COLS - 1) // MOE_COLS
        latent_later = (tiles_used, [(net.weights[:, WG_END:WG_END + WA_END], dram["w_latent"],
                                      net.latent_loaded)])
        stage_condition(net)
        stage_mixer(net)
        stage_moe(net, MOE0, moe0_weights, condition_input(net, "_moe0"), 2, latent_later)
        stage_latent_attention(net)
        stage_gqa(net)
        stage_moe(net, MOE1, moe1_weights, None, None)
        with nc.Block() as block:
            @block.sync
            def _(sp):
                sp.wait_ge(net.x_loaded, 16)
                sp.dma_start(out, net.x[:]).then_inc(net.out_stored, 16)
                sp.wait_ge(net.out_stored, 16)


def _channels(a):
    return np.ascontiguousarray(
        a.reshape(PAIRS, TOK, KT, P).transpose(3, 0, 2, 1).reshape(P, PAIRS * PAIR))


def _stationary(w):
    return w.reshape(-1, P, w.shape[1]).transpose(1, 0, 2).reshape(P, -1)


def _column(v, tiles):
    return v.reshape(tiles, P).T


def _padded(v, rows=P):
    out = np.zeros((rows, 1), np.float32)
    out[:len(v), 0] = v
    return out


def _params(i):
    conv_tiles = [XT_TILES, XT_TILES + 1, *range(XT_TILES)]
    w = i["L0_attn_conv_w"].reshape(CONV_TILES, P, TAPS)[conv_tiles]
    full = lambda x: np.full((P, 1), x, np.float32)
    zero = full(0.0)
    heads = np.zeros((P, 8), np.float32)
    heads[np.arange(P), np.arange(P) // A_HEAD] = A_HEAD ** -0.5
    cols = [
        np.concatenate([_column(i[n], KT) for n in ("L0_cond_w", "L0_cond2_w", "L1_cond_w",
                                                    "L1_cond2_w")], 1),
        np.concatenate([_column(i[n], KT) for n in ("L0_cond_u", "L0_cond2_u", "L1_cond_u",
                                                    "L1_cond2_u")], 1),
        w.transpose(1, 0, 2).reshape(P, -1),
        i["L0_attn_conv_b"].reshape(CONV_TILES, P)[conv_tiles].T,
        _padded(i["L0_attn_dt_bias"]), _padded(i["L0_attn_A_log"]),
        np.repeat(i["L0_attn_D_param"], HEAD).reshape(XT_TILES, P).T,
        _column(i["L0_attn_norm_w"], XT_TILES),
        full(EPS_MIXER), full(np.log(0.5)),
        np.concatenate([i["L1_attn_q_ln_g"], i["L1_attn_kv_ln_g"]])[:, None],
        np.concatenate([i["L1_attn_q_ln_b"], i["L1_attn_kv_ln_b"]])[:, None],
        full(1e-5), _column(i["L1_ffn_attn_norm_w"], KT), _column(i["L1_ffn_ffn_norm_w"], KT),
        full(1e-6), heads,
        np.broadcast_to(i["cond_512"].reshape(1, -1), (P, BATCH * 64)),
        np.broadcast_to(i["L0_ffn_gate_b"], (P, E0)),
        i["L1_ffn_q_norm_w"][:, None], i["L1_ffn_k_norm_w"][:, None],
        _stationary(i["L0_ffn_gate_w"].T), _stationary(i["L1_ffn_gate_w"].T),
    ]
    out = np.concatenate(cols, 1)
    assert out.shape[1] == PP_END
    return np.ascontiguousarray(out)


def _bf16_constants():
    out = np.zeros((P, CB_END), np.float32)
    r = np.arange(P)
    out[r, CB_IDENT + r] = 1.0
    out[:, CB_MASK_QK:CB_MASK_QK + P][r[None, :] > r[:, None]] = -1e30
    out[:, CB_MASK_QK + P:CB_MASK_QK + SEQ] = -1e30
    out[:, CB_MASK_ST:CB_MASK_ST + P][r[None, :] < r[:, None]] = -1e30
    for part in range(3):
        for h in range(HEADS):
            out[part * HEADS + h, CB_SEL + h * P:CB_SEL + (h + 1) * P] = 1.0
    return out.astype(mybir.dt.np(BF16))


def _mixer_weights(i):
    w = i["L0_attn_W_in"]
    tile = lambda row: _stationary(w[row:row + P].T)
    tiles = [_stationary(w[2 * INNER + 2 * STATE:].T), tile(2 * INNER), tile(2 * INNER + P)]
    for s in range(XT_TILES):
        tiles += [tile(INNER + s * P), tile(s * P)]
    tiles.append(_stationary(i["L0_attn_W_out"].T))
    return np.ascontiguousarray(np.concatenate(tiles, 1))


def _moe_tiles(w1, w3, w2):
    tiles = []
    for m in range(w2.shape[0] // P):
        c = slice(m * P, (m + 1) * P)
        tiles += [_stationary(w1[:, c]), _stationary(w3[:, c]), w2[c]]
    return np.ascontiguousarray(np.concatenate(tiles, 1))


def _moe0(i):
    pad = SHARED_TILES * P - FF
    wide = [np.concatenate([np.pad(i[f"L0_ffn_{n}_shared"], ((0, 0), (0, pad))),
                            i[f"L0_ffn_{n}_routed"].transpose(1, 0, 2).reshape(D, -1)], 1)
            for n in ("w1", "w3")]
    down = np.concatenate([np.pad(i["L0_ffn_w2_shared"], ((0, pad), (0, 0))),
                           i["L0_ffn_w2_routed"].reshape(-1, D)])
    return _moe_tiles(*wide, down)


def _moe1(i):
    return _moe_tiles(i["L1_ffn_wg"].reshape(-1, D).T, i["L1_ffn_wu"].reshape(-1, D).T,
                      i["L1_ffn_wd"].transpose(0, 2, 1).reshape(-1, D))


def _latent_weights(i):
    zeros = np.zeros((LATENT, D), np.float32)
    ukv = i["L1_attn_W_ukv"]
    v = np.pad(ukv[:, D:].reshape(LATENT, A_HEADS, A_HEAD),
               ((LATENT, 0), (0, 0), (0, SLOT - A_HEAD))).reshape(P, -1)
    o = np.pad(i["L1_attn_W_o"].T.reshape(A_HEADS, A_HEAD, D),
               ((0, 0), (0, SLOT - A_HEAD), (0, 0))).reshape(-1, D)
    down = np.concatenate([i["L1_attn_W_dq"], i["L1_attn_W_dkv"]], 1)
    parts = [_stationary(down), np.concatenate([i["L1_attn_W_uq"], zeros]),
             np.concatenate([zeros, ukv[:, :D]]), v, _stationary(o)]
    return np.ascontiguousarray(np.concatenate(parts, 1))


def _gqa_weights(i):
    qkv = np.concatenate([i["L1_ffn_q_w"], i["L1_ffn_k_w"], i["L1_ffn_v_w"]]).T
    return np.ascontiguousarray(
        np.concatenate([_stationary(qkv), _stationary(i["L1_ffn_o_w"].T)], 1))


def _rope(i):
    freqs = 1.0 / 1e6 ** (np.arange(0, Q_HEAD, 2, dtype=np.float32) / np.float32(Q_HEAD))
    angle = np.outer(np.arange(SEQ, dtype=np.float32), freqs.astype(np.float32))
    angle = angle.astype(np.float32)
    tables = np.stack([np.concatenate([np.cos(angle), np.cos(angle)], 1),
                       np.concatenate([-np.sin(angle), np.sin(angle)], 1)], 1)
    tables = tables.reshape(ST, P, 2, Q_HEAD).transpose(1, 0, 2, 3).reshape(P, -1)
    rows = [np.broadcast_to(i[n], (P, Q_HEAD)) for n in ("L1_ffn_q_norm_w", "L1_ffn_k_norm_w")]
    return np.concatenate([tables * Q_HEAD ** -0.5, tables, *rows], 1).astype(np.float32)


def _expert_sel(experts, rows=32):
    out = np.zeros((3 * rows, experts * FF), np.float32)
    for part in range(3):
        for e in range(experts):
            out[part * rows + e, e * FF:(e + 1) * FF] = 1.0
    return out.astype(mybir.dt.np(BF16))


def kernel(**inputs):
    import concourse.bacc as bacc
    from concourse.bass_utils import run_bass_kernel_spmd

    i = {n: np.asarray(a) for n, a in inputs.items()}
    arrays = {
        "x": _channels(i["x"].reshape(-1, D)),
        "f": _channels(i["fside_BxSxS_0"].reshape(-1, D)),
        "pp": _params(i),
        "cb": _bf16_constants(),
        "ident": np.eye(P, dtype=np.float32),
        "w_mixer": _mixer_weights(i),
        "w_latent": _latent_weights(i),
        "w_gqa": _gqa_weights(i), "rope": _rope(i),
        "w_moe0": _moe0(i), 
        "sel0": _expert_sel(E0),
        "w_moe1": _moe1(i), 
        "sel1": _expert_sel(E1),
    }
    nc = bacc.Bacc("TRN2", target_bir_lowering=False, num_devices=1)
    dram = {n: nc.dram_tensor(f"in_{n}", a.shape, mybir.dt.from_np(a.dtype), kind="ExternalInput").ap()
            for n, a in arrays.items()}
    out = nc.dram_tensor("out", _OUT, F32, kind="ExternalOutput").ap()
    _network(nc, dram, out)
    result = run_bass_kernel_spmd(nc, [{f"in_{n}": a for n, a in arrays.items()}], core_ids=[0])
    y = result.results[0]["out"]
    return y.reshape(P, PAIRS, KT, TOK).transpose(1, 3, 2, 0).reshape(BATCH, SEQ, D)
```
